# Optimizing a Trainium2 kernel written in Bass

```python
import numpy as np
import jax
import jax.numpy as jnp

def _softmax(x, axis=-1):
    return jax.nn.softmax(x, axis=axis)

def _gelu(x):
    return jax.nn.gelu(x, approximate=True)

def _silu(x):
    return jax.nn.silu(x)

def _sigmoid(x):
    return jax.nn.sigmoid(x)

def _layernorm(x, axis=-1, eps=1e-05):
    m = jnp.mean(x, axis=axis, keepdims=True)
    v = jnp.var(x, axis=axis, keepdims=True)
    return (x - m) / jnp.sqrt(v + eps)

def _scatter_add(tgt, idx, src, axis=0):
    return tgt.at[idx].add(src)

def _segment_sum(src, seg, n):
    return jax.ops.segment_sum(src, seg, n)
kernel_name = 'mk_early_fusion_d1_tok_img768_r4_b1e296'

def setup_inputs(seed: int=0):
    np.random.seed(seed)
    _w = jnp.asarray

    def _rec_inputs():
        import jax
        import jax.numpy as jnp
        _rk = jax.random.key(seed)
        x = 7.57192e-06 + 1.00007 * jax.random.normal(jax.random.fold_in(_rk, 1), (16, 64, 64, 3), jnp.float32)
        txt = -0.0429142 + 10 * jax.random.normal(jax.random.fold_in(_rk, 2), (16, 128, 192), jnp.float32)
        return (x, txt)
    x, txt = _rec_inputs()

    def _L0_tok_setup():
        import jax, jax.numpy as jnp
        import numpy as np
        PATCH = 16
        DIM = 192
        EPS = 0.001

        def _shifts(x):
            zw = jnp.zeros_like(x[:, :, :1, :])
            right = jnp.concatenate([zw, x[:, :, :-1, :]], axis=2)
            left = jnp.concatenate([x[:, :, 1:, :], zw], axis=2)
            zh = jnp.zeros_like(x[:, :1, :, :])
            down = jnp.concatenate([zh, x[:, :-1, :, :]], axis=1)
            up = jnp.concatenate([x[:, 1:, :, :], zh], axis=1)
            return [right, left, down, up]

        def _patchify(x, p):
            b, H, W, C = x.shape
            hh, ww = (H // p, W // p)
            x = x.reshape(b, hh, p, ww, p, C)
            x = x.transpose(0, 1, 3, 2, 4, 5)
            return x.reshape(b, hh * ww, p * p * C)
        key = jax.random.key(seed)
        k1, k2 = jax.random.split(key)
        b, H, Wd, C = (64, 224, 224, 3)
        F = PATCH * PATCH * 5 * C
        x = jax.random.normal(k1, (b, H, Wd, C), dtype=jnp.float32)
        gamma = jnp.ones((F,), dtype=jnp.float32)
        beta = jnp.zeros((F,), dtype=jnp.float32)
        W = jax.random.normal(k2, (F, DIM), dtype=jnp.float32)
        bb = jnp.zeros((DIM,), dtype=jnp.float32)
        return {'x': x, 'gamma': gamma, 'beta': beta, 'W': W, 'b': bb}
    _L0_tok_all = _L0_tok_setup()
    _L0_tok_in = {k: v for k, v in _L0_tok_all.items() if k in ('gamma', 'beta', 'W', 'b')}
    del _L0_tok_all

    def _L0_attn_setup():
        import jax, jax.numpy as jnp
        import numpy as np
        N_HEAD = 12
        key = jax.random.key(seed)
        k1, k2, k3 = jax.random.split(key, 3)
        nx = 192
        B, S = (2, 512)
        return {'hidden_states': jax.random.normal(k1, (B, S, nx), dtype=jnp.float32), 'w_attn': jax.random.normal(k2, (nx, 3 * nx), dtype=jnp.float32) * 0.02, 'b_attn': jnp.zeros((3 * nx,), dtype=jnp.float32), 'w_proj': jax.random.normal(k3, (nx, nx), dtype=jnp.float32) * 0.02, 'b_proj': jnp.zeros((nx,), dtype=jnp.float32)}
    _L0_attn_all = _L0_attn_setup()
    _L0_attn_in = {k: v for k, v in _L0_attn_all.items() if k in ('w_attn', 'b_attn', 'w_proj', 'b_proj')}
    del _L0_attn_all

    def _L0_ffn_setup():
        import jax, jax.numpy as jnp
        import numpy as np
        NUM_EXPERTS = 8
        TOP_K = 2
        CAP_FACTOR = 1.0
        D_MODEL = 192
        D_FF = 768
        key = jax.random.key(seed)
        k0, k1, k2, k3 = jax.random.split(key, 4)
        B, S, D = (1, 512, D_MODEL)
        inputs = jax.random.normal(k0, (B, S, D), dtype=jnp.float32)
        router_w = jax.random.normal(k1, (NUM_EXPERTS, D), dtype=jnp.float32) * D ** (-0.5)
        w1 = jax.random.normal(k2, (NUM_EXPERTS, D, D_FF), dtype=jnp.float32) * D ** (-0.5)
        w2 = jax.random.normal(k3, (NUM_EXPERTS, D_FF, D), dtype=jnp.float32) * D_FF ** (-0.5)
        return {'inputs': inputs, 'router_w': router_w, 'w1': w1, 'w2': w2}
    _L0_ffn_all = _L0_ffn_setup()
    _L0_ffn_in = {k: v for k, v in _L0_ffn_all.items() if k in ('router_w', 'w1', 'w2')}
    del _L0_ffn_all
    return {'x': x, 'txt': txt, 'L0_tok_gamma': _L0_tok_in['gamma'], 'L0_tok_beta': _L0_tok_in['beta'], 'L0_tok_W': _L0_tok_in['W'], 'L0_tok_b': _L0_tok_in['b'], 'L0_attn_w_attn': _L0_attn_in['w_attn'], 'L0_attn_b_attn': _L0_attn_in['b_attn'], 'L0_attn_w_proj': _L0_attn_in['w_proj'], 'L0_attn_b_proj': _L0_attn_in['b_proj'], 'L0_ffn_router_w': _L0_ffn_in['router_w'], 'L0_ffn_w1': _L0_ffn_in['w1'], 'L0_ffn_w2': _L0_ffn_in['w2']}

def reference(x, txt, L0_tok_gamma, L0_tok_beta, L0_tok_W, L0_tok_b, L0_attn_w_attn, L0_attn_b_attn, L0_attn_w_proj, L0_attn_b_proj, L0_ffn_router_w, L0_ffn_w1, L0_ffn_w2):
    import jax
    import jax.numpy as jnp

    def _L0_tok_ref(x, gamma, beta, W, b):
        import jax, jax.numpy as jnp
        import numpy as np
        PATCH = 16
        DIM = 192
        EPS = 0.001

        def _shifts(x):
            zw = jnp.zeros_like(x[:, :, :1, :])
            right = jnp.concatenate([zw, x[:, :, :-1, :]], axis=2)
            left = jnp.concatenate([x[:, :, 1:, :], zw], axis=2)
            zh = jnp.zeros_like(x[:, :1, :, :])
            down = jnp.concatenate([zh, x[:, :-1, :, :]], axis=1)
            up = jnp.concatenate([x[:, 1:, :, :], zh], axis=1)
            return [right, left, down, up]

        def _patchify(x, p):
            b, H, W, C = x.shape
            hh, ww = (H // p, W // p)
            x = x.reshape(b, hh, p, ww, p, C)
            x = x.transpose(0, 1, 3, 2, 4, 5)
            return x.reshape(b, hh * ww, p * p * C)
        x5 = jnp.concatenate([x] + _shifts(x), axis=-1)
        tokens = _patchify(x5, PATCH)
        mu = jnp.mean(tokens, axis=-1, keepdims=True)
        var = jnp.mean(jnp.square(tokens - mu), axis=-1, keepdims=True)
        ln = (tokens - mu) * jax.lax.rsqrt(var + EPS) * gamma + beta
        return jnp.einsum('bnf,fd->bnd', ln, W) + b

    def _L0_attn_ref(hidden_states, w_attn, b_attn, w_proj, b_proj):
        import jax, jax.numpy as jnp
        import numpy as np
        N_HEAD = 12
        B, S, nx = hidden_states.shape
        d_head = nx // N_HEAD
        qkv = hidden_states @ w_attn + b_attn
        q, k, v = jnp.split(qkv, 3, axis=-1)

        def split(x):
            return x.reshape(B, S, N_HEAD, d_head).transpose(0, 2, 1, 3)
        q, k, v = (split(q), split(k), split(v))
        w = jnp.einsum('bhsd,bhtd->bhst', q, k) / jnp.sqrt(jnp.float32(d_head))
        w = jax.nn.softmax(w, axis=-1)
        a = jnp.einsum('bhst,bhtd->bhsd', w, v)
        a = a.transpose(0, 2, 1, 3).reshape(B, S, nx)
        return a @ w_proj + b_proj

    def _L0_ffn_ref(inputs, router_w, w1, w2):
        import jax, jax.numpy as jnp
        import numpy as np
        NUM_EXPERTS = 8
        TOP_K = 2
        CAP_FACTOR = 1.0
        D_MODEL = 192
        D_FF = 768
        B, S, D = inputs.shape
        x = inputs.reshape(-1, D)
        N = x.shape[0]
        logits = x @ router_w.T
        probs = jax.nn.softmax(logits.astype(jnp.float32), axis=-1)
        weights, sel = jax.lax.top_k(probs, TOP_K)
        cap = int(CAP_FACTOR * N * TOP_K) + 1
        n_real = N * TOP_K
        expert_flat = sel.reshape(-1)
        weight_flat = weights.reshape(-1)
        token_idx = jnp.repeat(jnp.arange(N), TOP_K)
        pad = cap - n_real
        expert_flat = jnp.pad(expert_flat, (0, pad))
        weight_flat = jnp.pad(weight_flat, (0, pad))
        token_idx = jnp.pad(token_idx, (0, pad))
        valid = jnp.arange(cap) < n_real
        toks = x[token_idx]

        def mlp(w1e, w2e):
            return jax.nn.gelu(toks @ w1e) @ w2e
        ys = jax.vmap(mlp)(w1, w2)
        gate = (weight_flat * valid.astype(weight_flat.dtype)).astype(toks.dtype)
        res = ys[expert_flat, jnp.arange(cap)] * gate[:, None]
        out = jnp.zeros((N, D), dtype=inputs.dtype).at[token_idx].add(res)
        return out.reshape(B, S, D)
    h = _L0_tok_ref(x, L0_tok_gamma, L0_tok_beta, L0_tok_W, L0_tok_b)
    h = jnp.concatenate([h, txt], axis=1)
    h = h + _L0_attn_ref(_layernorm(h, axis=-1), L0_attn_w_attn, L0_attn_b_attn, L0_attn_w_proj, L0_attn_b_proj)
    h = h + _L0_ffn_ref(_layernorm(h, axis=-1), L0_ffn_router_w, L0_ffn_w1, L0_ffn_w2)
    return h

_drawn_inputs = setup_inputs


def setup_inputs(seed=0):
    import zlib

    import numpy as np

    out = dict(_drawn_inputs(seed))
    spreads = {'L0_tok_gamma': (1.0, 0.2),
     'L0_tok_beta': (0.0, 0.1),
     'L0_tok_b': (0.0, 0.8),
     'L0_attn_b_attn': (0.0, 0.8),
     'L0_attn_b_proj': (0.0, 0.8)}
    factors = {'L0_attn_w_attn': 8.0,
     'L0_attn_w_proj': 8.0,
     'L0_ffn_router_w': 5.142,
     'L0_ffn_w1': 5.092,
     'L0_ffn_w2': 4.611}
    for name, (base, spread) in spreads.items():
        noise = np.random.default_rng([zlib.crc32(name.encode()), seed]).standard_normal(out[name].shape)
        drawn = base * np.exp(spread * noise) if base else spread * noise
        out[name] = jnp.asarray(drawn.astype(out[name].dtype))
    for name, factor in factors.items():
        out[name] = (out[name] * factor).astype(out[name].dtype)
    return out
```

```python
from contextlib import ExitStack

import concourse.bass as bass
from concourse import mybir

F32 = mybir.dt.float32
F16 = mybir.dt.float16
I32 = mybir.dt.int32
U32 = mybir.dt.uint32
ALU = mybir.AluOpType
ACT = mybir.ActivationFunctionType
AX = mybir.AxisListType.X

P = 128
B, TXT, IMG, D = 16, 128, 16, 192
S = TXT + IMG
N = B * S
HEADS, DH = 12, 16
PAIRS = HEADS // 2
STK = 2 * 3 * DH
AUG = STK + 2
E, DFF, TOPK = 8, 768, 2
FC = DFF // P
NT = N // P
REGION = N + P
SPARE = E * REGION
SLOTS = N * TOPK // P + E - 1
ROW = 196
ROW_ID, ROW_GATE = 192, 193
HALO = 18 * 18 * 3
CH, CK = 40, 54 + 48
EPS_TOK, EPS_LN = 1e-3, 1e-5
AREA = 16900
STEPS = B // 2
SHIFTS = ((1, 1), (1, 0), (1, 2), (0, 1), (2, 1))

C_ID, C_UP = 0, 128
C_LOQ, C_LOK = 256, 257
C_Z = 258
C_VM = 260
C_DESC = 272
C_ER = 280
C_TID = 288
C_SLOT = C_TID + 2 * NT
C_TRI = C_SLOT + SLOTS + 1
NCONST = C_TRI + E * E


def build_program(nc, halo, txt, tok_w, tok_gb, rows, bqk, w_attn, w_proj, router, w1, w2, consts, out):
    with ExitStack() as ctx:
        def sb(name, shape, dt):
            return ctx.enter_context(nc.sbuf_tensor(name, shape, dt))

        def sem(name):
            return ctx.enter_context(nc.semaphore(name))

        bank = [ctx.enter_context(nc.psum_tensor(f"bank{i}", [P, 512], F32)) for i in range(8)]
        routed = nc.dram_tensor("routed_rows", [SPARE + P, ROW], F32, kind="Internal")
        expert_out = nc.dram_tensor("expert_out", [N * TOPK, D], F32, kind="Internal")

        cst = sb("cst", [P, NCONST], F32)
        ident = cst[:, C_ID:C_ID + P]
        id16 = sb("id16", [P, P], F16)
        negid16 = sb("negid16", [P, P], F16)
        up16 = sb("up16", [P, P], F16)
        ones16 = sb("ones16", [P, P], F16)
        scrap = sb("scrap", [1, 1], F32)
        nhalf = sb("nhalf", [P, B], F32)
        rowv = sb("rowv", [P, 3, D], F32)
        bq = sb("bq", [STK, 2 * PAIRS], F32)
        bqlo = sb("bqlo", [STK, 2 * PAIRS], F32)
        wqk = sb("wqk", [P, 4, 2 * PAIRS, STK], F16)
        wv = sb("wv", [P, 4, D], F16)
        wp = sb("wp", [P, 3, D], F32)
        rw32 = sb("rw32", [P, 2, E], F32)
        rw = sb("rw", [P, 4, E], F16)
        w1s = sb("w1s", [P, E, 4, DFF], F16)
        w2s = sb("w2s", [P, E, 2, FC * D], F16)
        h1 = sb("h1", [P, NT, D], F32)
        xt = sb("xt", [P, 3, N], F16)
        stage = sb("stage", [P, 3, 4 * D], F32)
        mv = sb("mv", [P, 16, 2], F32)
        ve = sb("ve", [P, 16], F32)
        rs = sb("rs", [P, 16], F32)
        bst = sb("bst", [P, 2, 10, 6], F32)
        xn32 = sb("xn32", [P, 2, D], F32)
        area = sb("area", [P, AREA], F32)

        def cut(cols, at):
            return area[:, at[0] - cols:at[0]]

        def region(cursor, cols):
            cursor[0] += cols
            assert cursor[0] <= AREA, cursor
            return area[:, cursor[0] - cols:cursor[0]]

        ta = [0]
        patch = region(ta, 2 * HALO).rearrange("p (t f) -> p t f", t=2)
        tokw = region(ta, CH * D)[0:CK, :].rearrange("p (c d) -> p c d", c=CH)
        tokgb = region(ta, 2 * CH)[0:CK, :].rearrange("p (g c) -> p g c", g=2)
        XG = 4
        xg = region(ta, XG * 256)[0:CK, :].rearrange("p (x t) -> p x t", x=XG)
        hl = region(ta, 2 * D).bitcast(F16).rearrange("p (u f) -> p u f", u=2)
        wa32 = region(ta, 2 * 3 * D).rearrange("p (k f) -> p k f", k=2)
        wt16 = region(ta, 4 * 2 * D // 2).bitcast(F16).rearrange("p (k f) -> p k f", k=4)

        aa = [0]
        SW = PAIRS * 2 * S
        qs, ks = [], []
        for i in range(2):
            qs.append(region(aa, SW // 2)[0:AUG, :].bitcast(F16).rearrange("p (r u t) -> p r u t", r=PAIRS, u=2))
            ks.append(region(aa, SW // 2)[0:AUG, :].bitcast(F16).rearrange("p (r u t) -> p r u t", r=PAIRS, u=2))
        qz = [region(aa, SW // 2)[0:AUG, :].bitcast(F16).rearrange("p (h r t) -> p h r t", h=2, r=PAIRS) for _ in range(2)]
        kz = [region(aa, SW // 2)[0:AUG, :].bitcast(F16).rearrange("p (h r t) -> p h r t", h=2, r=PAIRS) for _ in range(2)]
        hm = [region(aa, S)[0:STK, :].bitcast(F16) for _ in range(2)]
        pt = [region(aa, HEADS * S).rearrange("p (h t) -> p h t", h=HEADS) for _ in range(2)]
        ptr = [region(aa, 2 * S).rearrange("p (s t) -> p s t", s=2) for _ in range(2)]
        vt = [region(aa, HEADS * 32).rearrange("p (h d) -> p h d", h=HEADS) for _ in range(2)]
        vb = [region(aa, HEADS * 32).rearrange("p (h d) -> p h d", h=HEADS) for _ in range(2)]
        xrep = [region(aa, 3 * P // 2).bitcast(F16).rearrange("p (c t) -> p c t", c=3) for _ in range(2)]
        kzi = [region(aa, PAIRS * 16)[0:AUG, :].bitcast(F16).rearrange("p (r h t) -> p r h t", r=PAIRS, h=2) for _ in range(2)]
        mmax = [region(aa, 6).bitcast(F16) for _ in range(2)]
        mrem = [region(aa, 2).bitcast(F16).rearrange("p (s h) -> p s h", s=2) for _ in range(2)]
        rden = region(aa, 3 * S)
        vtmp = rden[:, 0:D]
        ot = [region(aa, 3 * S).rearrange("p (j t) -> p j t", j=3) for _ in range(2)]
        oti = region(aa, 3 * 2 * P).rearrange("p (j i t) -> p j i t", j=3, i=2)
        rowb = region(aa, 4 * ROW).rearrange("p (u k w) -> p u k w", u=2, k=2)
        x2 = region(aa, 2 * 3 * P // 2).bitcast(F16).rearrange("p (u c t) -> p u c t", u=2, c=3)
        lg = region(aa, 16).rearrange("p (u e) -> p u e", u=2)
        pr = region(aa, 16).rearrange("p (u e) -> p u e", u=2)
        tm = region(aa, 16).rearrange("p (u e) -> p u e", u=2)
        oh = region(aa, 32).rearrange("p (k u e) -> p k u e", k=2, u=2)
        sm = region(aa, 16).rearrange("p (k u) -> p k u", u=2)
        a16 = region(aa, 8).bitcast(F16).rearrange("p (u e) -> p u e", u=2)
        acc16 = region(aa, 4).bitcast(F16)
        pos = region(aa, 4).bitcast(U32).rearrange("p (k u) -> p k u", k=2)
        padrow = region(aa, ROW)
        ctab = pt[0].rearrange("p h t -> p (h t)")

        ea = [0]
        xr = [region(ea, ROW) for _ in range(4)]
        xe = [region(ea, 3 * P // 2).bitcast(F16).rearrange("p (c t) -> p c t", c=3) for _ in range(4)]
        g32 = [region(ea, DFF) for _ in range(2)]
        gh = [region(ea, DFF // 2).bitcast(F16) for _ in range(2)]
        gl = [region(ea, DFF // 2).bitcast(F16) for _ in range(2)]
        yb = [region(ea, D) for _ in range(4)]
        yk = [region(ea, 2 * D) for _ in range(4)]
        of = [region(ea, D) for _ in range(4)]
        itab = sb("itab", [1, 128], I32)

        (ld_c, ld_halo, ld_tw, ld_row, ld_txt, ld_wa, ld_wp, ld_st, pads_in, slot_in, yk_in, out_st) = [sem(n) for n in (
            "ld_c", "ld_halo", "ld_tw", "ld_row", "ld_txt", "ld_wa", "ld_wp", "ld_st", "pads_in", "slot_in", "yk_in", "out_st")]
        slot_ld = [sem(f"slot_ld{i}") for i in range(4)]
        y_st = [sem(f"y_st{i}") for i in range(4)]
        yk_ld = [sem(f"yk_ld{i}") for i in range(4)]
        ld_txts = [sem(f"ld_txt{i}") for i in range(2)]
        ld_stage = [sem(f"ld_stage{i}") for i in range(4)]
        names = ("pe_tt pe_tm pe_xt pe_P pe_S pe_A pe_V pe_ST pe_PV pe_OP pe_T pe_R pe_K pe_cnt pe_mT pe_LA pe_LB pe_L2 "
                 "ac_tg ac_hm ac_aux ac_exp ac_sm ac_hl ac_gh ac_g ac_misc "
                 "dv_pre dv_var0 dv_patch dv_tg dv_hl0 dv_xt dv_st dv_kz dv_qz dv_S dv_V dv_n dv_h dv_var dv_hl dv_x2 dv_l dv_A "
                 "dv_pos dv_tab dv_mT dv_gl dv_y dv_out dv_link "
                 "po_xrep po_rs0 po_rs po_row po_split po_link po_vb po_const row_st").split()
        sm_ = {n: sem(n) for n in names}

        class Link:

            def __init__(self, eng, semaphore):
                self.eng, self.sem, self.base, self.n = eng, semaphore, 0, 0

            def __call__(self, ins, alone=False):
                self.n += 1
                ins.then_inc(self.sem, 1)
                wait(self.eng, self.sem, self.base + self.n, alone)

        def wait(eng, name, value, alone=False):
            if isinstance(value, int) and value <= 0:
                return
            if alone and not isinstance(value, int):
                eng.wait_ge(ld_c, 16)
            eng.wait_ge(sm_[name] if isinstance(name, str) else name, value)

        def inc(ins, name, by=1):
            ins.then_inc(sm_[name], by)

        def halo_rows(t, shift, rb):
            dr, dc = SHIFTS[shift]
            at = (2 * rb + dr) * 54 + 3 * dc
            return patch[:, t, at:at + CK]

        def attention(step, eng, tally=None):
            step(eng, 0, 0)
            if tally:
                first = tally.base + tally.n
            with eng.Fori(0, (STEPS - 2) // 2) as j:
                if tally:
                    per = tally.per
                    tally.base, tally.n = j * per + first, 0
                step(eng, j * 2 + 1, 1)
                step(eng, j * 2 + 2, 0)
                if tally:
                    assert tally.n == per, (tally.n, per)
            if tally:
                tally.base, tally.n = first + per * ((STEPS - 2) // 2), 0
            step(eng, STEPS - 1, 1)

        block = ctx.enter_context(nc.Block())

        @block.sync
        def _(sp):
            sp.dma_start(cst[:], consts).then_inc(ld_c, 16)
            sp.dma_start(patch, halo.rearrange("(t p) f -> p t f", t=2)).then_inc(ld_halo, 16)
            sp.dma_start(tokgb, tok_gb).then_inc(ld_tw, 16)
            sp.dma_start(tokw, tok_w).then_inc(ld_tw, 16)
            sp.dma_start(rowv[:], rows.rearrange("(o k) d -> o k d", o=1).broadcast_to([P, 3, D])).then_inc(ld_row, 16)
            for u in range(2):
                sp.dma_start(h1[:, 8 * u:8 * u + 8, :], txt[8 * u:8 * u + 8].rearrange("b p d -> p b d")).then_inc(ld_txts[u], 16)
            sp.dma_start(wa32[:, 0, :], w_attn[0:P, :]).then_inc(ld_wa, 16)
            sp.dma_start(wa32[0:64, 1, :], w_attn[P:D, :]).then_inc(ld_wa, 16)
            sp.dma_start(wa32[64:P, 1, :], w_attn[P:D, :]).then_inc(ld_wa, 16)
            sp.dma_start(bq[:], bqk).then_inc(ld_wp, 16)
            sp.dma_start(wp[:], w_proj).then_inc(ld_wp, 16)
            sp.dma_start(rw32[:, 0, :], router[0:P, :]).then_inc(ld_wp, 16)
            sp.dma_start(rw32[0:64, 1, :], router[P:D, :]).then_inc(ld_wp, 16)
            sp.dma_start(rw32[64:P, 1, :], router[P:D, :]).then_inc(ld_wp, 16)
            with sp.Fori(0, E) as e:
                sp.wait_ge(sm_["po_const"], 1)
                wait(sp, "po_split", e * 8, alone=True)
                s = stage
                v = w1.rearrange("e d f -> (e d) f")
                sp.dma_start(s[:, 0, :], v[bass.ds(e * D, P), :]).then_inc(ld_stage[0], 16)
                sp.dma_start(s[0:64, 1, :], v[bass.ds(e * D + P, 64), :]).then_inc(ld_stage[1], 16)
                sp.dma_start(s[64:P, 1, :], v[bass.ds(e * D + P, 64), :]).then_inc(ld_stage[1], 16)
                v = w2.rearrange("e f d -> (e f) d")
                sp.dma_start(s[:, 2, :].rearrange("p (c d) -> p c d", c=4),
                             v[bass.ds(e * DFF, 4 * P), :].rearrange("(c p) d -> p c d", c=4)).then_inc(ld_stage[2], 16)
                wait(sp, "po_split", e * 8 + 2, alone=True)
                sp.dma_start(s[:, 0, 0:2 * D].rearrange("p (c d) -> p c d", c=2),
                             v[bass.ds(e * DFF + 4 * P, 2 * P), :].rearrange("(c p) d -> p c d", c=2)).then_inc(ld_stage[3], 16)
            sp.wait_ge(sm_["dv_tab"], 1)
            sp.dma_start(routed[SPARE:SPARE + P, :], padrow).then_inc(pads_in, 16)
            for e in range(E):
                r = nc.sync.value_load(itab[0:1, 64 + e:65 + e], min_val=0, max_val=SPARE - P)
                sp.dma_start(routed[bass.ds(r, P), :], padrow).then_inc(pads_in, 16)
            sp.wait_ge(pads_in, 16 * (E + 1))
            sp.wait_ge(sm_["row_st"], 16 * 4 * (STEPS + 1))

            def slot(s, p):
                r = nc.sync.value_load(itab[0:1, bass.ds(s, 1)], min_val=0, max_val=SPARE)
                if not isinstance(s, int) or s >= 4:
                    sp.wait_ge(y_st[p], (s - p) * 4)
                sp.dma_start(xr[p], routed[bass.ds(r, P), :]).then_inc(slot_ld[p], 16)

            for s in range(4):
                slot(s, s)
            with sp.Fori(0, (SLOTS - 3) // 4) as j:
                for p in range(4):
                    slot(j * 4 + (4 + p), p)
            for p in range(4):
                sp.wait_ge(y_st[p], 16 * len(range(p, SLOTS, 4)))
            ykv = expert_out.rearrange("(t k) d -> t (k d)", k=2)
            with sp.Fori(0, 4) as j:
                for p in range(4):
                    wait(sp, "dv_out", j * 4, alone=True)
                    sp.dma_start(yk[p], ykv[bass.ds(j * 4 * S + (p * S + IMG), P), :]).then_inc(yk_ld[p], 16)
            sp.wait_ge(sm_["dv_out"], 14)
            for i in range(2):
                v = ykv.rearrange("(i b t) w -> i b t w", i=2, t=S)[i, :, 0:IMG, :]
                for b in range(8):
                    sp.dma_start(yk[i][16 * b:16 * b + 16, :], v[b]).then_inc(yk_ld[i], 16)

        @block.tensor
        def _(pe):
            mm = nc.tensor.matmul
            pe.wait_ge(ld_c, 16)

            def transposes(c):
                if c == 0:
                    pe.wait_ge(sm_["dv_patch"], 2)
                wait(pe, "dv_tg" if c % 2 == 0 else "ac_tg", c // 2)
                for t in range(2):
                    last = nc.tensor.transpose(bank[c % 2][0:CK, P * t:P * t + P], halo_rows(t, c // 8, c % 8), ident)
                inc(last, "pe_tt")

            def products(c):
                wait(pe, "dv_tg" if c % 2 == 0 else "ac_tg", c // 2 + 1)
                if c == 0:
                    pe.wait_ge(ld_tw, 32)
                for t in range(2):
                    last = mm(bank[2 + t][:, 0:D], xg[:, c % XG, P * t:P * t + P], tokw[:, c, :], start=c == 0, stop=c == CH - 1)
                inc(last, "pe_tm")

            for c in range(CH + 2):
                if c < CH:
                    transposes(c)
                if c >= 2:
                    products(c - 2)
            pe.wait_ge(sm_["dv_pre"], 1)

            def to_features(i):
                for u in range(2):
                    wait(pe, "dv_hl0", i + 1)
                    wait(pe, "dv_xt", i * 2 + u - 1 if isinstance(i, int) else i * 2 + (u - 1))
                    o = bank[4 + u][:].bitcast(F16)
                    nc.tensor.transpose(o[:, 0:P], hl[:, u, 0:P], id16[:])
                    nc.tensor.transpose(o[:, P:2 * P], hl[:, u, 2 * P:3 * P], id16[:])
                    inc(nc.tensor.transpose(o[:, 2 * P:3 * P], hl[:, u, P:2 * P], id16[:]), "pe_xt")

            to_features(0)
            with pe.Fori(0, STEPS) as j:
                to_features(j + 1)

            def project(i, chunks):
                for c in chunks:
                    b = bank[c % 2]
                    wait(pe, "dv_st", i * 12 + (c - 1))
                    cols = bass.ds(i * 2 * S, 2 * S)
                    for n, (k, t) in enumerate(((0, 0), (1, 0), (0, 1), (2, 2), (3, 2))):
                        last = mm(b[0:STK, 0:2 * S], wqk[:, k, c, :], xt[:, t, cols], start=n == 0, stop=n == 4)
                    inc(last, "pe_P")

            def scores(i, par, u):
                wait(pe, "dv_kz", i * 2 + u + 1)
                if u == 0:
                    wait(pe, "dv_h", i * 2)
                for n in range(8):
                    b = bank[2 + n % 2]
                    wait(pe, "dv_S", i * 16 + (8 * u + n - 1))
                    if n < 6:
                        last = mm(b[:, 0:2 * S], qs[par][0:STK, n, u, 0:TXT], kz[u][0:STK, :, n, :], start=True, stop=True)
                    else:
                        for r in range(4 * (n - 6), min(4 * (n - 6) + 4, PAIRS)):
                            c = 32 * (r % 4)
                            last = mm(b[c:c + IMG, 0:2 * S], qs[par][0:STK, r, u, TXT:S], kz[u][0:STK, :, r, :], start=True, stop=True)
                    inc(last, "pe_S")

            def minus_max(i, u):
                wait(pe, "dv_S", i * 16 + (8 * u + 8))
                if u == 0:
                    wait(pe, "ac_exp", i * 14)
                else:
                    wait(pe, "ac_aux", i * 2 + 1)
                for r in range(PAIRS):
                    o = bank[4 + r // 3][STK:AUG, (r % 3) * S:(r % 3) * S + S]
                    mm(o[:, 0:TXT], mmax[u][:, 2 * r:2 * r + 2], negid16[:], start=True, stop=True)
                    c = 32 * (r % 4)
                    last = mm(o[:, TXT:S], mrem[u][:, r // 4, :], negid16[:, c:c + IMG], start=True, stop=True)
                inc(last, "pe_A")

            def values(i, u):
                wait(pe, "dv_S", i * 16 + 16)
                wait(pe, "po_xrep", i * 2 + u + 1)
                o = bank[2 + u]
                for n, (t, k) in enumerate(((0, 0), (0, 1), (1, 0), (2, 2), (2, 3))):
                    mm(o[:, 0:D], xt[:, t, bass.ds((i * 2 + u) * S, TXT)], wv[:, k, :], start=n == 0, stop=n == 4)
                for n, (t, k) in enumerate(((0, 0), (0, 1), (1, 0), (2, 2), (2, 3))):
                    last = mm(o[:, D:2 * D], xrep[u][:, t, :], wv[:, k, :], start=n == 0, stop=n == 4)
                inc(last, "pe_V")

            def scores_t(i, par, u):
                wait(pe, "dv_qz", i * 2 + u + 1)
                for n in range(7):
                    b = bank[4 + (n + u) % 2]
                    wait(pe, "ac_exp", i * 14 + (7 * u + n - 1))
                    if n == 0 and u == 0:
                        wait(pe, "ac_aux", i * 2 + 2)
                    if n < 6:
                        last = mm(b[:, 0:2 * S], ks[par][:, n, u, 0:TXT], qz[u][:, :, n, :], start=True, stop=True)
                    else:
                        for r in range(PAIRS):
                            c = 32 * (r % 4)
                            last = mm(b[c:c + 32, S * (r // 4):S * (r // 4) + S], kzi[u][:, r, :, :], qs[par][:, r, u, :], start=True, stop=True)
                    inc(last, "pe_ST")

            def weighted(i, u):
                wait(pe, "ac_exp", i * 14 + (7 * u + 7))
                wait(pe, "dv_V", i * 2 + u + 1)
                wait(pe, "po_vb", i * 2 + u + 1)
                wait(pe, "dv_n", i * 2 + u)
                for j in range(3):
                    k = P if j < 2 else 64
                    o = bank[6][:, S * j:S * j + S]
                    mm(o, vb[u][0:k, 4 * j:4 * j + 4, :], ptr[u][0:k, j // 2, :], start=True, stop=True)
                    for c in range(4):
                        last = mm(o[32 * c:32 * c + 32, :], vt[u][:, 4 * j + c, :], pt[u][:, 4 * j + c, :], start=False, stop=True,
                                  skip_group_check=True)
                inc(last, "pe_PV")

            def out_project(i, u, src):
                wait(pe, "dv_V", i * 2 + u + 1 if not (isinstance(i, int) and i == STEPS) else 2 * STEPS)
                for j in range(3):
                    last = mm(bank[2 + u][:, 0:D], src(j), wp[:, j, :], start=j == 0, stop=j == 2)
                inc(last, "pe_OP")

            def post_t(i):
                wait(pe, "dv_hl", i + 1)
                wait(pe, "dv_pos", i)
                for u in range(2):
                    o = bank[7][:].bitcast(F16)[:, 3 * P * u:3 * P * u + 3 * P]
                    r = rowb[:, u, 0, 0:D].bitcast(F16)
                    nc.tensor.transpose(o[:, 0:P], r[:, 0:P], id16[:])
                    nc.tensor.transpose(o[:, P:2 * P], r[:, 2 * P:3 * P], id16[:])
                    last = nc.tensor.transpose(o[:, 2 * P:3 * P], r[:, P:2 * P], id16[:])
                inc(last, "pe_T")

            def post_router(i):
                wait(pe, "dv_x2", i + 1)
                for u in range(2):
                    for n, (t, k) in enumerate(((0, 0), (0, 1), (1, 0), (2, 2), (2, 3))):
                        last = mm(bank[7][:, 384 + 8 * u:392 + 8 * u], x2[:, u, t, :], rw[:, k, :], start=n == 0, stop=n == 4)
                inc(last, "pe_R")

            def post_rank(i):
                wait(pe, "dv_A", i + 1)
                for u in range(2):
                    o = bank[7][:, 400 + 8 * u:408 + 8 * u]
                    mm(o, up16[:], a16[:, u, :], start=True, stop=False)
                    if u:
                        mm(o, ones16[:], a16[:, 0, :], start=False, stop=False)
                    last = mm(o, ones16[:], acc16, start=False, stop=True)
                inc(last, "pe_K")

            pe.wait_ge(sm_["dv_xt"], NT)
            pe.wait_ge(sm_["ac_misc"], 1)
            project(0, range(12))

            def step(pe, i, par):
                first, last_ = isinstance(i, int) and i == 0, isinstance(i, int) and i == STEPS - 1
                scores(i, par, 0)
                scores(i, par, 1)
                if not last_:
                    project(i + 1, range(0, 6))
                if not first:
                    post_t(i - 1)
                minus_max(i, 0)
                if not last_:
                    project(i + 1, range(6, 8))
                minus_max(i, 1)
                if not last_:
                    project(i + 1, range(8, 9))
                if not first:
                    post_router(i - 1)
                values(i, 0)
                values(i, 1)
                scores_t(i, par, 0)
                if not last_:
                    project(i + 1, range(9, 12))
                scores_t(i, par, 1)
                weighted(i, 0)
                if not first:
                    post_rank(i - 1)
                weighted(i, 1)
                for u in range(2):
                    wait(pe, "dv_n", i * 2 + u + 1)
                    out_project(i, u, lambda j: ot[u][:, j, 0:TXT])

            attention(step, pe)
            wait(pe, "dv_h", 2 * STEPS)
            for u in range(2):
                out_project(STEPS, u, lambda j: oti[:, j, u, :])
            for i in (STEPS - 1, STEPS):
                post_t(i)
                post_router(i)
                post_rank(i)
            wait(pe, "dv_pos", STEPS + 1)
            inc(mm(bank[7][0:1, 416:424], ones16[:, 0:1], acc16, start=True, stop=True), "pe_cnt")

            def slot_t(s, p):
                pe.wait_ge(slot_ld[p], ((s - p) * 4 + 16))
                wait(pe, "dv_mT", s - 1)
                o = bank[4 + p % 2][:].bitcast(F16)
                r = xr[p][:, 0:D].bitcast(F16)
                nc.tensor.transpose(o[:, 0:P], r[:, 0:P], id16[:])
                nc.tensor.transpose(o[:, P:2 * P], r[:, 2 * P:3 * P], id16[:])
                inc(nc.tensor.transpose(o[:, 2 * P:3 * P], r[:, P:2 * P], id16[:]), "pe_mT")

            def up(s, p):
                e = nc.tensor.value_load(itab[0:1, bass.ds(s + 72, 1)], min_val=0, max_val=E - 1)
                wait(pe, "dv_mT", s + 1)
                for f in range(FC):
                    if f in (0, 4):
                        wait(pe, "ac_g", (s - 2) * 2 + (1 if f == 0 else 2) if isinstance(s, int) else s * 2 + ((-3) if f == 0 else (-2)))
                    o = bank[2 * (p % 2) + f // 4][:, P * (f % 4):P * (f % 4) + P]
                    for n, (k, t) in enumerate(((0, 0), (1, 0), (0, 1), (2, 2), (3, 2))):
                        w = w1s[:, bass.ds(e, 1), k, P * f:P * f + P].rearrange("p a f -> p (a f)")
                        last = mm(o, w, xe[p][:, t, :], start=n == 0, stop=n == 4)
                    if f == 3:
                        inc(last, "pe_LA")
                inc(last, "pe_LB")

            def down(s, p):
                e = nc.tensor.value_load(itab[0:1, bass.ds(s + 72, 1)], min_val=0, max_val=E - 1)
                wait(pe, "dv_y", s - 1)
                for f in range(FC):
                    if f in (0, 4):
                        wait(pe, "dv_gl", s * 2 + (1 if f == 0 else 2))
                    for n, (g, k) in enumerate(((gh, 0), (gh, 1), (gl, 0))):
                        w = w2s[:, bass.ds(e, 1), k, D * f:D * f + D].rearrange("p a f -> p (a f)")
                        last = mm(bank[6 + p % 2][:, 0:D], g[p % 2][:, P * f:P * f + P], w,
                                  start=f == 0 and n == 0, stop=f == FC - 1 and n == 2)
                inc(last, "pe_L2")

            wait(pe, "dv_tab", 1)
            wait(pe, "po_split", 8 * E)
            slot_t(0, 0)
            for s in range(3):
                up(s, s)
                slot_t(s + 1, s + 1)
                if s:
                    down(s - 1, s - 1)
            with pe.Fori(0, (SLOTS - 3) // 4) as j:
                for n in range(4):
                    p = (3 + n) % 4
                    s = j * 4 + (3 + n)
                    up(s, p)
                    slot_t(s + 1, (p + 1) % 4)
                    down(s - 1, (p - 1) % 4)
            down(SLOTS - 1, (SLOTS - 1) % 4)

        @block.scalar
        def _(act):
            actf = nc.scalar.activation
            nc.scalar.preload_act_table(ACT.Exp)
            act.wait_ge(ld_c, 16)
            act.wait_ge(ld_tw, 32)
            for c in range(1, CH, 2):
                wait(act, "pe_tt", c + 1)
                wait(act, "pe_tm", c - XG + 1)
                inc(actf(xg[:, c % XG, :], bank[1][0:CK, 0:256], ACT.Identity, bias=tokgb[:, 1, c:c + 1], scale=tokgb[:, 0, c:c + 1]), "ac_tg")
            act.wait_ge(ld_wp, 80)
            for k in range(2):
                last = actf(bqlo[:, PAIRS * k:PAIRS * k + PAIRS], bq[:, PAIRS * k:PAIRS * k + PAIRS], ACT.Copy,
                            scale=cst[0:STK, C_LOQ + k:C_LOQ + k + 1])
            inc(last, "ac_misc")
            wait(act, "ac_misc", 1)

            def low_half(i, chunks):
                for c in chunks:
                    wait(act, "pe_P", i * 12 + (c + 1))
                    wait(act, "dv_st", i * 12 + (c - 1))
                    inc(actf(hm[c % 2], bank[c % 2][0:STK, 0:2 * S], ACT.Identity, bias=bqlo[:, c:c + 1],
                             scale=cst[0:STK, C_LOQ + c // PAIRS:C_LOQ + c // PAIRS + 1]), "ac_hm")

            def aux(i, par, u):
                wait(act, "pe_A", i * 2 + u + 1)
                for k in range(2):
                    last = actf(qs[par][STK:AUG, 3 * k:3 * k + 3, u, :], bank[4 + k][STK:AUG, 0:3 * S].rearrange("p (r t) -> p r t", r=3), ACT.Copy)
                inc(last, "ac_aux")

            def exps(i, u):
                wait(act, "pe_PV", i * 2 + (u - 1))
                for n in range(7):
                    b = bank[4 + (n + u) % 2]
                    wait(act, "pe_ST", i * 14 + (7 * u + n + 1))
                    if n < 6:
                        last = actf(pt[u][:, 2 * n:2 * n + 2, :], b[:, 0:2 * S].rearrange("p (h t) -> p h t", h=2), ACT.Exp, scale=DH ** -0.5)
                    else:
                        actf(ptr[u][:, 0, :], b[:, 0:S], ACT.Exp, scale=DH ** -0.5)
                        last = actf(ptr[u][0:64, 1, :], b[0:64, S:2 * S], ACT.Exp, scale=DH ** -0.5)
                    inc(last, "ac_exp")

            def post_exp(i):
                wait(act, "dv_l", i + 1)
                inc(actf(pr, lg, ACT.Exp), "ac_sm")

            low_half(0, range(12))

            def step(act, i, par):
                first, last_ = isinstance(i, int) and i == 0, isinstance(i, int) and i == STEPS - 1
                if not last_:
                    low_half(i + 1, range(0, 6))
                aux(i, par, 0)
                if not last_:
                    low_half(i + 1, range(6, 8))
                aux(i, par, 1)
                if not last_:
                    low_half(i + 1, range(8, 9))
                exps(i, 0)
                if not first:
                    post_exp(i - 1)
                if not last_:
                    low_half(i + 1, range(9, 12))
                exps(i, 1)

            attention(step, act)
            post_exp(STEPS - 1)
            post_exp(STEPS)
            nc.scalar.preload_act_table(ACT.Gelu_apprx_tanh)

            def gelus(s, p):
                q = p % 2
                for half, (a, b) in enumerate(((0, 512), (512, DFF))):
                    wait(act, "pe_LA" if half == 0 else "pe_LB", s + 1)
                    if half == 0:
                        wait(act, "pe_L2", s - 1)
                        wait(act, "dv_gl", s * 2 - 2)
                    src = bank[2 * q + half][:, 0:b - a]
                    actf(gh[q][:, a:b], src, ACT.Gelu_apprx_tanh)
                    inc(actf(g32[q][:, a:b], src, ACT.Gelu_apprx_tanh), "ac_g")

            for s in range(3):
                gelus(s, s)
            with act.Fori(0, (SLOTS - 3) // 4) as j:
                for n in range(4):
                    gelus(j * 4 + (3 + n), (3 + n) % 4)
            with act.Fori(0, 4) as j:
                for p in range(4):
                    wait(act, "dv_out", j * 4 + (p + 1))
                    act.dma_start(out.rearrange("b t d -> (b t) d")[bass.ds(j * 4 * S + (p * S + IMG), P), :], of[p]).then_inc(out_st, 16)
            for i in range(2):
                wait(act, "dv_out", 16 + i + 1)
                for b in range(8):
                    act.dma_start(out[8 * i + b, 0:IMG, :], of[i][16 * b:16 * b + 16, :]).then_inc(out_st, 16)
            act.wait_ge(out_st, 16 * (16 + 16))

        @block.vector
        def _(dve):
            v = nc.vector
            link = Link(dve, sm_["dv_link"])
            dve.wait_ge(ld_c, 16)
            v.tensor_copy(id16[:], ident)
            v.tensor_scalar(negid16[:], ident, -1.0, None, ALU.mult)
            v.tensor_copy(up16[:], cst[:, C_UP:C_UP + P])
            v.memset(bank[2][:], 0.0)
            v.memset(bank[3][:], 0.0)
            inc(v.memset(ones16[:], 1.0), "dv_pre")
            dve.wait_ge(ld_halo, 16)
            for t in range(2):
                for s in range(5):
                    dr, dc = SHIFTS[s]
                    view = patch[:, t, :].rearrange("p (r c) -> p r c", r=18)
                    for k in range(2):
                        last = v.bn_stats(bst[:, t, 2 * s + k, :], view[:, dr + 8 * k:dr + 8 * k + 8, 3 * dc:3 * dc + 48])
                link(last)
                link(v.bn_aggr(mv[:, t, :], bst[:, t, :, :].rearrange("p k s -> p (k s)")))
            inc(v.tensor_scalar(ve[:, 0:2], mv[:, 0:2, 1], EPS_TOK, None, ALU.add), "dv_var0")
            wait(dve, "po_rs0", 1)
            for t in range(2):
                inc(v.tensor_scalar(patch[:, t, :], patch[:, t, :], mv[:, t, 0:1], rs[:, t:t + 1], ALU.subtract, ALU.mult), "dv_patch")
            dve.wait_ge(ld_tw, 32)
            for c in range(0, CH, 2):
                wait(dve, "pe_tt", c + 1)
                wait(dve, "pe_tm", c - XG + 1)
                inc(v.tensor_scalar(xg[:, c % XG, :], bank[0][0:CK, 0:256], tokgb[:, 0, c:c + 1], tokgb[:, 1, c:c + 1], ALU.mult, ALU.add), "dv_tg")
            dve.wait_ge(ld_row, 16)
            wait(dve, "pe_tm", CH)
            for t in range(2):
                last = v.tensor_tensor(h1[:, B + t, :], bank[2 + t][:, 0:D], rowv[:, 0, :], ALU.add)
            link(last)
            dve.wait_ge(ld_txts[0], 16)
            dve.wait_ge(ld_txts[1], 16)

            def norm_stats(tiles, n):
                for u in range(n):
                    last = v.bn_stats(bst[:, u, 0, :], tiles(u))
                link(last)
                v.memset(scrap[:], 0.0)
                for u in range(n):
                    last = v.bn_aggr(mv[:, u, :], bst[:, u, 0, :])
                link(last)
                return v.tensor_scalar(ve[:, 0:n], mv[:, 0:n, 1], EPS_LN, None, ALU.add)

            def norm(i, where):
                tile = (lambda u: h1[:, B + u, :]) if where == "img" else (
                    lambda u: h1[:, bass.ds(i * 2 - 2 + u, 1), :].rearrange("p a d -> p (a d)"))
                inc(norm_stats(tile, 2), "dv_var0")
                wait(dve, "po_rs0", i + 2)
                wait(dve, "pe_xt", i * 2)
                for u in range(2):
                    last = v.tensor_scalar(xn32[:, u, :], tile(u), mv[:, u, 0:1], rs[:, u:u + 1], ALU.subtract, ALU.mult)
                link(last)
                for u in range(2):
                    v.tensor_tensor(tile(u), tile(u), rowv[:, 1, :], ALU.add)
                    last = v.tensor_copy(hl[:, u, 0:D], xn32[:, u, :])
                link(last)
                v.tensor_tensor(hl[:, :, D:2 * P], xn32[:, :, P:D], hl[:, :, P:D], ALU.subtract)
                inc(v.tensor_tensor(hl[:, :, 2 * P:3 * P], xn32[:, :, 0:P], hl[:, :, 0:P], ALU.subtract), "dv_hl0")

            def to_xt(i, where):
                for u in range(2):
                    wait(dve, "pe_xt", i * 2 + u + 1)
                    src = bank[4 + u][:].bitcast(F16)[:, 0:3 * P].rearrange("p (c t) -> p c t", c=3)
                    if where == "img":
                        for c in range(3):
                            dst = xt[:, c, :].rearrange("p (b t) -> p b t", b=B)[:, 8 * u:8 * u + 8, TXT:S]
                            last = v.tensor_copy(dst, src[:, c, :].rearrange("p (b t) -> p b t", b=8))
                    else:
                        last = v.tensor_copy(xt[:, :, bass.ds((i * 2 - 2 + u) * S, TXT)], src)
                    inc(last, "dv_xt")

            norm(0, "img")
            to_xt(0, "img")
            n0 = link.base + link.n
            with dve.Fori(0, STEPS) as j:
                link.base, link.n = j * 4 + n0, 0
                norm(j + 1, "txt")
                to_xt(j + 1, "txt")
                assert link.n == 4, link.n
            link.base, link.n = n0 + 4 * STEPS, 0
            wait(dve, "po_const", 1)
            for par in range(2):
                v.memset(ks[par][STK:AUG, :, :, :], 1.0)
            link(v.memset(acc16, 0.0))

            def stacks(i, par, chunks):
                for c in chunks:
                    wait(dve, "ac_hm", i * 12 + (c + 1))
                    dst = (qs, ks)[c // PAIRS][par][0:STK, c % PAIRS, :, :].rearrange("p u t -> p (u t)")
                    inc(v.scalar_tensor_tensor(dst, bank[c % 2][0:STK, 0:2 * S], bq[:, c:c + 1], hm[c % 2], ALU.add, ALU.subtract), "dv_st")

            def separate(which, i, par, u):
                src, dst, name = (ks, kz, "dv_kz") if which == "k" else (qs, qz, "dv_qz")
                if which == "q":
                    wait(dve, "ac_aux", i * 2 + u + 1)
                else:
                    wait(dve, "dv_st", i * 12 + 12)
                    wait(dve, "pe_ST", i * 14 + 7 * u - 7 if u else i * 14 - 7)
                for h in range(2):
                    last = v.tensor_scalar(dst[u][:, h, :, :], src[par][:, :, u, :], cst[0:AUG, C_Z + h:C_Z + h + 1], None, ALU.mult)
                if which == "k":
                    for h in range(2):
                        last = v.tensor_scalar(kzi[u][:, :, h, :], ks[par][:, :, u, TXT:S], cst[0:AUG, C_Z + h:C_Z + h + 1], None, ALU.mult)
                inc(last, name)

            def maxima(i, u):
                for n in range(8):
                    wait(dve, "pe_S", i * 16 + (8 * u + n + 1))
                    if n == 0:
                        wait(dve, "pe_A", i * 2 + (u - 1))
                    b = bank[2 + n % 2][:, 0:2 * S].rearrange("p (h t) -> p h t", h=2)
                    if n < 6:
                        last = v.tensor_reduce(mmax[u][:, 2 * n:2 * n + 2], b, AX, ALU.max)
                    elif n == 6:
                        last = v.tensor_reduce(mrem[u][:, 0, :], b, AX, ALU.max)
                    else:
                        last = v.tensor_reduce(mrem[u][0:64, 1, :], b[0:64], AX, ALU.max)
                    inc(last, "dv_S")

            def value_rows(i, u):
                wait(dve, "pe_V", i * 2 + u + 1)
                wait(dve, "pe_PV", i * 2 + (u - 1))
                wait(dve, "po_vb", i * 2 + u)
                b = bank[2 + u]
                bias = rowv[:, 2, :].rearrange("p (h d) -> p h d", h=HEADS)
                v.tensor_tensor(vt[u][:, :, 0:DH], b[:, 0:D].rearrange("p (h d) -> p h d", h=HEADS), bias, ALU.add)
                inc(v.tensor_tensor(vtmp, b[:, D:2 * D], rowv[:, 2, :], ALU.add), "dv_V")

            def normalise(i, par, u):
                wait(dve, "pe_PV", i * 2 + u + 1, alone=True)
                wait(dve, "po_vb", i * 2 + 2, alone=True)
                link(v.stream_shuffle(rden, bank[6][:, 0:3 * S], [16 + k % 16 for k in range(32)]))
                link(v.reciprocal(rden, rden))
                wait(dve, "pe_OP", i * 2 + (u - 1))
                inc(v.tensor_tensor(ot[u].rearrange("p j t -> p (j t)"), bank[6][:, 0:3 * S], rden, ALU.mult), "dv_n")
                wait(dve, "dv_n", i * 2 + u + 1)
                dst = oti.rearrange("p j i (b t) -> p j (i b) t", b=8)[:, :, bass.ds(i * 2 + u, 1), :].rearrange("p j b t -> p j (b t)")
                link(v.tensor_copy(dst, ot[u][:, :, TXT:S]))

            def residual(i, u):
                wait(dve, "pe_OP", i * 2 + u + 1)
                t = h1[:, bass.ds(i * 2 + u, 1), :].rearrange("p a d -> p (a d)")
                inc(v.tensor_tensor(t, bank[2 + u][:, 0:D], t, ALU.add), "dv_h")

            def post_stats(i):
                wait(dve, "dv_h", i * 2 + 2, alone=True)
                inc(norm_stats(lambda u: h1[:, bass.ds(i * 2 + u, 1), :].rearrange("p a d -> p (a d)"), 2), "dv_var")

            def post_rows(i):
                wait(dve, "po_rs", i + 1)
                for u in range(2):
                    t = h1[:, bass.ds(i * 2 + u, 1), :].rearrange("p a d -> p (a d)")
                    last = v.tensor_scalar(xn32[:, u, :], t, mv[:, u, 0:1], rs[:, u:u + 1], ALU.subtract, ALU.mult)
                link(last)
                dve.wait_ge(sm_["row_st"], i * 64) if not (isinstance(i, int) and i == 0) else None
                link(v.tensor_copy(rowb[:, :, 0, 0:D].bitcast(F16)[:, :, 0:D], xn32[:]))
                r = rowb[:, :, 0, 0:D].bitcast(F16)
                v.tensor_tensor(r[:, :, D:2 * P], xn32[:, :, P:D], r[:, :, P:D], ALU.subtract)
                inc(v.tensor_tensor(r[:, :, 2 * P:3 * P], xn32[:, :, 0:P], r[:, :, 0:P], ALU.subtract), "dv_hl")

            def post_x2(i):
                wait(dve, "pe_T", i + 1)
                inc(v.tensor_copy(x2.rearrange("p u c t -> p (u c t)"), bank[7][:].bitcast(F16)[:, 0:6 * P]), "dv_x2")

            def each(ap):
                return ap.rearrange("p (u o) -> p u o", o=1).broadcast_to([P, 2, E])

            def const8(c):
                return cst[:, c:c + E].rearrange("p (o e) -> p o e", o=1).broadcast_to([P, 2, E])

            def post_logits(i):
                wait(dve, "pe_R", i + 1)
                l = bank[7][:, 384:400].rearrange("p (u e) -> p u e", u=2)
                link(v.tensor_reduce(sm[:, 0, :], l, AX, ALU.max))
                inc(v.tensor_tensor(lg, l, each(sm[:, 0, :]), ALU.subtract), "dv_l")

            def post_top2(i):
                wait(dve, "ac_sm", i + 1)
                link(v.tensor_reduce(sm[:, 1, :], pr, AX, ALU.add))
                link(v.reciprocal(sm[:, 1, :], sm[:, 1, :]))
                link(v.tensor_tensor(pr, pr, each(sm[:, 1, :]), ALU.mult))
                for k in range(2):
                    link(v.tensor_reduce(sm[:, 2 + k, :], pr, AX, ALU.max))
                    link(v.tensor_tensor(tm, pr, each(sm[:, 2 + k, :]), ALU.is_equal))
                    link(v.tensor_tensor(tm, tm, const8(C_DESC), ALU.mult))
                    link(v.tensor_reduce(sm[:, 4, :], tm, AX, ALU.max))
                    link(v.tensor_tensor(oh[:, k, :, :], const8(C_DESC), each(sm[:, 4, :]), ALU.is_equal))
                    if k == 0:
                        link(v.scalar_tensor_tensor(pr.rearrange("p u e -> p (u e)"), oh[:, 0, :, :].rearrange("p u e -> p (u e)"), -4.0,
                                                    pr.rearrange("p u e -> p (u e)"), ALU.mult, ALU.add))
                wait(dve, "po_row", i + 1)
                for k in range(2):
                    v.tensor_copy(rowb[:, :, k, ROW_GATE:ROW_GATE + 1].rearrange("p u o -> p (u o)"), sm[:, 2 + k, :])
                inc(v.tensor_tensor(a16, oh[:, 0, :, :], oh[:, 1, :, :], ALU.add), "dv_A")

            def post_pos(i):
                wait(dve, "pe_K", i + 1)
                link(v.tensor_tensor(lg, bank[7][:, 400:416].rearrange("p (u e) -> p u e", u=2), const8(C_ER), ALU.add))
                for k in range(2):
                    link(v.tensor_tensor(tm, lg, oh[:, k, :, :], ALU.mult))
                    link(v.tensor_reduce(sm[:, 5 + k, :], tm, AX, ALU.add))
                for u in range(2):
                    link(v.tensor_tensor(acc16, acc16, a16[:, u, :], ALU.add))
                inc(v.tensor_copy(pos, sm[:, 5:7, :]), "dv_pos")

            stacks(0, 0, range(12))
            separate("k", 0, 0, 0)
            separate("k", 0, 0, 1)

            def step(dve, i, par):
                first, last_ = isinstance(i, int) and i == 0, isinstance(i, int) and i == STEPS - 1
                maxima(i, 0)
                maxima(i, 1)
                if not last_:
                    stacks(i + 1, 1 - par, range(0, 6))
                if not first:
                    post_rows(i - 1)
                separate("q", i, par, 0)
                if not last_:
                    stacks(i + 1, 1 - par, range(6, 8))
                separate("q", i, par, 1)
                if not last_:
                    stacks(i + 1, 1 - par, range(8, 9))
                if not first:
                    post_x2(i - 1)
                value_rows(i, 0)
                value_rows(i, 1)
                if not first:
                    post_logits(i - 1)
                if not last_:
                    stacks(i + 1, 1 - par, range(9, 12))
                if not first:
                    post_top2(i - 1)
                if not last_:
                    separate("k", i + 1, 1 - par, 0)
                normalise(i, par, 0)
                if not last_:
                    separate("k", i + 1, 1 - par, 1)
                if not first:
                    post_pos(i - 1)
                normalise(i, par, 1)
                residual(i, 0)
                residual(i, 1)
                post_stats(i)

            link.per = 64
            attention(step, dve, link)
            post_rows(STEPS - 1)
            post_x2(STEPS - 1)
            post_logits(STEPS - 1)
            post_top2(STEPS - 1)
            post_pos(STEPS - 1)
            residual(STEPS, 0)
            residual(STEPS, 1)
            post_stats(STEPS)
            post_rows(STEPS)
            post_x2(STEPS)
            post_logits(STEPS)
            post_top2(STEPS)
            post_pos(STEPS)
            wait(dve, "pe_cnt", 1)
            wait(dve, "dv_pos", STEPS + 1)
            cnt, til, cum, fl = ctab[0:1, 0:8], ctab[0:1, 8:16], ctab[0:1, 16:24], ctab[0:1, 24:32]
            link(v.tensor_copy(cnt, bank[7][0:1, 416:424]))
            link(v.tensor_scalar(fl, cnt, 127.0, None, ALU.add))
            link(v.tensor_copy(itab[0:1, 64:72], fl))
            link(v.tensor_scalar(itab[0:1, 120:128], itab[0:1, 64:72], 7, None, ALU.arith_shift_right))
            link(v.tensor_copy(til, itab[0:1, 120:128]))
            pairs8 = ctab[0:1, 32:96].rearrange("p (a b) -> p a b", a=E)
            link(v.tensor_tensor(pairs8, til.rearrange("p (o e) -> p o e", o=1).broadcast_to([1, E, E]),
                                 cst[0:1, C_TRI:C_TRI + E * E].rearrange("p (a b) -> p a b", a=E), ALU.mult))
            link(v.tensor_reduce(cum, pairs8, AX, ALU.add))
            NS = SLOTS + 1
            ge = ctab[0:1, 96:96 + NS * E].rearrange("p (s e) -> p s e", s=NS)
            st = ctab[0:1, 460:460 + NS]
            ex = ctab[0:1, 510:510 + NS]
            slots = cst[0:1, C_SLOT:C_SLOT + NS]
            link(v.tensor_tensor(ge, slots.rearrange("p (s o) -> p s o", o=1).broadcast_to([1, NS, E]),
                                 cum.rearrange("p (o e) -> p o e", o=1).broadcast_to([1, NS, E]), ALU.is_ge))
            link(v.tensor_reduce(ex, ge, AX, ALU.add))
            link(v.tensor_tensor(ge, ge, til.rearrange("p (o e) -> p o e", o=1).broadcast_to([1, NS, E]), ALU.mult))
            link(v.tensor_reduce(st, ge, AX, ALU.add))
            link(v.tensor_tensor(st, slots, st, ALU.subtract))
            link(v.tensor_scalar(st, st, float(P), None, ALU.mult))
            link(v.scalar_tensor_tensor(st, ex, float(REGION), st, ALU.mult, ALU.add))
            v.tensor_scalar(itab[0:1, 0:NS], st, float(SPARE), None, ALU.min)
            v.tensor_scalar(itab[0:1, 72:72 + NS], ex, float(E - 1), None, ALU.min)
            inc(v.tensor_tensor(itab[0:1, 64:72], cnt, cst[0:1, C_ER:C_ER + E], ALU.add), "dv_tab")

            def low_g(s, p, half):
                wait(dve, "ac_g", s * 2 + half + 1)
                q, (a, b) = p % 2, ((0, 512), (512, DFF))[half]
                inc(v.tensor_tensor(gl[q][:, a:b], g32[q][:, a:b], gh[q][:, a:b], ALU.subtract), "dv_gl")

            def slot_x(s, p):
                wait(dve, "pe_mT", s + 1)
                wait(dve, "pe_LB", s - 3)
                inc(v.tensor_copy(xe[p].rearrange("p c t -> p (c t)"), bank[4 + p % 2][:].bitcast(F16)[:, 0:3 * P]), "dv_mT")

            def slot_y(s, p):
                wait(dve, "pe_L2", s + 1)
                if not isinstance(s, int) or s >= 4:
                    dve.wait_ge(y_st[p], (s - p) * 4)
                inc(v.tensor_scalar(yb[p], bank[6 + p % 2][:, 0:D], xr[p][:, ROW_GATE:ROW_GATE + 1], None, ALU.mult), "dv_y")

            slot_x(0, 0)
            for s in range(3):
                low_g(s, s, 0)
                slot_x(s + 1, s + 1)
                low_g(s, s, 1)
                if s:
                    slot_y(s - 1, s - 1)
            with dve.Fori(0, (SLOTS - 3) // 4) as j:
                for n in range(4):
                    p, s = (3 + n) % 4, j * 4 + (3 + n)
                    low_g(s, p, 0)
                    slot_x(s + 1, (p + 1) % 4)
                    low_g(s, p, 1)
                    slot_y(s - 1, (p - 1) % 4)
            slot_y(SLOTS - 1, (SLOTS - 1) % 4)

            def finish(t, p, uses):
                dve.wait_ge(yk_ld[p], uses)
                res = h1[:, bass.ds(t, 1), :].rearrange("p a d -> p (a d)")
                link(v.tensor_tensor(yk[p][:, 0:D], yk[p][:, 0:D], yk[p][:, D:2 * D], ALU.add))
                inc(v.tensor_tensor(of[p], res, yk[p][:, 0:D], ALU.add), "dv_out")

            n0 = link.base + link.n
            with dve.Fori(0, 4) as j:
                link.base, link.n = j * 4 + n0, 0
                for p in range(4):
                    if p == 0:
                        dve.wait_ge(out_st, j * 64)
                    finish(j * 4 + p, p, j * 16 + 16)
            link.base, link.n = n0 + 16, 0
            dve.wait_ge(out_st, 16 * 16)
            for i in range(2):
                finish(16 + i, i, 4 * 16 + 8 * 16)

        @block.gpsimd
        def _(pool):
            g = nc.gpsimd
            link = Link(pool, sm_["po_link"])
            link(g.memset(nhalf[:], -0.5))

            def powers(n):
                return g.tensor_tensor(rs[:, 0:n], ve[:, 0:n], nhalf[:, 0:n], ALU.pow)

            wait(pool, "dv_var0", 1, alone=True)
            inc(powers(2), "po_rs0")

            pool.wait_ge(ld_wa, 48)
            pool.wait_ge(ld_wp, 80)
            for k in range(2):
                g.tensor_copy(wt16[:, 2 * k, :], wa32[:, k, 0:2 * D])
                g.tensor_copy(wv[:, 2 * k, :], wa32[:, k, 2 * D:3 * D])
                last = g.tensor_copy(rw[:, 2 * k, :], rw32[:, k, :])
            link(last)
            for k in range(2):
                g.tensor_tensor(wt16[:, 2 * k + 1, :], wa32[:, k, 0:2 * D], wt16[:, 2 * k, :], ALU.subtract)
                g.tensor_tensor(wv[:, 2 * k + 1, :], wa32[:, k, 2 * D:3 * D], wv[:, 2 * k, :], ALU.subtract)
                last = g.tensor_tensor(rw[:, 2 * k + 1, :], rw32[:, k, :], rw[:, 2 * k, :], ALU.subtract)
            link(last)
            for i in range(1):
                wait(pool, "dv_var0", 2, alone=True)
                inc(powers(2), "po_rs0")
            for k in range(4):
                for s in range(3):
                    dst = wqk[:, k, :, :].rearrange("p r (h s d) -> p (r h) s d", h=2, s=3)[:, :, s, :]
                    last = g.tensor_copy(dst, wt16[:, k, :].rearrange("p (n d) -> p n d", d=DH))
            link(last)
            with pool.Fori(0, STEPS) as j:
                wait(pool, "dv_var0", j + 3, alone=True)
                inc(powers(2), "po_rs0")
            wait(pool, "dv_xt", NT, alone=True)
            wait(pool, "pe_xt", NT, alone=True)
            wait(pool, "pe_tm", CH, alone=True)
            for u in range(2):
                g.memset(vt[u][:, :, DH:32], 1.0)
                for k in range(DH):
                    g.tensor_copy(vb[u][:, :, DH + k:DH + k + 1].rearrange("p h o -> p (h o)"), cst[:, C_VM:C_VM + HEADS])
            g.memset(padrow, 0.0)
            g.memset(mrem[0], 0.0)
            link(g.memset(mrem[1], 0.0))
            link(g.memset(padrow[:, ROW_ID:ROW_ID + 1].bitcast(I32), 1 << 24))
            last = g.memset(rowb.rearrange("p u k w -> p (u k w)"), 0.0)
            inc(last, "po_const")
            wait(pool, "po_const", 1, alone=True)

            def block_values(i, u):
                wait(pool, "dv_V", i * 2 + u + 1, alone=True)
                m = cst[:, C_VM:C_VM + HEADS].rearrange("p (h o) -> p h o", o=1).broadcast_to([P, HEADS, DH])
                inc(g.tensor_tensor(vb[u][:, :, 0:DH], vtmp.rearrange("p (h d) -> p h d", h=HEADS), m, ALU.mult), "po_vb")

            def image_rows(i, u):
                wait(pool, "pe_V", i * 2 + (u - 1), alone=True)
                for c in range(3):
                    src = xt[:, c:c + 1, bass.ds((i * 2 + u) * S + TXT, IMG)].broadcast_to([P, 8, IMG])
                    last = g.tensor_copy(xrep[u][:, c, :].rearrange("p (b t) -> p b t", b=8), src)
                inc(last, "po_xrep")

            def rows_twice(i):
                wait(pool, "dv_hl", i + 1, alone=True)
                for k in range(2):
                    src = cst[:, C_TID:C_TID + 2 * NT].rearrange("p (t k) -> p t k", k=2)[:, bass.ds(i * 2, 2), k:k + 1]
                    g.tensor_copy(rowb[:, :, k, ROW_ID:ROW_ID + 1].bitcast(I32), src)
                inc(g.tensor_copy(rowb[:, :, 1, 0:D], rowb[:, :, 0, 0:D]), "po_row")

            def scatter(i):
                wait(pool, "dv_pos", i + 1, alone=True)
                for u in range(2):
                    for k in range(2):
                        g.indirect_dma_start(routed[:, :], bass.IndirectOffsetOnAxis(ap=pos[:, k, u:u + 1], axis=0),
                                             rowb[:, u, k, :], None).then_inc(sm_["row_st"], 16)

            def split(e):
                parts = ((0, DFF, w1s, 0, 0), (1, DFF, w1s, 2, 0), (2, 4 * D, w2s, 0, 0), (0, 2 * D, w2s, 0, 4 * D))
                for n, (slot_, size, dst, k, at) in enumerate(parts):
                    per = 32 if n == 1 else 16
                    wait(pool, ld_stage[n], e * per + per, alone=True)
                    hi = dst[:, bass.ds(e, 1), k, at:at + size].rearrange("p a f -> p (a f)")
                    lo = dst[:, bass.ds(e, 1), k + 1, at:at + size].rearrange("p a f -> p (a f)")
                    inc(g.tensor_copy(hi, stage[:, slot_, 0:size]), "po_split")
                    wait(pool, "po_split", e * 8 + (2 * n + 1), alone=True)
                    last = g.tensor_tensor(lo, stage[:, slot_, 0:size], hi, ALU.subtract)
                    inc(last, "po_split")

            def step(pool, i, par):
                first = isinstance(i, int) and i == 0
                if not first:
                    rows_twice(i - 1)
                image_rows(i, 0)
                image_rows(i, 1)
                block_values(i, 0)
                block_values(i, 1)
                split(i)
                if not first:
                    scatter(i - 1)
                wait(pool, "dv_var", i + 1, alone=True)
                inc(powers(2), "po_rs")

            attention(step, pool)
            rows_twice(STEPS - 1)
            scatter(STEPS - 1)
            wait(pool, "dv_var", STEPS + 1, alone=True)
            inc(powers(2), "po_rs")
            rows_twice(STEPS)
            scatter(STEPS)

            bound = g.to_reg(N * TOPK - 1)

            def put(s, p):
                wait(pool, "dv_y", s + 1 if isinstance(s, int) else g.to_reg(s + 1), alone=True)
                g.indirect_dma_start(expert_out[:, :], bass.IndirectOffsetOnAxis(ap=xr[p][:, ROW_ID:ROW_ID + 1].bitcast(U32), axis=0),
                                     yb[p], None, bounds_check=bound, oob_is_err=False).then_inc(y_st[p], 16)

            for s in range(3):
                put(s, s)
            with pool.Fori(0, (SLOTS - 3) // 4) as j:
                for n in range(4):
                    put(j * 4 + (3 + n), (3 + n) % 4)


def constants():
    import numpy as np
    c = np.zeros((P, NCONST), np.float32)
    r = np.arange(P)
    c[:, C_ID:C_ID + P] = np.eye(P)
    c[:, C_UP:C_UP + P] = r[:, None] < r[None, :]
    part = (r[:STK] // DH) % 3
    c[:STK, C_LOQ] = part == 2
    c[:STK, C_LOK] = part == 1
    for h in range(2):
        c[48 * h:48 * h + 48, C_Z + h] = 1
        c[STK + h, C_Z + h] = 1
    head = np.arange(HEADS)
    c[:, C_VM:C_VM + HEADS] = (r[:, None] // IMG) == (head[None, :] % 8)
    c[:, C_DESC:C_DESC + E] = E - np.arange(E)
    c[:, C_ER:C_ER + E] = np.arange(E) * REGION
    for t in range(NT):
        token = t * S + IMG + r if t < B else ((t - B) * 8 + r // IMG) * S + r % IMG
        for k in range(2):
            c[:, C_TID + 2 * t + k] = 2 * token + k
    c[:, C_SLOT:C_SLOT + SLOTS + 1] = np.arange(SLOTS + 1)
    c[:, C_TRI:] = np.tril(np.ones((E, E))).ravel()
    return c


def kernel(x, txt, L0_tok_gamma, L0_tok_beta, L0_tok_W, L0_tok_b, L0_attn_w_attn, L0_attn_b_attn, L0_attn_w_proj,
           L0_attn_b_proj, L0_ffn_router_w, L0_ffn_w1, L0_ffn_w2):
    import numpy as np
    import concourse.bacc as bacc
    from concourse.bass_utils import run_bass_kernel_spmd

    x = np.asarray(x)
    xp = np.pad(x, ((0, 0), (1, 1), (1, 1), (0, 0)))
    halo = np.stack([xp[:, 16 * a:16 * a + 18, 16 * b:16 * b + 18, :] for a in range(4) for b in range(4)], 1)

    def by_shift(a):
        a = np.asarray(a).reshape(8, 2, 16, 5, 3, -1)
        a = a.transpose(1, 2, 4, 3, 0, 5).reshape(2, 48, CH, -1)
        return np.pad(a, ((0, 0), (0, 6), (0, 0), (0, 0))).reshape(108, CH, -1)[:CK]

    ba = np.asarray(L0_attn_b_attn)
    bqk = np.tile(ba[:2 * D].reshape(2 * PAIRS, 2, 1, DH), (1, 1, 3, 1)).reshape(2 * PAIRS, STK).T
    wp = np.zeros((4, 32, 3, D), np.float32)
    wp[:, :DH] = np.asarray(L0_attn_w_proj).reshape(3, 4, DH, D).transpose(1, 2, 0, 3)
    arrays = {
        "a_halo": halo.reshape(B * IMG, HALO),
        "a_txt": np.asarray(txt),
        "a_tok_w": by_shift(L0_tok_W),
        "a_tok_gb": np.stack([by_shift(L0_tok_gamma)[..., 0], by_shift(L0_tok_beta)[..., 0]], 1),
        "a_rows": np.stack([np.asarray(L0_tok_b), np.asarray(L0_attn_b_proj), ba[2 * D:]]),
        "a_bqk": bqk,
        "a_w_attn": np.asarray(L0_attn_w_attn),
        "a_w_proj": wp.reshape(P, 3, D),
        "a_router": np.asarray(L0_ffn_router_w).T,
        "a_w1": np.asarray(L0_ffn_w1),
        "a_w2": np.asarray(L0_ffn_w2),
        "a_consts": constants(),
    }
    arrays = {k: np.ascontiguousarray(a) for k, a in arrays.items()}
    nc = bacc.Bacc("TRN2", target_bir_lowering=False, num_devices=1)
    args = [nc.dram_tensor(k, a.shape, mybir.dt.from_np(a.dtype), kind="ExternalInput").ap() for k, a in arrays.items()]
    out = nc.dram_tensor("out", (B, S, D), F32, kind="ExternalOutput").ap()
    build_program(nc, *args, out)
    r = run_bass_kernel_spmd(nc, [arrays], core_ids=[0])
    return r.results[0]["out"]
```

```python
from contextlib import ExitStack

import concourse.bass as bass
from concourse import mybir

F32 = mybir.dt.float32
F16 = mybir.dt.float16
I32 = mybir.dt.int32
U32 = mybir.dt.uint32
ALU = mybir.AluOpType
ACT = mybir.ActivationFunctionType
AX = mybir.AxisListType.X

P = 128
B, TXT, IMG, D = 16, 128, 16, 192
S = TXT + IMG
N = B * S
HEADS, DH = 12, 16
PAIRS = HEADS // 2
STK = 2 * 3 * DH
AUG = STK + 2
E, DFF, TOPK = 8, 768, 2
FC = DFF // P
NT = N // P
SR = 2 * P
REGION = N + SR
SPARE = E * REGION
SLOTS = (N * TOPK - E) // SR + E
ROW = 196
ROW_ID, ROW_GATE = 192, 193
HALO = 18 * 18 * 3
TG = 10
CH, CK = 40, 54 + 48
EPS_TOK, EPS_LN = 1e-3, 1e-5
AREA = 17250
STEPS = B // 2
NBLK = -(-3 * S // 32)
XT_AT = 7
SHIFTS = ((1, 1), (1, 0), (1, 2), (0, 1), (2, 1))

C_ID, C_UP = 0, 128
C_LOQ, C_LOK = 256, 257
C_Z = 258
C_VM = 260
C_DESC = 272
C_ER = 280
C_TID = 288
C_SLOT = C_TID + 2 * NT
C_TRI = C_SLOT + SLOTS + 1
NCONST = C_TRI + E * E


def build_program(nc, halo, txt, tok_w, tok_gb, rows, bvt, bqk, w_attn, w_proj, router, w1, w2, consts, out):
    with ExitStack() as ctx:
        def sb(name, shape, dt):
            return ctx.enter_context(nc.sbuf_tensor(name, shape, dt))

        def sem(name):
            return ctx.enter_context(nc.semaphore(name))

        bank = [ctx.enter_context(nc.psum_tensor(f"bank{i}", [P, 512], F32)) for i in range(8)]
        routed = nc.dram_tensor("routed_rows", [SPARE + SR, ROW], F32, kind="Internal")
        expert_out = nc.dram_tensor("expert_out", [N * TOPK, D], F32, kind="Internal")

        cst = sb("cst", [P, NCONST], F32)
        ident = cst[:, C_ID:C_ID + P]
        id16 = sb("id16", [P, P], F16)
        negid16 = sb("negid16", [P, P], F16)
        up16 = sb("up16", [P, P], F16)
        ones16 = sb("ones16", [P, P], F16)
        scrap = sb("scrap", [1, 1], F32)
        nhalf = sb("nhalf", [P, B], F32)
        
        bq = sb("bq", [STK, 2 * PAIRS], F32)
        bqlo = sb("bqlo", [STK, 2 * PAIRS], F32)
        wqk = sb("wqk", [P, 4, 2 * PAIRS, STK], F16)
        wv = sb("wv", [P, 4, D], F16)
        wp = sb("wp", [P, 3, D], F32)
        rw32 = sb("rw32", [P, 2, E], F32)
        rw = sb("rw", [P, 4, E], F16)
        w1s = sb("w1s", [P, E, 4, DFF], F16)
        w2s = sb("w2s", [P, E, 2, FC * D], F16)
        h1 = sb("h1", [P, NT, D], F32)
        xt = sb("xt", [P, 3, N], F16)
        stage = sb("stage", [P, 3, 4 * D], F32)
        mv = sb("mv", [P, NT, 2], F32)
        ve = sb("ve", [P, NT], F32)
        rs = sb("rs", [P, NT], F32)
        bst = sb("bst", [P, 2, 10, 6], F32)
        bst_tiles = bst[:].rearrange("p u k s -> p (u k) s")
        xn32 = sb("xn32", [P, 2, D], F32)
        area = sb("area", [P, AREA], F32)

        def cut(cols, at):
            return area[:, at[0] - cols:at[0]]

        def region(cursor, cols):
            cursor[0] += cols
            assert cursor[0] <= AREA, cursor
            return area[:, cursor[0] - cols:cursor[0]]

        ta = [0]
        patch = region(ta, 2 * HALO).rearrange("p (t f) -> p t f", t=2)
        tokw = region(ta, CH * D)[0:CK, :].rearrange("p (c d) -> p c d", c=CH)
        tokgb = region(ta, 2 * CH)[0:CK, :].rearrange("p (g c) -> p g c", g=2)
        XG = 4
        rowv = region(ta, D)
        xg = region(ta, XG * 256)[0:CK, :].rearrange("p (x t) -> p x t", x=XG)
        hl = region(ta, 4 * D).bitcast(F16).rearrange("p (v u f) -> p v u f", v=2, u=2)
        wa32 = region(ta, 2 * 3 * D).rearrange("p (k f) -> p k f", k=2)
        wt16 = region(ta, 4 * 2 * D // 2).bitcast(F16).rearrange("p (k f) -> p k f", k=4)

        SW = PAIRS * 2 * S

        def stack(cursor):
            return region(cursor, SW // 2)[0:AUG, :].bitcast(F16).rearrange("p (r u t) -> p r u t", r=PAIRS, u=2)

        cc = [ta[0]]
        vts = region(cc, 2 * HEADS * 32).rearrange("p (h d) -> p h d", h=2 * HEADS)
        vt = [vts[:, HEADS * u:HEADS * u + HEADS, :] for u in range(2)]
        vb = [region(cc, HEADS * 32).rearrange("p (h d) -> p h d", h=HEADS) for _ in range(2)]
        mrem = [region(cc, 2).bitcast(F16).rearrange("p (s h) -> p s h", s=2) for _ in range(2)]
        rowb = region(cc, 4 * ROW).rearrange("p (u k w) -> p u k w", u=2, k=2)
        acc16 = region(cc, 4).bitcast(F16)
        padrow = region(cc, ROW)
        ks = [stack(cc)]
        bv = region(cc, 3 * 32).rearrange("p (j c) -> p j c", j=3)
        top = region(cc, 16).rearrange("p (u e) -> p u e", u=2)
        topi = region(cc, 16).bitcast(U32).rearrange("p (u e) -> p u e", u=2)
        topf = region(cc, 4).rearrange("p (u k) -> p u k", u=2)
        lg = region(cc, 16).rearrange("p (u e) -> p u e", u=2)
        pr = region(cc, 16).rearrange("p (u e) -> p u e", u=2)
        oh = region(cc, 32).rearrange("p (u k e) -> p u k e", u=2, k=2)
        place = region(cc, 16).rearrange("p (u e) -> p u e", u=2)
        hit = region(cc, 32).rearrange("p (u k e) -> p u k e", u=2, k=2)
        den = region(cc, 2)
        aa = [0]
        ks.append(stack(aa))
        qs = [stack(aa) for _ in range(2)]
        qz = [region(aa, SW // 2)[0:AUG, :].bitcast(F16).rearrange("p (h r t) -> p h r t", h=2, r=PAIRS) for _ in range(2)]
        kz = [region(aa, SW // 2)[0:AUG, :].bitcast(F16).rearrange("p (h r t) -> p h r t", h=2, r=PAIRS) for _ in range(2)]
        hm = [region(aa, S)[0:STK, :].bitcast(F16) for _ in range(2)]
        pt = [region(aa, HEADS * S).rearrange("p (h t) -> p h t", h=HEADS) for _ in range(2)]
        ptr = [region(aa, 2 * S).rearrange("p (s t) -> p s t", s=2) for _ in range(2)]
        xrep = [region(aa, 3 * P // 2).bitcast(F16).rearrange("p (c t) -> p c t", c=3) for _ in range(2)]
        kzi = [region(aa, PAIRS * 16)[0:AUG, :].bitcast(F16).rearrange("p (r h t) -> p r h t", r=PAIRS, h=2) for _ in range(2)]
        mmax = [region(aa, 6).bitcast(F16) for _ in range(2)]
        rden = region(aa, NBLK * 32)
        rec = region(aa, NBLK)
        ot = [region(aa, 3 * S).rearrange("p (j t) -> p j t", j=3) for _ in range(2)]
        oti = region(aa, 3 * 2 * P).rearrange("p (j i t) -> p j i t", j=3, i=2)
        x2 = region(aa, 2 * 3 * P // 2).bitcast(F16).rearrange("p (u c t) -> p u c t", u=2, c=3)
        a16 = region(aa, 8).bitcast(F16).rearrange("p (u e) -> p u e", u=2)
        pos = region(aa, 4).bitcast(U32).rearrange("p (u k) -> p u k", u=2)
        assert aa[0] <= ta[0], (aa, ta)
        ctab = pt[0].rearrange("p h t -> p (h t)")

        ea = [0]
        xr = [region(ea, 2 * ROW).rearrange("p (h w) -> p h w", h=2) for _ in range(4)]
        xe = [region(ea, 3 * SR // 2).bitcast(F16).rearrange("p (c t) -> p c t", c=3) for _ in range(2)]
        g32 = [region(ea, 2 * SR) for _ in range(3)]
        gh = [region(ea, FC * SR // 2).bitcast(F16) for _ in range(2)]
        gl = [region(ea, FC * SR // 2).bitcast(F16) for _ in range(2)]
        yb = [region(ea, 2 * D).rearrange("p (h d) -> p h d", h=2) for _ in range(4)]
        yk = [region(ea, 2 * D) for _ in range(4)]
        of = [region(ea, D) for _ in range(4)]
        itab = sb("itab", [1, 128], I32)

        (ld_c, ld_halo, ld_tw, ld_row, ld_txt, ld_wa, ld_wp, ld_st, pads_in, slot_in, yk_in, out_st) = [sem(n) for n in (
            "ld_c", "ld_halo", "ld_tw", "ld_row", "ld_txt", "ld_wa", "ld_wp", "ld_st", "pads_in", "slot_in", "yk_in", "out_st")]
        slot_ld = [sem(f"slot_ld{i}") for i in range(4)]
        y_st = [sem(f"y_st{i}") for i in range(4)]
        yk_ld = [sem(f"yk_ld{i}") for i in range(4)]
        ld_txts = [sem(f"ld_txt{i}") for i in range(2)]
        ld_tws = [sem(f"ld_tw{i}") for i in range(4)]
        ld_stage = [sem(f"ld_stage{i}") for i in range(4)]
        names = ("pe_tt pe_tm pe_xt pe_P pe_S pe_A pe_V pe_ST pe_PV pe_OP pe_T pe_R pe_K pe_cnt pe_mT pe_up pe_L2 "
                 "ac_tg ac_hm ac_aux ac_exp ac_sm ac_hl ac_gh ac_g ac_misc ac_xt ac_vt ac_x2 ac_split dv_vb dv_wp pe_bv "
                 "dv_pre dv_var0 dv_patch dv_tg dv_hl0 dv_xt dv_st dv_kz dv_qz dv_S dv_n dv_h dv_var dv_hl dv_x2 dv_l dv_A "
                 "dv_pos dv_tab dv_mT dv_gl dv_y dv_out dv_link "
                 "po_xrep po_rs0 po_rs po_row po_split po_link po_const po_wqk row_st").split()
        sm_ = {n: sem(n) for n in names}

        class Link:

            def __init__(self, eng, semaphore):
                self.eng, self.sem, self.base, self.n = eng, semaphore, 0, 0

            def put(self, ins):
                self.n += 1
                ins.then_inc(self.sem, 1)
                return self.base + self.n

            def __call__(self, ins, alone=False):
                wait(self.eng, self.sem, self.put(ins), alone)

        def wait(eng, name, value, alone=False):
            if isinstance(value, int) and value <= 0:
                return
            if alone and not isinstance(value, int):
                eng.wait_ge(ld_c, 16)
            eng.wait_ge(sm_[name] if isinstance(name, str) else name, value)

        def inc(ins, name, by=1):
            ins.then_inc(sm_[name], by)

        def halo_rows(t, shift, rb):
            dr, dc = SHIFTS[shift]
            at = (2 * rb + dr) * 54 + 3 * dc
            return patch[:, t, at:at + CK]

        def attention(step, eng, tally=None):
            step(eng, 0, 0)
            if tally:
                first = tally.base + tally.n
            with eng.Fori(0, (STEPS - 2) // 2) as j:
                if tally:
                    per = tally.per
                    tally.base, tally.n = j * per + first, 0
                step(eng, j * 2 + 1, 1)
                step(eng, j * 2 + 2, 0)
                if tally:
                    assert tally.n == per, (tally.n, per)
            if tally:
                tally.base, tally.n = first + per * ((STEPS - 2) // 2), 0
            step(eng, STEPS - 1, 1)

        PARTS = ((0, DFF, w1s, 0, 0), (1, DFF, w1s, 2, 0), (2, 4 * D, w2s, 0, 0), (0, 2 * D, w2s, 0, 4 * D))

        block = ctx.enter_context(nc.Block())

        @block.sync
        def _(sp):
            sp.dma_start(patch, halo.rearrange("(t p) f -> p t f", t=2)).then_inc(ld_halo, 16)
            sp.dma_start(cst[:], consts).then_inc(ld_c, 16)
            sp.dma_start(tokgb, tok_gb).then_inc(ld_tw, 16)

            def token_weights(g):
                sp.dma_start(tokw[:, TG * g:TG * g + TG, :], tok_w[:, TG * g:TG * g + TG, :]).then_inc(ld_tws[g], 16)

            token_weights(0)
            for u in range(2):
                sp.dma_start(h1[:, 8 * u:8 * u + 8, :], txt[8 * u:8 * u + 8].rearrange("b p d -> p b d")).then_inc(ld_txts[u], 16)
            token_weights(1)
            sp.dma_start(wa32[:, 0, :], w_attn[0:P, :]).then_inc(ld_wa, 16)
            sp.dma_start(wa32[0:64, 1, :], w_attn[P:D, :]).then_inc(ld_wa, 16)
            sp.dma_start(wa32[64:P, 1, :], w_attn[P:D, :]).then_inc(ld_wa, 16)
            token_weights(2)
            token_weights(3)
            sp.dma_start(rowv, rows.broadcast_to([P, D])).then_inc(ld_row, 16)
            sp.dma_start(bv, bvt).then_inc(ld_wp, 16)
            sp.dma_start(bq[:], bqk).then_inc(ld_wp, 16)
            sp.dma_start(wp[:], w_proj).then_inc(ld_wp, 16)
            sp.dma_start(rw32[:, 0, :], router[0:P, :]).then_inc(ld_wp, 16)
            sp.dma_start(rw32[0:64, 1, :], router[P:D, :]).then_inc(ld_wp, 16)
            sp.dma_start(rw32[64:P, 1, :], router[P:D, :]).then_inc(ld_wp, 16)
            with sp.Fori(0, E) as e:
                sp.wait_ge(sm_["po_wqk"], 1)
                wait(sp, "po_split", e * 4, alone=True)
                s = stage
                v = w1.rearrange("e d f -> (e d) f")
                sp.dma_start(s[:, 0, :], v[bass.ds(e * D, P), :]).then_inc(ld_stage[0], 16)
                sp.dma_start(s[0:64, 1, :], v[bass.ds(e * D + P, 64), :]).then_inc(ld_stage[1], 16)
                sp.dma_start(s[64:P, 1, :], v[bass.ds(e * D + P, 64), :]).then_inc(ld_stage[1], 16)
                v = w2.rearrange("e f d -> (e f) d")
                sp.dma_start(s[:, 2, :].rearrange("p (c d) -> p c d", c=4),
                             v[bass.ds(e * DFF, 4 * P), :].rearrange("(c p) d -> p c d", c=4)).then_inc(ld_stage[2], 16)
                wait(sp, "po_split", e * 4 + 1, alone=True)
                sp.dma_start(s[:, 0, 0:2 * D].rearrange("p (c d) -> p c d", c=2),
                             v[bass.ds(e * DFF + 4 * P, 2 * P), :].rearrange("(c p) d -> p c d", c=2)).then_inc(ld_stage[3], 16)
            sp.wait_ge(sm_["dv_tab"], 1)
            twice = padrow.rearrange("p (o w) -> p o w", o=1).broadcast_to([P, 2, ROW])
            sp.dma_start(routed[SPARE:SPARE + SR, :].rearrange("(p h) w -> p h w", h=2), twice).then_inc(pads_in, 16)
            for e in range(E):
                r = nc.sync.value_load(itab[0:1, 64 + e:65 + e], min_val=0, max_val=SPARE - SR)
                sp.dma_start(routed[bass.ds(r, SR), :].rearrange("(p h) w -> p h w", h=2), twice).then_inc(pads_in, 16)
            sp.wait_ge(pads_in, 16 * (E + 1))
            sp.wait_ge(sm_["row_st"], 16 * 4 * (STEPS + 1))

            def slot(s, p):
                r = nc.sync.value_load(itab[0:1, bass.ds(s, 1)], min_val=0, max_val=SPARE)
                if not isinstance(s, int) or s >= 4:
                    sp.wait_ge(y_st[p], (s - p) * 8)
                sp.dma_start(xr[p], routed[bass.ds(r, SR), :].rearrange("(p h) w -> p h w", h=2)).then_inc(slot_ld[p], 16)

            for s in range(6):
                slot(s, s % 4)
            with sp.Fori(0, (SLOTS - 5) // 4) as j:
                for n in range(4):
                    slot(j * 4 + (6 + n), (6 + n) % 4)
            for p in range(4):
                sp.wait_ge(y_st[p], 32 * len(range(p, SLOTS, 4)))
            ykv = expert_out.rearrange("(t k) d -> t (k d)", k=2)
            with sp.Fori(0, 4) as j:
                for p in range(4):
                    wait(sp, "dv_out", j * 4, alone=True)
                    sp.dma_start(yk[p], ykv[bass.ds(j * 4 * S + (p * S + IMG), P), :]).then_inc(yk_ld[p], 16)
            sp.wait_ge(sm_["dv_out"], 14)
            for i in range(2):
                v = ykv.rearrange("(i b t) w -> i b t w", i=2, t=S)[i, :, 0:IMG, :]
                for b in range(8):
                    sp.dma_start(yk[i][16 * b:16 * b + 16, :], v[b]).then_inc(yk_ld[i], 16)

        @block.tensor
        def _(pe):
            mm = nc.tensor.matmul
            pe.wait_ge(ld_c, 16)

            def transposes(c):
                if c == 0:
                    pe.wait_ge(sm_["dv_patch"], 2)
                wait(pe, "dv_tg" if c % 2 == 0 else "ac_tg", c // 2)
                for t in range(2):
                    last = nc.tensor.transpose(bank[c % 2][0:CK, P * t:P * t + P], halo_rows(t, c // 8, c % 8), ident)
                inc(last, "pe_tt")

            def products(c):
                wait(pe, "dv_tg" if c % 2 == 0 else "ac_tg", c // 2 + 1)
                if c % TG == 0:
                    pe.wait_ge(ld_tws[c // TG], 16)
                for t in range(2):
                    last = mm(bank[2 + t][:, 0:D], xg[:, c % XG, P * t:P * t + P], tokw[:, c, :], start=c == 0, stop=c == CH - 1)
                inc(last, "pe_tm")

            def to_features(i):
                wait(pe, "dv_hl0", i + 1)
                wait(pe, "ac_xt", 2 * (i - 1))
                for u in range(2):
                    o = bank[4 + 2 * (i % 2) + u][:].bitcast(F16)
                    r = hl[:, i % 2, u, :]
                    nc.tensor.transpose(o[:, 0:P], r[:, 0:P], id16[:])
                    nc.tensor.transpose(o[:, P:2 * P], r[:, 2 * P:3 * P], id16[:])
                    inc(nc.tensor.transpose(o[:, 2 * P:3 * P], r[:, P:2 * P], id16[:]), "pe_xt")

            for c in range(CH + 2):
                if c < CH:
                    transposes(c)
                if c >= 2:
                    products(c - 2)
                if c % 2 and 0 <= c // 2 - XT_AT < B // 2:
                    to_features(c // 2 - XT_AT)
            to_features(B // 2)

            def project(i, chunks):
                for c in chunks:
                    b = bank[c % 2]
                    wait(pe, "dv_st", i * 12 + (c - 1))
                    cols = bass.ds(i * 2 * S, 2 * S)
                    for n, (k, t) in enumerate(((0, 0), (1, 0), (0, 1), (2, 2), (3, 2))):
                        last = mm(b[0:STK, 0:2 * S], wqk[:, k, c, :], xt[:, t, cols], start=n == 0, stop=n == 4)
                    inc(last, "pe_P")

            def scores(i, par, u, n):
                b = bank[2 + n % 2]
                if n == 0:
                    wait(pe, "dv_kz", i * 2 + u + 1)
                    if u:
                        wait(pe, "dv_h", i * 2)
                    else:
                        wait(pe, "dv_vb", i)
                        wait(pe, "ac_vt", i)
                wait(pe, "dv_S", i * 16 + (8 * u + n - 1))
                if n < 6:
                    last = mm(b[:, 0:2 * S], qs[par][0:STK, n, u, 0:TXT], kz[u][0:STK, :, n, :], start=True, stop=True)
                else:
                    for r in range(4 * (n - 6), min(4 * (n - 6) + 4, PAIRS)):
                        c = 32 * (r % 4)
                        last = mm(b[c:c + IMG, 0:2 * S], qs[par][0:STK, r, u, TXT:S], kz[u][0:STK, :, r, :], start=True, stop=True)
                inc(last, "pe_S")

            def minus_max(i, u):
                wait(pe, "dv_S", i * 16 + (8 * u + 8))
                wait(pe, "ac_exp", i * 14 + 7 * u)
                for r in range(PAIRS):
                    o = bank[4 + r // 3][STK:AUG, (r % 3) * S:(r % 3) * S + S]
                    mm(o[:, 0:TXT], mmax[u][:, 2 * r:2 * r + 2], negid16[:], start=True, stop=True)
                    c = 32 * (r % 4)
                    last = mm(o[:, TXT:S], mrem[u][:, r // 4, :], negid16[:, c:c + IMG], start=True, stop=True)
                inc(last, "pe_A")

            def values(i):
                wait(pe, "dv_S", i * 16 + 16)
                wait(pe, "po_xrep", i + 1)
                for image in range(2):
                    for u in range(2):
                        for n, (t, k) in enumerate(((0, 0), (0, 1), (1, 0), (2, 2), (2, 3))):
                            x = xrep[u][:, t, :] if image else xt[:, t, bass.ds((i * 2 + u) * S, TXT)]
                            last = mm(bank[2 + image][:, D * u:D * u + D], x, wv[:, k, :], start=n == 0, stop=n == 4)
                    inc(last, "pe_V")

            def scores_t(i, par, u, n):
                b = bank[4 + (n + u) % 2]
                if n == 0:
                    wait(pe, "dv_qz", i * 2 + u + 1)
                    wait(pe, "ac_aux", i * 2 + u + 1)
                wait(pe, "ac_exp", i * 14 + (7 * u + n - 1))
                if n < 6:
                    last = mm(b[:, 0:2 * S], ks[par][:, n, u, 0:TXT], qz[u][:, :, n, :], start=True, stop=True)
                else:
                    for r in range(PAIRS):
                        c = 32 * (r % 4)
                        last = mm(b[c:c + 32, S * (r // 4):S * (r // 4) + S], kzi[u][:, r, :, :], qs[par][:, r, u, :], start=True, stop=True)
                inc(last, "pe_ST")

            def weighted(i, u):
                wait(pe, "ac_exp", i * 14 + (7 * u + 7))
                wait(pe, "ac_vt", i + 1)
                wait(pe, "dv_vb", i + 1)
                wait(pe, "dv_n", i * 2 + u)
                for j in range(3):
                    k = P if j < 2 else 64
                    o = bank[6][:, S * j:S * j + S]
                    mm(o, vb[u][0:k, 4 * j:4 * j + 4, :], ptr[u][0:k, j // 2, :], start=True, stop=True)
                    for c in range(4):
                        last = mm(o[32 * c:32 * c + 32, :], vt[u][:, 4 * j + c, :], pt[u][:, 4 * j + c, :], start=False, stop=True,
                                  skip_group_check=True)
                inc(last, "pe_PV")

            def out_project(i, u, src):
                for j in range(3):
                    last = mm(bank[2 + u][:, 0:D], src(j), wp[:, j, :], start=j == 0, stop=j == 2)
                inc(last, "pe_OP")

            def post_t(i):
                wait(pe, "dv_hl", i + 1)
                wait(pe, "dv_pos", i)
                for u in range(2):
                    o = bank[7][:].bitcast(F16)[:, 3 * P * u:3 * P * u + 3 * P]
                    r = rowb[:, u, 0, 0:D].bitcast(F16)
                    nc.tensor.transpose(o[:, 0:P], r[:, 0:P], id16[:])
                    nc.tensor.transpose(o[:, P:2 * P], r[:, 2 * P:3 * P], id16[:])
                    last = nc.tensor.transpose(o[:, 2 * P:3 * P], r[:, P:2 * P], id16[:])
                inc(last, "pe_T")

            def post_router(i):
                wait(pe, "ac_x2", i + 1)
                for u in range(2):
                    for n, (t, k) in enumerate(((0, 0), (0, 1), (1, 0), (2, 2), (2, 3))):
                        last = mm(bank[7][:, 384 + 8 * u:392 + 8 * u], x2[:, u, t, :], rw[:, k, :], start=n == 0, stop=n == 4)
                inc(last, "pe_R")

            def post_rank(i):
                wait(pe, "dv_A", i + 1)
                for u in range(2):
                    o = bank[7][:, 400 + 8 * u:408 + 8 * u]
                    mm(o, up16[:], a16[:, u, :], start=True, stop=False)
                    if u:
                        mm(o, ones16[:], a16[:, 0, :], start=False, stop=False)
                    last = mm(o, ones16[:], acc16, start=False, stop=True)
                inc(last, "pe_K")

            pe.wait_ge(sm_["dv_xt"], 1)
            pe.wait_ge(sm_["ac_xt"], B + 1)
            pe.wait_ge(sm_["po_wqk"], 1)
            project(0, range(12))
            for j in range(3):
                last = mm(bank[6][0:32, 0:D], bv[:, j, :], wp[:, j, :], start=j == 0, stop=j == 2)
            inc(last, "pe_bv")
            for n in range(8):
                scores(0, 0, 0, n)
            minus_max(0, 0)

            def step(pe, i, par):
                first, last_ = isinstance(i, int) and i == 0, isinstance(i, int) and i == STEPS - 1
                for n in range(8):
                    if n < 7:
                        scores_t(i, par, 0, n)
                    scores(i, par, 1, n)
                    if not last_:
                        project(i + 1, [n])
                minus_max(i, 1)
                if not last_:
                    project(i + 1, [8, 9])
                values(i)
                if not last_:
                    project(i + 1, [10, 11])
                if not first:
                    post_t(i - 1)
                weighted(i, 0)
                for n in range(8):
                    if n < 7:
                        scores_t(i, par, 1, n)
                    if not last_:
                        scores(i + 1, 1 - par, 0, n)
                    if n == 0 and not first:
                        post_router(i - 1)
                if not last_:
                    minus_max(i + 1, 0)
                wait(pe, "dv_n", i * 2 + 1)
                if not last_:
                    wait(pe, "dv_S", i * 16 + 24)
                else:
                    wait(pe, "ac_vt", i + 1)
                    wait(pe, "dv_vb", i + 1)
                if first:
                    wait(pe, "dv_wp", 1)
                out_project(i, 0, lambda j: ot[0][:, j, 0:TXT])
                weighted(i, 1)
                if not first:
                    post_rank(i - 1)
                wait(pe, "dv_n", i * 2 + 2)
                out_project(i, 1, lambda j: ot[1][:, j, 0:TXT])

            attention(step, pe)
            wait(pe, "dv_h", 2 * STEPS)
            for u in range(2):
                out_project(STEPS, u, lambda j: oti[:, j, u, :])
            for i in (STEPS - 1, STEPS):
                post_t(i)
                post_router(i)
                post_rank(i)
            wait(pe, "dv_pos", STEPS + 1)
            inc(mm(bank[7][0:1, 416:424], ones16[:, 0:1], acc16, start=True, stop=True), "pe_cnt")

            def experts_of(s, n):
                return nc.values_load_multi_w_load_instructions(itab[0:1, bass.ds(s + 72, n)], engines=[nc.tensor.engine],
                                                                min_val=0, max_val=E - 1)[1]

            def slot_t(s, p):
                pe.wait_ge(slot_ld[p], ((s - p) * 4 + 16))
                wait(pe, "dv_mT", s)
                o = bank[6][:].bitcast(F16)
                for h in range(2):
                    r = xr[p][:, h, 0:D].bitcast(F16)
                    for c, at in enumerate((0, 2 * P, P)):
                        last = nc.tensor.transpose(o[:, SR * c + P * h:SR * c + P * h + P], r[:, at:at + P], id16[:])
                inc(last, "pe_mT")

            def up(s, q, e):
                wait(pe, "dv_mT", s + 1)
                for f in range(FC):
                    if f % 2 == 0:
                        wait(pe, "ac_g", s * 3 + (f // 2 - 5))
                    o = bank[3 * q + f // 2][:, SR * (f % 2):SR * (f % 2) + SR]
                    for n, (k, t) in enumerate(((0, 0), (0, 1), (1, 0), (2, 2), (3, 2))):
                        w = w1s[:, bass.ds(e, 1), k, P * f:P * f + P].rearrange("p a f -> p (a f)")
                        last = mm(o, w, xe[q][:, t, :], start=n == 0, stop=n == 4)
                    if f % 2:
                        inc(last, "pe_up")

            def down(s, q, e):
                wait(pe, "dv_y", s)
                for h in range(2):
                    for f in range(FC):
                        if h == 0 and f % 2 == 0:
                            wait(pe, "dv_gl", s * 3 + (f // 2 + 1))
                        at = SR * f + P * h
                        for n, (g, k) in enumerate(((gh, 0), (gh, 1), (gl, 0))):
                            w = w2s[:, bass.ds(e, 1), k, D * f:D * f + D].rearrange("p a f -> p (a f)")
                            last = mm(bank[7][:, D * h:D * h + D], g[q][:, at:at + P], w,
                                      start=f == 0 and n == 0, stop=f == FC - 1 and n == 2)
                inc(last, "pe_L2")

            wait(pe, "dv_tab", 1)
            wait(pe, "po_split", 4 * E)
            slot_t(0, 0)
            es = experts_of(0, 5)
            for s in range(5):
                up(s, s % 2, es[s])
                slot_t(s + 1, (s + 1) % 4)
                if s:
                    down(s - 1, (s - 1) % 2, es[s - 1])
            with pe.Fori(0, (SLOTS - 5) // 4) as j:
                es = experts_of(j * 4 + 4, 5)
                for n in range(4):
                    s = j * 4 + (5 + n)
                    up(s, (5 + n) % 2, es[n + 1])
                    slot_t(s + 1, (6 + n) % 4)
                    down(j * 4 + (4 + n), n % 2, es[n])
            down(SLOTS - 1, (SLOTS - 1) % 2, experts_of(SLOTS - 1, 1)[0])

        @block.scalar
        def _(act):
            actf = nc.scalar.activation
            nc.scalar.preload_act_table(ACT.Exp)
            act.wait_ge(ld_c, 16)
            act.wait_ge(ld_tw, 16)

            def to_xt(i):
                for u in range(2):
                    wait(act, "pe_xt", 2 * i + u + 1)
                    src = bank[4 + 2 * (i % 2) + u][:].bitcast(F16)[:, 0:3 * P].rearrange("p (c t) -> p c t", c=3)
                    inc(actf(xt[:, :, (2 * i + u) * S:(2 * i + u) * S + TXT], src, ACT.Copy), "ac_xt")

            for c in range(1, CH, 2):
                wait(act, "pe_tt", c + 1)
                wait(act, "pe_tm", c - XG + 1)
                inc(actf(xg[:, c % XG, :], bank[1][0:CK, 0:256], ACT.Identity, bias=tokgb[:, 1, c:c + 1], scale=tokgb[:, 0, c:c + 1]), "ac_tg")
                if 0 <= c // 2 - XT_AT - 1 < B // 2:
                    to_xt(c // 2 - XT_AT - 1)
            act.wait_ge(ld_wp, 96)
            for k in range(2):
                last = actf(bqlo[:, PAIRS * k:PAIRS * k + PAIRS], bq[:, PAIRS * k:PAIRS * k + PAIRS], ACT.Copy,
                            scale=cst[0:STK, C_LOQ + k:C_LOQ + k + 1])
            inc(last, "ac_misc")
            wait(act, "ac_misc", 1)
            wait(act, "pe_xt", B + 2)
            for c in range(3):
                src = bank[5][:].bitcast(F16)[:, P * c:P * c + P].rearrange("p (b t) -> p b t", b=8)
                last = actf(xt[:, c, :].rearrange("p (b t) -> p b t", b=B)[:, 8:B, TXT:S], src, ACT.Copy)
            inc(last, "ac_xt")

            def low_half(i, chunks):
                for c in chunks:
                    wait(act, "pe_P", i * 12 + (c + 1))
                    wait(act, "dv_st", i * 12 + (c - 1))
                    inc(actf(hm[c % 2], bank[c % 2][0:STK, 0:2 * S], ACT.Identity, bias=bqlo[:, c:c + 1],
                             scale=cst[0:STK, C_LOQ + c // PAIRS:C_LOQ + c // PAIRS + 1]), "ac_hm")

            def aux(i, par, u):
                wait(act, "pe_A", i * 2 + u + 1)
                for k in range(2):
                    last = actf(qs[par][STK:AUG, 3 * k:3 * k + 3, u, :], bank[4 + k][STK:AUG, 0:3 * S].rearrange("p (r t) -> p r t", r=3), ACT.Copy)
                inc(last, "ac_aux")

            def exps(i, u, n):
                if n == 0:
                    wait(act, "pe_PV", i * 2 + (u - 1))
                b = bank[4 + (n + u) % 2]
                wait(act, "pe_ST", i * 14 + (7 * u + n + 1))
                if n < 6:
                    last = actf(pt[u][:, 2 * n:2 * n + 2, :], b[:, 0:2 * S].rearrange("p (h t) -> p h t", h=2), ACT.Exp, scale=DH ** -0.5)
                else:
                    actf(ptr[u][:, 0, :], b[:, 0:S], ACT.Exp, scale=DH ** -0.5)
                    last = actf(ptr[u][0:64, 1, :], b[0:64, S:2 * S], ACT.Exp, scale=DH ** -0.5)
                inc(last, "ac_exp")

            def value_rows(i):
                wait(act, "pe_V", i * 2 + 1)
                wait(act, "pe_PV", i * 2)
                inc(actf(vts[:, :, 0:DH], bank[2][:, 0:2 * D].rearrange("p (h d) -> p h d", h=2 * HEADS), ACT.Copy), "ac_vt")

            def post_x2(i):
                wait(act, "pe_T", i + 1)
                inc(actf(x2.rearrange("p u c t -> p (u c t)"), bank[7][:].bitcast(F16)[:, 0:6 * P], ACT.Copy), "ac_x2")

            def post_exp(i):
                wait(act, "dv_l", i + 1)
                inc(actf(pr, lg, ACT.Exp), "ac_sm")

            def split_high(e, n):
                slot_, size, dst, k, at = PARTS[n]
                wait(act, ld_stage[n], e * (32 if n == 1 else 16) + (32 if n == 1 else 16))
                hi = dst[:, bass.ds(e, 1), k, at:at + size].rearrange("p a f -> p (a f)")
                inc(actf(hi, stage[:, slot_, 0:size], ACT.Copy), "ac_split")

            low_half(0, range(12))
            aux(0, 0, 0)

            def step(act, i, par):
                first, last_ = isinstance(i, int) and i == 0, isinstance(i, int) and i == STEPS - 1
                for n in range(8):
                    if n < 7:
                        exps(i, 0, n)
                    if not last_:
                        low_half(i + 1, [n])
                aux(i, par, 1)
                if not last_:
                    low_half(i + 1, [8, 9])
                value_rows(i)
                if not last_:
                    low_half(i + 1, [10, 11])
                if not first:
                    post_x2(i - 1)
                for n in range(7):
                    exps(i, 1, n)
                    if n in (0, 2, 4):
                        split_high(i, n // 2)
                    if n == 5 and not first:
                        post_exp(i - 1)
                if not last_:
                    aux(i + 1, 1 - par, 0)
                split_high(i, 3)

            attention(step, act)
            for i in (STEPS - 1, STEPS):
                post_x2(i)
                post_exp(i)
            nc.scalar.preload_act_table(ACT.Gelu_apprx_tanh)

            def gelus(s, q):
                for b in range(3):
                    wait(act, "pe_up", s * 3 + (b + 1))
                    if b == 0:
                        wait(act, "pe_L2", s - 1)
                    wait(act, "dv_gl", s * 3 + (b - 2))
                    src = bank[3 * q + b][:, 0:2 * SR]
                    actf(gh[q][:, 2 * SR * b:2 * SR * b + 2 * SR], src, ACT.Gelu_apprx_tanh)
                    inc(actf(g32[b], src, ACT.Gelu_apprx_tanh), "ac_g")

            for s in range(5):
                gelus(s, s % 2)
            with act.Fori(0, (SLOTS - 5) // 4) as j:
                for n in range(4):
                    gelus(j * 4 + (5 + n), (5 + n) % 2)
            with act.Fori(0, 4) as j:
                for p in range(4):
                    wait(act, "dv_out", j * 4 + (p + 1))
                    act.dma_start(out.rearrange("b t d -> (b t) d")[bass.ds(j * 4 * S + (p * S + IMG), P), :], of[p]).then_inc(out_st, 16)
            for i in range(2):
                wait(act, "dv_out", 16 + i + 1)
                for b in range(8):
                    act.dma_start(out[8 * i + b, 0:IMG, :], of[i][16 * b:16 * b + 16, :]).then_inc(out_st, 16)
            act.wait_ge(out_st, 16 * (16 + 16))

        @block.vector
        def _(dve):
            v = nc.vector
            link = Link(dve, sm_["dv_link"])
            dve.wait_ge(ld_c, 16)
            v.tensor_copy(id16[:], ident)
            v.tensor_scalar(negid16[:], ident, -1.0, None, ALU.mult)
            v.tensor_copy(up16[:], cst[:, C_UP:C_UP + P])
            v.memset(bank[2][:], 0.0)
            v.memset(bank[3][:], 0.0)
            inc(v.memset(ones16[:], 1.0), "dv_pre")
            dve.wait_ge(ld_halo, 16)
            for t in range(2):
                for s in range(5):
                    dr, dc = SHIFTS[s]
                    view = patch[:, t, :].rearrange("p (r c) -> p r c", r=18)
                    for k in range(2):
                        last = v.bn_stats(bst[:, t, 2 * s + k, :], view[:, dr + 8 * k:dr + 8 * k + 8, 3 * dc:3 * dc + 48])
                link(last)
                link(v.bn_aggr(mv[:, t, :], bst[:, t, :, :].rearrange("p k s -> p (k s)")))
            inc(v.tensor_scalar(ve[:, 0:2], mv[:, 0:2, 1], EPS_TOK, None, ALU.add), "dv_var0")
            wait(dve, "po_rs0", 1)
            for t in range(2):
                inc(v.tensor_scalar(patch[:, t, :], patch[:, t, :], mv[:, t, 0:1], rs[:, t:t + 1], ALU.subtract, ALU.mult), "dv_patch")
            def tile_stats(t):
                return v.bn_stats(bst_tiles[:, t, :], h1[:, t, :])

            def tile_variances(tiles):
                for t in tiles:
                    last = v.bn_aggr(mv[:, t, :], bst_tiles[:, t, :])
                link(last)
                a, b = tiles[0], tiles[-1] + 1
                inc(v.tensor_scalar(ve[:, a:b], mv[:, a:b, 1], EPS_LN, None, ALU.add), "dv_var0")

            def norm(i):
                wait(dve, "po_rs0", 2 if i < B // 2 else 3)
                wait(dve, "dv_hl0", i)
                for u in range(2):
                    t = 2 * i + u
                    last = v.tensor_scalar(xn32[:, u, :], h1[:, t, :], mv[:, t, 0:1], rs[:, t:t + 1], ALU.subtract, ALU.mult)
                link(last)
                wait(dve, "pe_xt", 2 * (i - 1))
                r = hl[:, i % 2, :, :]
                link(v.tensor_copy(r[:, :, 0:D], xn32[:]))
                v.tensor_tensor(r[:, :, D:2 * P], xn32[:, :, P:D], r[:, :, P:D], ALU.subtract)
                inc(v.tensor_tensor(r[:, :, 2 * P:3 * P], xn32[:, :, 0:P], r[:, :, 0:P], ALU.subtract), "dv_hl0")

            dve.wait_ge(ld_tw, 16)
            for m in range(CH // 2):
                c = 2 * m
                wait(dve, "pe_tt", c + 1)
                wait(dve, "pe_tm", c - XG + 1)
                inc(v.tensor_scalar(xg[:, c % XG, :], bank[0][0:CK, 0:256], tokgb[:, 0, c:c + 1], tokgb[:, 1, c:c + 1], ALU.mult, ALU.add), "dv_tg")
                if 1 <= m < 5:
                    if m % 2:
                        dve.wait_ge(ld_txts[m // 2], 16)
                    for t in range(4 * (m - 1), 4 * m):
                        last = tile_stats(t)
                    if m == 4:
                        link(last)
                        tile_variances(range(B))
                if 0 <= m - XT_AT + 1 < B // 2:
                    norm(m - XT_AT + 1)
            dve.wait_ge(ld_row, 16)
            wait(dve, "pe_tm", CH)
            for t in range(2):
                last = v.tensor_tensor(h1[:, B + t, :], bank[2 + t][:, 0:D], rowv, ALU.add)
            link(last)
            for t in range(2):
                last = tile_stats(B + t)
            link(last)
            tile_variances(range(B, NT))
            norm(B // 2)
            wait(dve, "pe_xt", B + 1)
            for c in range(3):
                src = bank[4][:].bitcast(F16)[:, P * c:P * c + P].rearrange("p (b t) -> p b t", b=8)
                last = v.tensor_copy(xt[:, c, :].rearrange("p (b t) -> p b t", b=B)[:, 0:8, TXT:S], src)
            inc(last, "dv_xt")
            wait(dve, "po_const", 2)

            def norm_stats(tiles, n):
                for u in range(n):
                    last = v.bn_stats(bst[:, u, 0, :], tiles(u))
                link(last)
                v.memset(scrap[:], 0.0)
                for u in range(n):
                    last = v.bn_aggr(mv[:, u, :], bst[:, u, 0, :])
                link(last)
                return v.tensor_scalar(ve[:, 0:n], mv[:, 0:n, 1], EPS_LN, None, ALU.add)

            def stacks(i, par, chunks):
                for c in chunks:
                    wait(dve, "ac_hm", i * 12 + (c + 1))
                    dst = (qs, ks)[c // PAIRS][par][0:STK, c % PAIRS, :, :].rearrange("p u t -> p (u t)")
                    inc(v.scalar_tensor_tensor(dst, bank[c % 2][0:STK, 0:2 * S], bq[:, c:c + 1], hm[c % 2], ALU.add, ALU.subtract), "dv_st")

            def separate(which, i, par, u):
                src, dst, name = (ks, kz, "dv_kz") if which == "k" else (qs, qz, "dv_qz")
                if which == "q":
                    wait(dve, "ac_aux", i * 2 + u + 1)
                else:
                    wait(dve, "dv_st", i * 12 + 12)
                    wait(dve, "pe_ST", i * 14 + 7 * u - 7 if u else i * 14 - 7)
                for h in range(2):
                    last = v.tensor_scalar(dst[u][:, h, :, :], src[par][:, :, u, :], cst[0:AUG, C_Z + h:C_Z + h + 1], None, ALU.mult)
                if which == "k":
                    for h in range(2):
                        last = v.tensor_scalar(kzi[u][:, :, h, :], ks[par][:, :, u, TXT:S], cst[0:AUG, C_Z + h:C_Z + h + 1], None, ALU.mult)
                inc(last, name)

            def maxima(i, u, n):
                wait(dve, "pe_S", i * 16 + (8 * u + n + 1))
                if n == 0:
                    wait(dve, "pe_A", i * 2 + (u - 1))
                b = bank[2 + n % 2][:, 0:2 * S].rearrange("p (h t) -> p h t", h=2)
                if n < 6:
                    last = v.tensor_reduce(mmax[u][:, 2 * n:2 * n + 2], b, AX, ALU.max)
                elif n == 6:
                    last = v.tensor_reduce(mrem[u][:, 0, :], b, AX, ALU.max)
                else:
                    last = v.tensor_reduce(mrem[u][0:64, 1, :], b[0:64], AX, ALU.max)
                inc(last, "dv_S")

            def block_values(i):
                wait(dve, "pe_V", i * 2 + 2)
                wait(dve, "pe_PV", i * 2)
                m = cst[:, C_VM:C_VM + HEADS].rearrange("p (h o) -> p h o", o=1).broadcast_to([P, HEADS, DH])
                for u in range(2):
                    last = v.tensor_tensor(vb[u][:, :, 0:DH], bank[3][:, D * u:D * u + D].rearrange("p (h d) -> p h d", h=HEADS), m, ALU.mult)
                inc(last, "dv_vb")

            def normalise(i, u):
                wait(dve, "pe_PV", i * 2 + u + 1)
                link(v.transpose(rden, bank[6][:, 0:32 * NBLK]))
                link(v.reciprocal(rec, rden.rearrange("p (k b) -> p k b", b=32)[:, :, DH:DH + 1].rearrange("p k o -> p (k o)")))
                link(v.transpose(rden, rec.rearrange("p (k o) -> p k o", o=1).broadcast_to([P, NBLK, 32])))
                wait(dve, "pe_OP", i * 2 + (u - 1))
                inc(v.tensor_tensor(ot[u].rearrange("p j t -> p (j t)"), bank[6][:, 0:3 * S], rden[:, 0:3 * S], ALU.mult), "dv_n")
                wait(dve, "dv_n", i * 2 + u + 1)
                dst = oti.rearrange("p j i (b t) -> p j (i b) t", b=8)[:, :, bass.ds(i * 2 + u, 1), :].rearrange("p j b t -> p j (b t)")
                link(v.tensor_copy(dst, ot[u][:, :, TXT:S]))

            def residual(i, u):
                wait(dve, "pe_OP", i * 2 + u + 1)
                t = h1[:, bass.ds(i * 2 + u, 1), :].rearrange("p a d -> p (a d)")
                inc(v.tensor_tensor(t, bank[2 + u][:, 0:D], t, ALU.add), "dv_h")

            def post_stats(i):
                wait(dve, "dv_h", i * 2 + 2, alone=True)
                inc(norm_stats(lambda u: h1[:, bass.ds(i * 2 + u, 1), :].rearrange("p a d -> p (a d)"), 2), "dv_var")

            def post_rows(i):
                wait(dve, "po_rs", i + 1)
                for u in range(2):
                    t = h1[:, bass.ds(i * 2 + u, 1), :].rearrange("p a d -> p (a d)")
                    last = v.tensor_scalar(xn32[:, u, :], t, mv[:, u, 0:1], rs[:, u:u + 1], ALU.subtract, ALU.mult)
                link(last)
                dve.wait_ge(sm_["row_st"], i * 64) if not (isinstance(i, int) and i == 0) else None
                link(v.tensor_copy(rowb[:, :, 0, 0:D].bitcast(F16)[:, :, 0:D], xn32[:]))
                r = rowb[:, :, 0, 0:D].bitcast(F16)
                v.tensor_tensor(r[:, :, D:2 * P], xn32[:, :, P:D], r[:, :, P:D], ALU.subtract)
                inc(v.tensor_tensor(r[:, :, 2 * P:3 * P], xn32[:, :, 0:P], r[:, :, 0:P], ALU.subtract), "dv_hl")

            def const8(c, shape):
                ap = cst[:, c:c + E]
                return (ap.rearrange("p (o e) -> p o e", o=1) if len(shape) == 3 else ap.rearrange("p (o q e) -> p o q e", o=1, q=1)).broadcast_to(shape)

            def route(i, part, before):
                if part:
                    wait(dve, "dv_link", before)
                l = bank[7][:, 384:400].rearrange("p (u e) -> p u e", u=2)
                if part == 0:
                    wait(dve, "pe_R", i + 1)
                if part < 2:
                    v.memset(scrap[:], 0.0)
                if part == 0:
                    for u in range(2):
                        last = v.max(top[:, u, :], l[:, u, :])
                elif part == 1:
                    for u in range(2):
                        last = v.max_index(topi[:, u, :], top[:, u, :], l[:, u, :])
                elif part == 2:
                    inc(v.tensor_tensor(lg, top, top[:, :, 0:1].broadcast_to([P, 2, E]), ALU.subtract), "dv_l")
                    last = v.tensor_copy(topf, topi[:, :, 0:2])
                elif part == 3:
                    last = v.tensor_tensor(oh, const8(C_SLOT, [P, 2, 2, E]),
                                           topf.rearrange("p u (k o) -> p u k o", o=1).broadcast_to([P, 2, 2, E]), ALU.is_equal)
                elif part == 4:
                    last = v.tensor_tensor(a16, oh[:, :, 0, :], oh[:, :, 1, :], ALU.add)
                    inc(v.memset(scrap[:], 0.0), "dv_A")
                    wait(dve, "ac_sm", i + 1)
                elif part == 5:
                    last = v.tensor_reduce(den, pr, AX, ALU.add)
                elif part == 6:
                    last = v.reciprocal(den, den)
                else:
                    wait(dve, "po_row", i + 1)
                    last = v.tensor_tensor(rowb[:, :, :, ROW_GATE:ROW_GATE + 1].rearrange("p u k o -> p u (k o)"), pr[:, :, 0:2],
                                           den.rearrange("p (u o) -> p u o", o=1).broadcast_to([P, 2, 2]), ALU.mult)
                return link.put(last)

            def post_pos(i):
                wait(dve, "pe_K", i + 1)
                link(v.tensor_tensor(place, bank[7][:, 400:416].rearrange("p (u e) -> p u e", u=2), const8(C_ER, [P, 2, E]), ALU.add))
                v.tensor_tensor(acc16, acc16, a16[:, 0, :], ALU.add)
                link(v.tensor_tensor(hit, oh, place.rearrange("p u (o e) -> p u o e", o=1).broadcast_to([P, 2, 2, E]), ALU.mult))
                v.tensor_tensor(acc16, acc16, a16[:, 1, :], ALU.add)
                with nc.allow_low_precision(reason="one term of each sum is not zero, a whole number"):
                    inc(v.tensor_reduce(pos, hit, AX, ALU.add), "dv_pos")

            stacks(0, 0, range(12))
            separate("k", 0, 0, 0)
            separate("k", 0, 0, 1)

            for n in range(8):
                maxima(0, 0, n)
            separate("q", 0, 0, 0)
            wait(dve, "pe_bv", 1)
            inc(v.tensor_tensor(wp[0:32, 0, :], wp[0:32, 0, :], bank[6][0:32, 0:D], ALU.add), "dv_wp")
            wait(dve, "dv_wp", 1)
            v.memset(bank[6][:, 3 * S:32 * NBLK], 1.0)

            def step(dve, i, par):
                first, last_ = isinstance(i, int) and i == 0, isinstance(i, int) and i == STEPS - 1
                for n in range(8):
                    maxima(i, 1, n)
                    if not last_:
                        stacks(i + 1, 1 - par, [n])
                if not first:
                    post_rows(i - 1)
                separate("q", i, par, 1)
                if not last_:
                    stacks(i + 1, 1 - par, [8, 9])
                block_values(i)
                if not last_:
                    stacks(i + 1, 1 - par, [10, 11])
                    separate("k", i + 1, 1 - par, 0)
                at = None
                for n in range(8):
                    if not last_:
                        maxima(i + 1, 0, n)
                    if n == 0:
                        normalise(i, 0)
                    if not first:
                        at = route(i - 1, n, at)
                if not last_:
                    separate("k", i + 1, 1 - par, 1)
                    separate("q", i + 1, 1 - par, 0)
                residual(i, 0)
                if not first:
                    post_pos(i - 1)
                normalise(i, 1)
                residual(i, 1)
                post_stats(i)

            link.per = 44
            attention(step, dve, link)

            def post(i):
                at = None
                for part in range(8):
                    at = route(i, part, at)
                post_pos(i)

            post_rows(STEPS - 1)
            residual(STEPS, 0)
            residual(STEPS, 1)
            post(STEPS - 1)
            post_stats(STEPS)
            post_rows(STEPS)
            post(STEPS)
            wait(dve, "pe_cnt", 1)
            wait(dve, "dv_pos", STEPS + 1)
            cnt, til, cum, fl = ctab[0:1, 0:8], ctab[0:1, 8:16], ctab[0:1, 16:24], ctab[0:1, 24:32]
            link(v.tensor_copy(cnt, bank[7][0:1, 416:424]))
            link(v.tensor_scalar(fl, cnt, SR - 1.0, None, ALU.add))
            link(v.tensor_copy(itab[0:1, 64:72], fl))
            link(v.tensor_scalar(itab[0:1, 120:128], itab[0:1, 64:72], SR.bit_length() - 1, None, ALU.arith_shift_right))
            link(v.tensor_copy(til, itab[0:1, 120:128]))
            pairs8 = ctab[0:1, 32:96].rearrange("p (a b) -> p a b", a=E)
            link(v.tensor_tensor(pairs8, til.rearrange("p (o e) -> p o e", o=1).broadcast_to([1, E, E]),
                                 cst[0:1, C_TRI:C_TRI + E * E].rearrange("p (a b) -> p a b", a=E), ALU.mult))
            link(v.tensor_reduce(cum, pairs8, AX, ALU.add))
            NS = SLOTS + 1
            ge = ctab[0:1, 96:96 + NS * E].rearrange("p (s e) -> p s e", s=NS)
            st = ctab[0:1, 460:460 + NS]
            ex = ctab[0:1, 510:510 + NS]
            slots = cst[0:1, C_SLOT:C_SLOT + NS]
            link(v.tensor_tensor(ge, slots.rearrange("p (s o) -> p s o", o=1).broadcast_to([1, NS, E]),
                                 cum.rearrange("p (o e) -> p o e", o=1).broadcast_to([1, NS, E]), ALU.is_ge))
            link(v.tensor_reduce(ex, ge, AX, ALU.add))
            link(v.tensor_tensor(ge, ge, til.rearrange("p (o e) -> p o e", o=1).broadcast_to([1, NS, E]), ALU.mult))
            link(v.tensor_reduce(st, ge, AX, ALU.add))
            link(v.tensor_tensor(st, slots, st, ALU.subtract))
            link(v.tensor_scalar(st, st, float(SR), None, ALU.mult))
            link(v.scalar_tensor_tensor(st, ex, float(REGION), st, ALU.mult, ALU.add))
            v.tensor_scalar(itab[0:1, 0:NS], st, float(SPARE), None, ALU.min)
            v.tensor_scalar(itab[0:1, 72:72 + NS], ex, float(E - 1), None, ALU.min)
            inc(v.tensor_tensor(itab[0:1, 64:72], cnt, cst[0:1, C_ER:C_ER + E], ALU.add), "dv_tab")

            def low_g(s, q, b):
                wait(dve, "ac_g", s * 3 + (b + 1))
                at = slice(2 * SR * b, 2 * SR * b + 2 * SR)
                inc(v.tensor_tensor(gl[q][:, at], g32[b], gh[q][:, at], ALU.subtract), "dv_gl")

            def slot_x(s, q):
                wait(dve, "pe_mT", s + 1)
                wait(dve, "pe_up", s * 3 - 3)
                inc(v.tensor_copy(xe[q].rearrange("p c t -> p (c t)"), bank[6][:].bitcast(F16)[:, 0:3 * SR]), "dv_mT")

            def slot_y(s, p):
                wait(dve, "pe_L2", s + 1)
                if not isinstance(s, int) or s >= 4:
                    dve.wait_ge(y_st[p], (s - p) * 8)
                for h in range(2):
                    last = v.tensor_scalar(yb[p][:, h, :], bank[7][:, D * h:D * h + D], xr[p][:, h, ROW_GATE:ROW_GATE + 1], None, ALU.mult)
                inc(last, "dv_y")

            def slot_step(s, p):
                low_g(s, p % 2, 0)
                slot_x(s + 1, (p + 1) % 2)
                low_g(s, p % 2, 1)
                low_g(s, p % 2, 2)
                if not isinstance(s, int) or s:
                    slot_y(s - 1, (p - 1) % 4)

            slot_x(0, 0)
            for s in range(5):
                slot_step(s, s % 4)
            with dve.Fori(0, (SLOTS - 5) // 4) as j:
                for n in range(4):
                    slot_step(j * 4 + (5 + n), (5 + n) % 4)
            slot_y(SLOTS - 1, (SLOTS - 1) % 4)

            def finish(t, p, uses):
                dve.wait_ge(yk_ld[p], uses)
                res = h1[:, bass.ds(t, 1), :].rearrange("p a d -> p (a d)")
                link(v.tensor_tensor(yk[p][:, 0:D], yk[p][:, 0:D], yk[p][:, D:2 * D], ALU.add))
                inc(v.tensor_tensor(of[p], res, yk[p][:, 0:D], ALU.add), "dv_out")

            n0 = link.base + link.n
            with dve.Fori(0, 4) as j:
                link.base, link.n = j * 4 + n0, 0
                for p in range(4):
                    if p == 0:
                        dve.wait_ge(out_st, j * 64)
                    finish(j * 4 + p, p, j * 16 + 16)
            link.base, link.n = n0 + 16, 0
            dve.wait_ge(out_st, 16 * 16)
            for i in range(2):
                finish(16 + i, i, 4 * 16 + 8 * 16)

        @block.gpsimd
        def _(pool):
            g = nc.gpsimd
            link = Link(pool, sm_["po_link"])
            link(g.memset(nhalf[:], -0.5))

            def powers(a, b):
                return g.tensor_tensor(rs[:, a:b], ve[:, a:b], nhalf[:, 0:b - a], ALU.pow)

            wait(pool, "dv_var0", 1, alone=True)
            inc(powers(0, 2), "po_rs0")
            pool.wait_ge(ld_c, 16)
            for u in range(2):
                g.memset(vt[u][:, :, DH:32], 1.0)
                for k in range(DH):
                    g.tensor_copy(vb[u][:, :, DH + k:DH + k + 1].rearrange("p h o -> p (h o)"), cst[:, C_VM:C_VM + HEADS])
                g.memset(mrem[u], 0.0)
            g.memset(acc16, 0.0)
            link(g.memset(padrow, 0.0))
            link(g.memset(padrow[:, ROW_ID:ROW_ID + 1].bitcast(I32), 1 << 24))
            link(g.memset(ks[0][STK:AUG, :, :, :], 1.0))
            inc(g.memset(rowb.rearrange("p u k w -> p (u k w)"), 0.0), "po_const")

            pool.wait_ge(ld_wa, 48)
            pool.wait_ge(ld_wp, 96)
            for k in range(2):
                g.tensor_copy(wt16[:, 2 * k, :], wa32[:, k, 0:2 * D])
                g.tensor_copy(wv[:, 2 * k, :], wa32[:, k, 2 * D:3 * D])
                last = g.tensor_copy(rw[:, 2 * k, :], rw32[:, k, :])
            link(last)
            for k in range(2):
                g.tensor_tensor(wt16[:, 2 * k + 1, :], wa32[:, k, 0:2 * D], wt16[:, 2 * k, :], ALU.subtract)
                g.tensor_tensor(wv[:, 2 * k + 1, :], wa32[:, k, 2 * D:3 * D], wv[:, 2 * k, :], ALU.subtract)
                last = g.tensor_tensor(rw[:, 2 * k + 1, :], rw32[:, k, :], rw[:, 2 * k, :], ALU.subtract)
            link(last)
            wait(pool, "dv_var0", 2, alone=True)
            inc(powers(0, B), "po_rs0")
            for k in range(4):
                for s in range(3):
                    dst = wqk[:, k, :, :].rearrange("p r (h s d) -> p (r h) s d", h=2, s=3)[:, :, s, :]
                    last = g.tensor_copy(dst, wt16[:, k, :].rearrange("p (n d) -> p n d", d=DH))
            inc(last, "po_wqk")
            wait(pool, "dv_var0", 3, alone=True)
            inc(powers(B, NT), "po_rs0")
            wait(pool, "po_rs0", 3, alone=True)
            wait(pool, "pe_tm", CH, alone=True)
            inc(g.memset(ks[1][STK:AUG, :, :, :], 1.0), "po_const")
            wait(pool, "po_const", 2, alone=True)
            wait(pool, "dv_xt", 1, alone=True)
            wait(pool, "ac_xt", B + 1, alone=True)

            def image_rows(i):
                wait(pool, "pe_V", i * 2, alone=True)
                for u in range(2):
                    for c in range(3):
                        src = xt[:, c:c + 1, bass.ds((i * 2 + u) * S + TXT, IMG)].broadcast_to([P, 8, IMG])
                        last = g.tensor_copy(xrep[u][:, c, :].rearrange("p (b t) -> p b t", b=8), src)
                inc(last, "po_xrep")

            def rows_twice(i):
                wait(pool, "dv_hl", i + 1, alone=True)
                for k in range(2):
                    src = cst[:, C_TID:C_TID + 2 * NT].rearrange("p (t k) -> p t k", k=2)[:, bass.ds(i * 2, 2), k:k + 1]
                    g.tensor_copy(rowb[:, :, k, ROW_ID:ROW_ID + 1].bitcast(I32), src)
                inc(g.tensor_copy(rowb[:, :, 1, 0:D], rowb[:, :, 0, 0:D]), "po_row")

            def scatter(i):
                wait(pool, "dv_pos", i + 1, alone=True)
                for u in range(2):
                    for k in range(2):
                        g.indirect_dma_start(routed[:, :], bass.IndirectOffsetOnAxis(ap=pos[:, u, k:k + 1], axis=0),
                                             rowb[:, u, k, :], None).then_inc(sm_["row_st"], 16)

            def split_low(e, n):
                slot_, size, dst, k, at = PARTS[n]
                wait(pool, "ac_split", e * 4 + (n + 1), alone=True)
                hi = dst[:, bass.ds(e, 1), k, at:at + size].rearrange("p a f -> p (a f)")
                lo = dst[:, bass.ds(e, 1), k + 1, at:at + size].rearrange("p a f -> p (a f)")
                inc(g.tensor_tensor(lo, stage[:, slot_, 0:size], hi, ALU.subtract), "po_split")

            def step(pool, i, par):
                first = isinstance(i, int) and i == 0
                image_rows(i)
                if not first:
                    rows_twice(i - 1)
                for n in range(3):
                    split_low(i, n)
                if not first:
                    scatter(i - 1)
                split_low(i, 3)
                wait(pool, "dv_var", i + 1, alone=True)
                inc(powers(0, 2), "po_rs")

            attention(step, pool)
            rows_twice(STEPS - 1)
            scatter(STEPS - 1)
            wait(pool, "dv_var", STEPS + 1, alone=True)
            inc(powers(0, 2), "po_rs")
            rows_twice(STEPS)
            scatter(STEPS)

            bound = g.to_reg(N * TOPK - 1)

            def put(s, p):
                wait(pool, "dv_y", s + 1 if isinstance(s, int) else g.to_reg(s + 1), alone=True)
                for h in range(2):
                    g.indirect_dma_start(expert_out[:, :], bass.IndirectOffsetOnAxis(ap=xr[p][:, h, ROW_ID:ROW_ID + 1].bitcast(U32), axis=0),
                                         yb[p][:, h, :], None, bounds_check=bound, oob_is_err=False).then_inc(y_st[p], 16)

            for s in range(5):
                put(s, s % 4)
            with pool.Fori(0, (SLOTS - 5) // 4) as j:
                for n in range(4):
                    put(j * 4 + (5 + n), (5 + n) % 4)


def constants():
    import numpy as np
    c = np.zeros((P, NCONST), np.float32)
    r = np.arange(P)
    c[:, C_ID:C_ID + P] = np.eye(P)
    c[:, C_UP:C_UP + P] = r[:, None] < r[None, :]
    part = (r[:STK] // DH) % 3
    c[:STK, C_LOQ] = part == 2
    c[:STK, C_LOK] = part == 1
    for h in range(2):
        c[48 * h:48 * h + 48, C_Z + h] = 1
        c[STK + h, C_Z + h] = 1
    head = np.arange(HEADS)
    c[:, C_VM:C_VM + HEADS] = (r[:, None] // IMG) == (head[None, :] % 8)
    c[:, C_DESC:C_DESC + E] = E - np.arange(E)
    c[:, C_ER:C_ER + E] = np.arange(E) * REGION
    for t in range(NT):
        token = t * S + IMG + r if t < B else ((t - B) * 8 + r // IMG) * S + r % IMG
        for k in range(2):
            c[:, C_TID + 2 * t + k] = 2 * token + k
    c[:, C_SLOT:C_SLOT + SLOTS + 1] = np.arange(SLOTS + 1)
    c[:, C_TRI:] = np.tril(np.ones((E, E))).ravel()
    return c


def kernel(x, txt, L0_tok_gamma, L0_tok_beta, L0_tok_W, L0_tok_b, L0_attn_w_attn, L0_attn_b_attn, L0_attn_w_proj,
           L0_attn_b_proj, L0_ffn_router_w, L0_ffn_w1, L0_ffn_w2):
    import numpy as np
    import concourse.bacc as bacc
    from concourse.bass_utils import run_bass_kernel_spmd

    x = np.asarray(x)
    xp = np.pad(x, ((0, 0), (1, 1), (1, 1), (0, 0)))
    halo = np.stack([xp[:, 16 * a:16 * a + 18, 16 * b:16 * b + 18, :] for a in range(4) for b in range(4)], 1)

    def by_shift(a):
        a = np.asarray(a).reshape(8, 2, 16, 5, 3, -1)
        a = a.transpose(1, 2, 4, 3, 0, 5).reshape(2, 48, CH, -1)
        return np.pad(a, ((0, 0), (0, 6), (0, 0), (0, 0))).reshape(108, CH, -1)[:CK]

    ba = np.asarray(L0_attn_b_attn)
    bqk = np.tile(ba[:2 * D].reshape(2 * PAIRS, 2, 1, DH), (1, 1, 3, 1)).reshape(2 * PAIRS, STK).T
    wp = np.zeros((4, 32, 3, D), np.float32)
    wp[:, :DH] = np.asarray(L0_attn_w_proj).reshape(3, 4, DH, D).transpose(1, 2, 0, 3)
    wp[0, DH, 0] = np.asarray(L0_attn_b_proj)
    bv = np.zeros((4, 32, 3, 32), np.float32)
    bv[:, :DH, :, DH] = ba[2 * D:].reshape(3, 4, DH).transpose(1, 2, 0)
    arrays = {
        "a_halo": halo.reshape(B * IMG, HALO),
        "a_txt": np.asarray(txt),
        "a_tok_w": by_shift(L0_tok_W),
        "a_tok_gb": np.stack([by_shift(L0_tok_gamma)[..., 0], by_shift(L0_tok_beta)[..., 0]], 1),
        "a_rows": np.asarray(L0_tok_b)[None],
        "a_bv": bv.reshape(P, 3, 32),
        "a_bqk": bqk,
        "a_w_attn": np.asarray(L0_attn_w_attn),
        "a_w_proj": wp.reshape(P, 3, D),
        "a_router": np.asarray(L0_ffn_router_w).T,
        "a_w1": np.asarray(L0_ffn_w1),
        "a_w2": np.asarray(L0_ffn_w2),
        "a_consts": constants(),
    }
    arrays = {k: np.ascontiguousarray(a) for k, a in arrays.items()}
    nc = bacc.Bacc("TRN2", target_bir_lowering=False, num_devices=1)
    args = [nc.dram_tensor(k, a.shape, mybir.dt.from_np(a.dtype), kind="ExternalInput").ap() for k, a in arrays.items()]
    out = nc.dram_tensor("out", (B, S, D), F32, kind="ExternalOutput").ap()
    build_program(nc, *args, out)
    r = run_bass_kernel_spmd(nc, [arrays], core_ids=[0])
    return r.results[0]["out"]
```

```python
from contextlib import ExitStack

import concourse.bass as bass
from concourse import mybir

F32 = mybir.dt.float32
F16 = mybir.dt.float16
I32 = mybir.dt.int32
U32 = mybir.dt.uint32
ALU = mybir.AluOpType
ACT = mybir.ActivationFunctionType
AX = mybir.AxisListType.X

P = 128
B, TXT, IMG, D = 16, 128, 16, 192
S = TXT + IMG
N = B * S
HEADS, DH = 12, 16
PAIRS = HEADS // 2
STK = 2 * 3 * DH
AUG = STK + 2
E, DFF, TOPK = 8, 768, 2
FC = DFF // P
NT = N // P
SR = 2 * P
REGION = N + SR
SPARE = E * REGION
UNITS = (N * TOPK - E) // P + E
SMALL = E // 2
LARGE = max(UNITS // 2, (UNITS - E) // 2 + E - SMALL)
SLOTS = LARGE + SMALL
ROW = 196
ROW_ID, ROW_GATE = 192, 193
HALO = 18 * 18 * 3
TG = 10
CH, CK = 40, 54 + 48
EPS_TOK, EPS_LN = 1e-3, 1e-5
AREA = 17250
STEPS = B // 2
NBLK = -(-3 * S // 32)
XT_AT = 7
SHIFTS = ((1, 1), (1, 0), (1, 2), (0, 1), (2, 1))

C_ID, C_UP = 0, 128
C_LOQ, C_LOK = 256, 257
C_Z = 258
C_VM = 260
C_DESC = 272
C_ER = 280
C_TID = 288
C_SLOT = C_TID + 2 * NT
C_TRI = C_SLOT + SLOTS + 1
NCONST = C_TRI + E * E


def build_program(nc, halo, txt, tok_w, tok_gb, rows, bvt, bqk, w_attn, w_proj, router, w1, w2, consts, out):
    with ExitStack() as ctx:
        def sb(name, shape, dt):
            return ctx.enter_context(nc.sbuf_tensor(name, shape, dt))

        def sem(name):
            return ctx.enter_context(nc.semaphore(name))

        bank = [ctx.enter_context(nc.psum_tensor(f"bank{i}", [P, 512], F32)) for i in range(8)]
        routed = nc.dram_tensor("routed_rows", [SPARE + SR, ROW], F32, kind="Internal")
        expert_out = nc.dram_tensor("expert_out", [N * TOPK, D], F32, kind="Internal")

        cst = sb("cst", [P, NCONST], F32)
        ident = cst[:, C_ID:C_ID + P]
        id16 = sb("id16", [P, P], F16)
        negid16 = sb("negid16", [P, P], F16)
        up16 = sb("up16", [P, P], F16)
        ones16 = sb("ones16", [P, P], F16)
        scrap = sb("scrap", [1, 1], F32)
        nhalf = sb("nhalf", [P, B], F32)
        
        bq = sb("bq", [STK, 2 * PAIRS], F32)
        bqlo = sb("bqlo", [STK, 2 * PAIRS], F32)
        wqk = sb("wqk", [P, 4, 2 * PAIRS, STK], F16)
        wv = sb("wv", [P, 4, D], F16)
        wp = sb("wp", [P, 3, D], F32)
        rw32 = sb("rw32", [P, 2, E], F32)
        rw = sb("rw", [P, 4, E], F16)
        w1s = sb("w1s", [P, E, 4, DFF], F16)
        w2s = sb("w2s", [P, E, 2, FC * D], F16)
        h1 = sb("h1", [P, NT, D], F32)
        xt = sb("xt", [P, 3, N], F16)
        stage = sb("stage", [P, 3, 4 * D], F32)
        mv = sb("mv", [P, NT, 2], F32)
        ve = sb("ve", [P, NT], F32)
        rs = sb("rs", [P, NT], F32)
        bst = sb("bst", [P, 2, 10, 6], F32)
        bst_tiles = bst[:].rearrange("p u k s -> p (u k) s")
        xn32 = sb("xn32", [P, 2, D], F32)
        area = sb("area", [P, AREA], F32)

        def cut(cols, at):
            return area[:, at[0] - cols:at[0]]

        def region(cursor, cols):
            cursor[0] += cols
            assert cursor[0] <= AREA, cursor
            return area[:, cursor[0] - cols:cursor[0]]

        ta = [0]
        patch = region(ta, 2 * HALO).rearrange("p (t f) -> p t f", t=2)
        tokw = region(ta, CH * D)[0:CK, :].rearrange("p (c d) -> p c d", c=CH)
        tokgb = region(ta, 2 * CH)[0:CK, :].rearrange("p (g c) -> p g c", g=2)
        XG = 4
        rowv = region(ta, D)
        xg = region(ta, XG * 256)[0:CK, :].rearrange("p (x t) -> p x t", x=XG)
        hl = region(ta, 4 * D).bitcast(F16).rearrange("p (v u f) -> p v u f", v=2, u=2)
        wa32 = region(ta, 2 * 3 * D).rearrange("p (k f) -> p k f", k=2)
        wt16 = region(ta, 4 * 2 * D // 2).bitcast(F16).rearrange("p (k f) -> p k f", k=4)

        SW = PAIRS * 2 * S

        def stack(cursor):
            return region(cursor, SW // 2)[0:AUG, :].bitcast(F16).rearrange("p (r u t) -> p r u t", r=PAIRS, u=2)

        cc = [ta[0]]
        vts = region(cc, 2 * HEADS * 32).rearrange("p (h d) -> p h d", h=2 * HEADS)
        vt = [vts[:, HEADS * u:HEADS * u + HEADS, :] for u in range(2)]
        vb = [region(cc, HEADS * 32).rearrange("p (h d) -> p h d", h=HEADS) for _ in range(2)]
        mrem = [region(cc, 2).bitcast(F16).rearrange("p (s h) -> p s h", s=2) for _ in range(2)]
        rowb = region(cc, 4 * ROW).rearrange("p (u k w) -> p u k w", u=2, k=2)
        acc16 = region(cc, 4).bitcast(F16)
        padrow = region(cc, ROW)
        ks = [stack(cc)]
        bv = region(cc, 3 * 32).rearrange("p (j c) -> p j c", j=3)
        top = region(cc, 16).rearrange("p (u e) -> p u e", u=2)
        topi = region(cc, 16).bitcast(U32).rearrange("p (u e) -> p u e", u=2)
        topf = region(cc, 4).rearrange("p (u k) -> p u k", u=2)
        lg = region(cc, 16).rearrange("p (u e) -> p u e", u=2)
        pr = region(cc, 16).rearrange("p (u e) -> p u e", u=2)
        oh = region(cc, 32).rearrange("p (u k e) -> p u k e", u=2, k=2)
        place = region(cc, 16).rearrange("p (u e) -> p u e", u=2)
        hit = region(cc, 32).rearrange("p (u k e) -> p u k e", u=2, k=2)
        den = region(cc, 2)
        aa = [0]
        ks.append(stack(aa))
        qs = [stack(aa) for _ in range(2)]
        qz = [region(aa, SW // 2)[0:AUG, :].bitcast(F16).rearrange("p (h r t) -> p h r t", h=2, r=PAIRS) for _ in range(2)]
        kz = [region(aa, SW // 2)[0:AUG, :].bitcast(F16).rearrange("p (h r t) -> p h r t", h=2, r=PAIRS) for _ in range(2)]
        hm = [region(aa, S)[0:STK, :].bitcast(F16) for _ in range(2)]
        pt = [region(aa, HEADS * S).rearrange("p (h t) -> p h t", h=HEADS) for _ in range(2)]
        ptr = [region(aa, 2 * S).rearrange("p (s t) -> p s t", s=2) for _ in range(2)]
        xrep = [region(aa, 3 * P // 2).bitcast(F16).rearrange("p (c t) -> p c t", c=3) for _ in range(2)]
        kzi = [region(aa, PAIRS * 16)[0:AUG, :].bitcast(F16).rearrange("p (r h t) -> p r h t", r=PAIRS, h=2) for _ in range(2)]
        mmax = [region(aa, 6).bitcast(F16) for _ in range(2)]
        rden = region(aa, NBLK * 32)
        rec = region(aa, NBLK)
        ot = [region(aa, 3 * S).rearrange("p (j t) -> p j t", j=3) for _ in range(2)]
        oti = region(aa, 3 * 2 * P).rearrange("p (j i t) -> p j i t", j=3, i=2)
        x2 = region(aa, 2 * 3 * P // 2).bitcast(F16).rearrange("p (u c t) -> p u c t", u=2, c=3)
        a16 = region(aa, 8).bitcast(F16).rearrange("p (u e) -> p u e", u=2)
        pos = region(aa, 4).bitcast(U32).rearrange("p (u k) -> p u k", u=2)
        assert aa[0] <= ta[0], (aa, ta)
        rowb_last = pt[1].rearrange("p h t -> p (h t)")[:, 0:4 * ROW].rearrange("p (u k w) -> p u k w", u=2, k=2)
        pos_last = pt[1].rearrange("p h t -> p (h t)")[:, 4 * ROW:4 * ROW + 4].bitcast(U32).rearrange("p (u k) -> p u k", u=2)
        ctab = pt[0].rearrange("p h t -> p (h t)")

        ea = [0]
        xr = [region(ea, 2 * ROW).rearrange("p (h w) -> p h w", h=2) for _ in range(4)]
        xe = [region(ea, 3 * SR // 2).bitcast(F16).rearrange("p (c t) -> p c t", c=3) for _ in range(2)]
        g32 = [region(ea, 2 * SR) for _ in range(3)]
        gh = [region(ea, FC * SR // 2).bitcast(F16) for _ in range(2)]
        gl = [region(ea, FC * SR // 2).bitcast(F16) for _ in range(2)]
        yb = [region(ea, 2 * D).rearrange("p (h d) -> p h d", h=2) for _ in range(4)]
        fa = [0]
        yk = [region(fa, 4 * D).rearrange("p (t k d) -> p t k d", t=2, k=2) for _ in range(NT // 2)]
        of = [region(fa, 2 * D).rearrange("p (t d) -> p t d", t=2) for _ in range(NT // 2)]
        itab = sb("itab", [1, 128], I32)

        (ld_c, ld_halo, ld_tw, ld_row, ld_wa, ld_wp, pads_in, out_st) = [sem(n) for n in (
            "ld_c", "ld_halo", "ld_tw", "ld_row", "ld_wa", "ld_wp", "pads_in", "out_st")]
        slot_ld = [sem(f"slot_ld{i}") for i in range(4)]
        y_st = [sem(f"y_st{i}") for i in range(4)]
        yk_ld = [sem(f"yk_ld{i}") for i in range(NT // 2)]
        ld_txts = [sem(f"ld_txt{i}") for i in range(2)]
        ld_tws = [sem(f"ld_tw{i}") for i in range(4)]
        ld_stage = [sem(f"ld_stage{i}") for i in range(4)]
        (pe_tt, pe_tm, pe_xt, pe_P, pe_S, pe_A, pe_V, pe_ST, pe_PV, pe_OP, pe_T, pe_R, pe_K, pe_cnt, pe_mT, pe_up,
         pe_L2, ac_tg, ac_hm, ac_aux, ac_exp, ac_sm, ac_g, ac_misc, ac_xt, ac_vt, ac_x2, ac_split, dv_vb, dv_wp,
         pe_bv, dv_pre, dv_var0, dv_patch, dv_tg, dv_hl0, dv_xt, dv_st, dv_kz, dv_qz, dv_S, dv_n, dv_h, dv_var, dv_hl,
         dv_l, dv_A, dv_pos, dv_tab, dv_mT, dv_gl, dv_y, dv_out, dv_link, po_xrep, po_rs0, po_rs, po_row, po_split,
         po_link, po_const, po_zero, po_wqk, row_st) = [sem(n) for n in (
            "pe_tt pe_tm pe_xt pe_P pe_S pe_A pe_V pe_ST pe_PV pe_OP pe_T pe_R pe_K pe_cnt pe_mT pe_up pe_L2 ac_tg "
            "ac_hm ac_aux ac_exp ac_sm ac_g ac_misc ac_xt ac_vt ac_x2 ac_split dv_vb dv_wp pe_bv dv_pre dv_var0 "
            "dv_patch dv_tg dv_hl0 dv_xt dv_st dv_kz dv_qz dv_S dv_n dv_h dv_var dv_hl dv_l dv_A dv_pos dv_tab dv_mT "
            "dv_gl dv_y dv_out dv_link po_xrep po_rs0 po_rs po_row po_split po_link po_const po_zero po_wqk row_st").split()]

        class Link:

            def __init__(self, eng, semaphore):
                self.eng, self.sem, self.base, self.n = eng, semaphore, 0, 0

            def put(self, ins):
                self.n += 1
                ins.then_inc(self.sem, 1)
                return self.base + self.n

            def __call__(self, ins):
                self.eng.wait_ge(self.sem, self.put(ins))

        def chunks_of(buffer, b, rows):
            both = buffer[:, 2 * SR * b:2 * SR * b + 2 * SR]
            return both if rows == SR else both.rearrange("p (f t) -> p f t", f=2)[:, :, 0:rows]

        def counted(value):
            return not isinstance(value, int) or value > 0

        def wait_alone(eng, semaphore, value):
            eng.wait_ge(ld_c, 16)
            eng.wait_ge(semaphore, value)

        def halo_rows(t, shift, rb):
            dr, dc = SHIFTS[shift]
            at = (2 * rb + dr) * 54 + 3 * dc
            return patch[:, t, at:at + CK]

        twice = padrow.rearrange("p (o w) -> p o w", o=1).broadcast_to([P, 2, ROW])

        def stack_of(c):
            return (c + PAIRS) % (2 * PAIRS)

        def attention(step, eng, tally=None):
            step(eng, 0, 0)
            if tally:
                first = tally.base + tally.n
            with eng.Fori(0, (STEPS - 2) // 2) as j:
                if tally:
                    per = tally.per
                    tally.base, tally.n = j * per + first, 0
                step(eng, j * 2 + 1, 1)
                step(eng, j * 2 + 2, 0)
                if tally:
                    assert tally.n == per, (tally.n, per)
            if tally:
                tally.base, tally.n = first + per * ((STEPS - 2) // 2), 0
            step(eng, STEPS - 1, 1)

        PARTS = ((0, DFF, w1s, 0, 0), (1, DFF, w1s, 2, 0), (2, 4 * D, w2s, 0, 0), (0, 2 * D, w2s, 0, 4 * D))

        block = ctx.enter_context(nc.Block())

        @block.sync
        def _(sp):
            sp.dma_start(patch, halo.rearrange("(t p) f -> p t f", t=2)).then_inc(ld_halo, 16)
            sp.dma_start(cst[:], consts).then_inc(ld_c, 16)
            sp.dma_start(tokgb, tok_gb).then_inc(ld_tw, 16)

            def token_weights(g):
                sp.dma_start(tokw[:, TG * g:TG * g + TG, :], tok_w[:, TG * g:TG * g + TG, :]).then_inc(ld_tws[g], 16)

            token_weights(0)
            for u in range(2):
                sp.dma_start(h1[:, 8 * u:8 * u + 8, :], txt[8 * u:8 * u + 8].rearrange("b p d -> p b d")).then_inc(ld_txts[u], 16)
            token_weights(1)
            sp.dma_start(wa32[:, 0, :], w_attn[0:P, :]).then_inc(ld_wa, 16)
            sp.dma_start(wa32[0:64, 1, :], w_attn[P:D, :]).then_inc(ld_wa, 16)
            sp.dma_start(wa32[64:P, 1, :], w_attn[P:D, :]).then_inc(ld_wa, 16)
            token_weights(2)
            token_weights(3)
            sp.dma_start(rowv, rows.broadcast_to([P, D])).then_inc(ld_row, 16)
            sp.dma_start(bv, bvt).then_inc(ld_wp, 16)
            sp.dma_start(bq[:], bqk).then_inc(ld_wp, 16)
            sp.dma_start(wp[:], w_proj).then_inc(ld_wp, 16)
            sp.dma_start(rw32[:, 0, :], router[0:P, :]).then_inc(ld_wp, 16)
            sp.dma_start(rw32[0:64, 1, :], router[P:D, :]).then_inc(ld_wp, 16)
            sp.dma_start(rw32[64:P, 1, :], router[P:D, :]).then_inc(ld_wp, 16)
            with sp.Fori(0, E) as e:
                sp.wait_ge(po_wqk, 1)
                wait_alone(sp, po_split, e * 4)
                s = stage
                v = w1.rearrange("e d f -> (e d) f")
                sp.dma_start(s[:, 0, :], v[bass.ds(e * D, P), :]).then_inc(ld_stage[0], 16)
                sp.dma_start(s[0:64, 1, :], v[bass.ds(e * D + P, 64), :]).then_inc(ld_stage[1], 16)
                sp.dma_start(s[64:P, 1, :], v[bass.ds(e * D + P, 64), :]).then_inc(ld_stage[1], 16)
                v = w2.rearrange("e f d -> (e f) d")
                sp.dma_start(s[:, 2, :].rearrange("p (c d) -> p c d", c=4),
                             v[bass.ds(e * DFF, 4 * P), :].rearrange("(c p) d -> p c d", c=4)).then_inc(ld_stage[2], 16)
                wait_alone(sp, po_split, e * 4 + 1)
                sp.dma_start(s[:, 0, 0:2 * D].rearrange("p (c d) -> p c d", c=2),
                             v[bass.ds(e * DFF + 4 * P, 2 * P), :].rearrange("(c p) d -> p c d", c=2)).then_inc(ld_stage[3], 16)
            sp.wait_ge(po_const, 2)
            sp.dma_start(routed[SPARE:SPARE + SR, :].rearrange("(p h) w -> p h w", h=2), twice).then_inc(pads_in, 16)

            def table(at, n, top):
                return nc.values_load_multi_w_load_instructions(itab[0:1, at:at + n], engines=[nc.sync.engine], min_val=0, max_val=top)[1]

            sp.wait_ge(dv_tab, 1)
            for r in table(64, E // 2, SPARE - SR):
                sp.dma_start(routed[bass.ds(r, SR), :].rearrange("(p h) w -> p h w", h=2), twice).then_inc(pads_in, 16)
            sp.wait_ge(dv_tab, 2)
            first_slots = table(0, 5, SPARE)
            sp.wait_ge(pads_in, 16 * (E + 1))
            sp.wait_ge(row_st, 16 * 4 * (STEPS + 1))

            def slot(s, p, r):
                if not isinstance(s, int) or s >= 4:
                    sp.wait_ge(y_st[p], (s - p) * 8)
                if isinstance(s, int) and s >= LARGE:
                    sp.dma_start(xr[p][:, 0, :], routed[bass.ds(r, P), :]).then_inc(slot_ld[p], 16)
                else:
                    sp.dma_start(xr[p], routed[bass.ds(r, SR), :].rearrange("(p h) w -> p h w", h=2)).then_inc(slot_ld[p], 16)

            for s, r in enumerate(first_slots):
                slot(s, s % 4, r)
            with sp.Fori(0, (LARGE - 5) // 4) as j:
                for n in range(4):
                    s = j * 4 + (5 + n)
                    slot(s, (5 + n) % 4, nc.sync.value_load(itab[0:1, bass.ds(s, 1)], min_val=0, max_val=SPARE))
            sp.wait_ge(dv_tab, 3)
            for n, r in enumerate(table(LARGE, SMALL, SPARE)):
                slot(LARGE + n, (LARGE + n) % 4, r)
            for p in range(4):
                sp.wait_ge(y_st[p], sum(32 if s < LARGE else 16 for s in range(p, SLOTS, 4)))
            ykv = expert_out.rearrange("(b t k) d -> b t (k d)", b=B, k=2)
            for u in range(2):
                sp.dma_start(yk[0][:, u, :, :].rearrange("p k d -> p (k d)"), ykv[8 * u:8 * u + 8, 0:IMG, :]).then_inc(yk_ld[0], 16)
            for i in range(B // 2):
                sp.dma_start(yk[1 + i].rearrange("p t k d -> p t (k d)"), ykv[2 * i:2 * i + 2, IMG:S, :].rearrange("b t w -> t b w")).then_inc(yk_ld[1 + i], 16)

        @block.tensor
        def _(pe):
            mm = nc.tensor.matmul
            pe.wait_ge(ld_c, 16)

            def transposes(c):
                if c == 0:
                    pe.wait_ge(dv_patch, 2)
                if counted(c // 2):
                    pe.wait_ge(dv_tg if c % 2 == 0 else ac_tg, c // 2)
                for t in range(2):
                    last = nc.tensor.transpose(bank[c % 2][0:CK, P * t:P * t + P], halo_rows(t, c // 8, c % 8), ident)
                last.then_inc(pe_tt, 1)

            def products(c):
                pe.wait_ge(dv_tg if c % 2 == 0 else ac_tg, c // 2 + 1)
                if c % TG == 0:
                    pe.wait_ge(ld_tws[c // TG], 16)
                for t in range(2):
                    last = mm(bank[2 + t][:, 0:D], xg[:, c % XG, P * t:P * t + P], tokw[:, c, :], start=c == 0, stop=c == CH - 1)
                last.then_inc(pe_tm, 1)

            def to_features(i):
                pe.wait_ge(dv_hl0, i + 1)
                if counted(2 * (i - 1)):
                    pe.wait_ge(ac_xt, 2 * (i - 1))
                for u in range(2):
                    o = bank[4 + 2 * (i % 2) + u][:].bitcast(F16)
                    r = hl[:, i % 2, u, :]
                    nc.tensor.transpose(o[:, 0:P], r[:, 0:P], id16[:])
                    nc.tensor.transpose(o[:, P:2 * P], r[:, 2 * P:3 * P], id16[:])
                    nc.tensor.transpose(o[:, 2 * P:3 * P], r[:, P:2 * P], id16[:]).then_inc(pe_xt, 1)

            for c in range(CH + 2):
                if c < CH:
                    transposes(c)
                if c >= 2:
                    products(c - 2)
                if c % 2 and 0 <= c // 2 - XT_AT < B // 2:
                    to_features(c // 2 - XT_AT)
            to_features(B // 2)

            def project(i, chunks):
                for c in chunks:
                    b = bank[c % 2]
                    if counted(i * 12 + (c - 1)):
                        pe.wait_ge(dv_st, i * 12 + (c - 1))
                    if c == 0:
                        if counted(i * 2 - 3):
                            pe.wait_ge(dv_h, i * 2 - 3)
                    elif c == 9:
                        if counted(i * 2 - 2):
                            pe.wait_ge(dv_h, i * 2 - 2)
                    cols = bass.ds(i * 2 * S, 2 * S)
                    for n, (k, t) in enumerate(((0, 0), (1, 0), (0, 1), (2, 2), (3, 2))):
                        last = mm(b[0:STK, 0:2 * S], wqk[:, k, stack_of(c), :], xt[:, t, cols], start=n == 0, stop=n == 4)
                    last.then_inc(pe_P, 1)

            def scores(i, par, u, n):
                b = bank[2 + n % 2]
                if n == 0:
                    pe.wait_ge(dv_kz, i * 2 + u + 1)
                    if not u:
                        if counted(i):
                            pe.wait_ge(dv_vb, i)
                        if counted(i):
                            pe.wait_ge(ac_vt, i)
                if not u:
                    pe.wait_ge(dv_st, i * 12 + min(7 + n, 12))
                if counted(i * 16 + (8 * u + n - 1)):
                    pe.wait_ge(dv_S, i * 16 + (8 * u + n - 1))
                if n < 6:
                    last = mm(b[:, 0:2 * S], qs[par][0:STK, n, u, 0:TXT], kz[u][0:STK, :, n, :], start=True, stop=True)
                else:
                    for r in range(4 * (n - 6), min(4 * (n - 6) + 4, PAIRS)):
                        c = 32 * (r % 4)
                        last = mm(b[c:c + IMG, 0:2 * S], qs[par][0:STK, r, u, TXT:S], kz[u][0:STK, :, r, :], start=True, stop=True)
                last.then_inc(pe_S, 1)

            def minus_max(i, u):
                pe.wait_ge(dv_S, i * 16 + (8 * u + 8))
                if counted(i * 14 + 7 * u):
                    pe.wait_ge(ac_exp, i * 14 + 7 * u)
                for r in range(PAIRS):
                    o = bank[4 + r // 3][STK:AUG, (r % 3) * S:(r % 3) * S + S]
                    mm(o[:, 0:TXT], mmax[u][:, 2 * r:2 * r + 2], negid16[:], start=True, stop=True)
                    c = 32 * (r % 4)
                    last = mm(o[:, TXT:S], mrem[u][:, r // 4, :], negid16[:, c:c + IMG], start=True, stop=True)
                last.then_inc(pe_A, 1)

            def values(i):
                pe.wait_ge(dv_S, i * 16 + 16)
                pe.wait_ge(po_xrep, i + 1)
                for image in range(2):
                    for u in range(2):
                        for n, (t, k) in enumerate(((0, 0), (0, 1), (1, 0), (2, 2), (2, 3))):
                            x = xrep[u][:, t, :] if image else xt[:, t, bass.ds((i * 2 + u) * S, TXT)]
                            last = mm(bank[2 + image][:, D * u:D * u + D], x, wv[:, k, :], start=n == 0, stop=n == 4)
                    last.then_inc(pe_V, 1)

            def scores_t(i, par, u, n):
                b = bank[4 + (n + u) % 2]
                if n == 0:
                    pe.wait_ge(dv_qz, i * 2 + u + 1)
                    pe.wait_ge(ac_aux, i * 2 + u + 1)
                if counted(i * 14 + (7 * u + n - 1)):
                    pe.wait_ge(ac_exp, i * 14 + (7 * u + n - 1))
                if n < 6:
                    last = mm(b[:, 0:2 * S], ks[par][:, n, u, 0:TXT], qz[u][:, :, n, :], start=True, stop=True)
                else:
                    for r in range(PAIRS):
                        c = 32 * (r % 4)
                        last = mm(b[c:c + 32, S * (r // 4):S * (r // 4) + S], kzi[u][:, r, :, :], qs[par][:, r, u, :], start=True, stop=True)
                last.then_inc(pe_ST, 1)

            def weighted(i, u):
                pe.wait_ge(ac_exp, i * 14 + (7 * u + 7))
                pe.wait_ge(ac_vt, i + 1)
                pe.wait_ge(dv_vb, i + 1)
                if counted(i * 2 + u):
                    pe.wait_ge(dv_n, i * 2 + u)
                for j in range(3):
                    k = P if j < 2 else 64
                    o = bank[6][:, S * j:S * j + S]
                    mm(o, vb[u][0:k, 4 * j:4 * j + 4, :], ptr[u][0:k, j // 2, :], start=True, stop=True)
                    for c in range(4):
                        last = mm(o[32 * c:32 * c + 32, :], vt[u][:, 4 * j + c, :], pt[u][:, 4 * j + c, :], start=False, stop=True,
                                  skip_group_check=True)
                last.then_inc(pe_PV, 1)

            def out_project(i, u, src):
                for j in range(3):
                    last = mm(bank[u][:, 0:D], src(j), wp[:, j, :], start=j == 0, stop=j == 2)
                last.then_inc(pe_OP, 1)

            def post_t(i, rows=rowb, b=7):
                pe.wait_ge(dv_hl, i + 1)
                if b == 7:
                    pe.wait_ge(dv_pos, i)
                for u in range(2):
                    o = bank[b][:].bitcast(F16)[:, 3 * P * u:3 * P * u + 3 * P]
                    r = rows[:, u, 0, 0:D].bitcast(F16)
                    nc.tensor.transpose(o[:, 0:P], r[:, 0:P], id16[:])
                    nc.tensor.transpose(o[:, P:2 * P], r[:, 2 * P:3 * P], id16[:])
                    last = nc.tensor.transpose(o[:, 2 * P:3 * P], r[:, P:2 * P], id16[:])
                last.then_inc(pe_T, 1)

            def post_router(i, b=7):
                pe.wait_ge(ac_x2, i + 1)
                for u in range(2):
                    for n, (t, k) in enumerate(((0, 0), (0, 1), (1, 0), (2, 2), (2, 3))):
                        last = mm(bank[b][:, 384 + 8 * u:392 + 8 * u], x2[:, u, t, :], rw[:, k, :], start=n == 0, stop=n == 4)
                last.then_inc(pe_R, 1)

            def post_rank(i, b=7):
                pe.wait_ge(dv_A, i + 1)
                pe.wait_ge(dv_pos, i)
                for u in range(2):
                    o = bank[b][:, 400 + 8 * u:408 + 8 * u]
                    mm(o, up16[:], a16[:, u, :], start=True, stop=False)
                    if u:
                        mm(o, ones16[:], a16[:, 0, :], start=False, stop=False)
                    last = mm(o, ones16[:], acc16, start=False, stop=True)
                last.then_inc(pe_K, 1)

            pe.wait_ge(dv_xt, 1)
            pe.wait_ge(ac_xt, B + 1)
            pe.wait_ge(po_wqk, 1)
            project(0, range(12))
            for j in range(3):
                last = mm(bank[6][0:32, 0:D], bv[:, j, :], wp[:, j, :], start=j == 0, stop=j == 2)
            last.then_inc(pe_bv, 1)
            for n in range(8):
                scores(0, 0, 0, n)
            minus_max(0, 0)

            def step(pe, i, par):
                first, last_ = isinstance(i, int) and i == 0, isinstance(i, int) and i == STEPS - 1
                for n in range(8):
                    if n < 7:
                        scores_t(i, par, 0, n)
                    scores(i, par, 1, n)
                    if not last_:
                        project(i + 1, [n])
                minus_max(i, 1)
                values(i)
                if not first:
                    pe.wait_ge(dv_n, i * 2)
                    pe.wait_ge(dv_st, i * 12 + (12 if last_ else 20))
                    out_project(i - 1, 1, lambda j: ot[1][:, j, 0:TXT])
                if not last_:
                    project(i + 1, [8, 9])
                weighted(i, 0)
                for n in range(8):
                    if n < 7:
                        scores_t(i, par, 1, n)
                    if not last_:
                        if n < 2:
                            project(i + 1, [10 + n])
                        scores(i + 1, 1 - par, 0, n)
                    if n == 6 and not first:
                        post_t(i - 1)
                pe.wait_ge(dv_n, i * 2 + 1)
                pe.wait_ge(dv_st, i * 12 + (12 if last_ else 24))
                if first:
                    pe.wait_ge(dv_wp, 1)
                out_project(i, 0, lambda j: ot[0][:, j, 0:TXT])
                if not first:
                    post_router(i - 1)
                if not last_:
                    minus_max(i + 1, 0)
                weighted(i, 1)
                if not first:
                    post_rank(i - 1)

            attention(step, pe)
            pe.wait_ge(dv_n, 2 * STEPS)
            out_project(STEPS - 1, 1, lambda j: ot[1][:, j, 0:TXT])
            pe.wait_ge(dv_h, 2 * STEPS)
            for u in range(2):
                out_project(STEPS, u, lambda j: oti[:, j, u, :])
            post_t(STEPS - 1)
            post_router(STEPS - 1)
            post_t(STEPS, rowb_last, 6)
            post_rank(STEPS - 1)
            post_router(STEPS, 6)
            post_rank(STEPS, 6)
            pe.wait_ge(dv_pos, STEPS + 1)
            mm(bank[7][0:1, 416:424], ones16[:, 0:1], acc16, start=True, stop=True).then_inc(pe_cnt, 1)

            def experts_of(s, n):
                return nc.values_load_multi_w_load_instructions(itab[0:1, bass.ds(s + 72, n)], engines=[nc.tensor.engine],
                                                                min_val=0, max_val=E - 1)[1]

            def slot_t(s, p, rows=SR):
                pe.wait_ge(slot_ld[p], ((s - p) * 4 + 16))
                if counted(s):
                    pe.wait_ge(dv_mT, s)
                o = bank[6][:].bitcast(F16)
                for h in range(rows // P):
                    r = xr[p][:, h, 0:D].bitcast(F16)
                    for c, at in enumerate((0, 2 * P, P)):
                        last = nc.tensor.transpose(o[:, SR * c + P * h:SR * c + P * h + P], r[:, at:at + P], id16[:])
                last.then_inc(pe_mT, 1)

            def up(s, q, e, rows=SR):
                pe.wait_ge(dv_mT, s + 1)
                for f in range(FC):
                    if f % 2 == 0:
                        if counted(s * 3 + (f // 2 - 5)):
                            pe.wait_ge(ac_g, s * 3 + (f // 2 - 5))
                    o = bank[3 * q + f // 2][:, SR * (f % 2):SR * (f % 2) + rows]
                    for n, (k, t) in enumerate(((0, 0), (0, 1), (1, 0), (2, 2), (3, 2))):
                        w = w1s[:, bass.ds(e, 1), k, P * f:P * f + P].rearrange("p a f -> p (a f)")
                        last = mm(o, w, xe[q][:, t, 0:rows], start=n == 0, stop=n == 4)
                    if f % 2:
                        last.then_inc(pe_up, 1)

            def down(s, q, e, rows=SR):
                if counted(s):
                    pe.wait_ge(dv_y, s)
                for h in range(rows // P):
                    for f in range(FC):
                        if h == 0 and f % 2 == 0:
                            pe.wait_ge(dv_gl, s * 3 + (f // 2 + 1))
                        at = SR * f + P * h
                        for k, halves in ((0, (gh, gl)), (1, (gh,))):
                            w = w2s[:, bass.ds(e, 1), k, D * f:D * f + D].rearrange("p a f -> p (a f)")
                            for g in halves:
                                last = mm(bank[7][:, D * h:D * h + D], g[q][:, at:at + P], w,
                                          start=f == 0 and k == 0 and g is gh, stop=f == FC - 1 and k == 1)
                last.then_inc(pe_L2, 1)

            pe.wait_ge(dv_tab, 2)
            slot_t(0, 0)
            pe.wait_ge(po_split, 4 * E)
            es = experts_of(0, 5)
            for s in range(5):
                up(s, s % 2, es[s])
                slot_t(s + 1, (s + 1) % 4)
                if s:
                    down(s - 1, (s - 1) % 2, es[s - 1])
            with pe.Fori(0, (LARGE - 5) // 4) as j:
                es = experts_of(j * 4 + 4, 5)
                for n in range(4):
                    s = j * 4 + (5 + n)
                    up(s, (5 + n) % 2, es[n + 1])
                    slot_t(s + 1, (6 + n) % 4)
                    down(j * 4 + (4 + n), n % 2, es[n])
            pe.wait_ge(dv_tab, 3)
            es = experts_of(LARGE - 1, SMALL + 1)
            for n in range(SMALL):
                s = LARGE + n
                up(s, s % 2, es[n + 1], P)
                if n + 1 < SMALL:
                    slot_t(s + 1, (s + 1) % 4, P)
                down(s - 1, (s - 1) % 2, es[n], P if n else SR)
            down(SLOTS - 1, (SLOTS - 1) % 2, es[SMALL], P)

        @block.scalar
        def _(act):
            actf = nc.scalar.activation
            nc.scalar.preload_act_table(ACT.Exp)
            act.wait_ge(ld_c, 16)
            act.wait_ge(ld_tw, 16)

            def to_xt(i):
                for u in range(2):
                    act.wait_ge(pe_xt, 2 * i + u + 1)
                    src = bank[4 + 2 * (i % 2) + u][:].bitcast(F16)[:, 0:3 * P].rearrange("p (c t) -> p c t", c=3)
                    actf(xt[:, :, (2 * i + u) * S:(2 * i + u) * S + TXT], src, ACT.Copy).then_inc(ac_xt, 1)

            for c in range(1, CH, 2):
                act.wait_ge(pe_tt, c + 1)
                if counted(c - XG + 1):
                    act.wait_ge(pe_tm, c - XG + 1)
                actf(xg[:, c % XG, :], bank[1][0:CK, 0:256], ACT.Identity, bias=tokgb[:, 1, c:c + 1], scale=tokgb[:, 0, c:c + 1]).then_inc(ac_tg, 1)
                if 0 <= c // 2 - XT_AT - 1 < B // 2:
                    to_xt(c // 2 - XT_AT - 1)
            act.wait_ge(ld_wp, 96)
            for k in range(2):
                last = actf(bqlo[:, PAIRS * k:PAIRS * k + PAIRS], bq[:, PAIRS * k:PAIRS * k + PAIRS], ACT.Copy,
                            scale=cst[0:STK, C_LOQ + k:C_LOQ + k + 1])
            last.then_inc(ac_misc, 1)
            act.wait_ge(ac_misc, 1)
            act.wait_ge(pe_xt, B + 2)
            for c in range(3):
                src = bank[5][:].bitcast(F16)[:, P * c:P * c + P].rearrange("p (b t) -> p b t", b=8)
                last = actf(xt[:, c, :].rearrange("p (b t) -> p b t", b=B)[:, 8:B, TXT:S], src, ACT.Copy)
            last.then_inc(ac_xt, 1)

            def low_half(i, chunks):
                for c in chunks:
                    act.wait_ge(pe_P, i * 12 + (c + 1))
                    if counted(i * 12 + (c - 1)):
                        act.wait_ge(dv_st, i * 12 + (c - 1))
                    q = stack_of(c)
                    actf(hm[c % 2], bank[c % 2][0:STK, 0:2 * S], ACT.Identity, bias=bqlo[:, q:q + 1],
                             scale=cst[0:STK, C_LOQ + q // PAIRS:C_LOQ + q // PAIRS + 1]).then_inc(ac_hm, 1)

            def aux(i, par, u):
                act.wait_ge(pe_A, i * 2 + u + 1)
                for k in range(2):
                    last = actf(qs[par][STK:AUG, 3 * k:3 * k + 3, u, :], bank[4 + k][STK:AUG, 0:3 * S].rearrange("p (r t) -> p r t", r=3), ACT.Copy)
                last.then_inc(ac_aux, 1)

            def exps(i, u, n):
                if n == 0:
                    if counted(i * 2 + (u - 1)):
                        act.wait_ge(pe_PV, i * 2 + (u - 1))
                b = bank[4 + (n + u) % 2]
                act.wait_ge(pe_ST, i * 14 + (7 * u + n + 1))
                if n < 6:
                    last = actf(pt[u][:, 2 * n:2 * n + 2, :], b[:, 0:2 * S].rearrange("p (h t) -> p h t", h=2), ACT.Exp, scale=DH ** -0.5)
                else:
                    actf(ptr[u][:, 0, :], b[:, 0:S], ACT.Exp, scale=DH ** -0.5)
                    last = actf(ptr[u][0:64, 1, :], b[0:64, S:2 * S], ACT.Exp, scale=DH ** -0.5)
                last.then_inc(ac_exp, 1)

            def value_rows(i):
                act.wait_ge(pe_V, i * 2 + 1)
                if counted(i * 2):
                    act.wait_ge(pe_PV, i * 2)
                actf(vts[:, :, 0:DH], bank[2][:, 0:2 * D].rearrange("p (h d) -> p h d", h=2 * HEADS), ACT.Copy).then_inc(ac_vt, 1)

            def post_x2(i, b=7):
                act.wait_ge(pe_T, i + 1)
                actf(x2.rearrange("p u c t -> p (u c t)"), bank[b][:].bitcast(F16)[:, 0:6 * P], ACT.Copy).then_inc(ac_x2, 1)

            def post_exp(i):
                act.wait_ge(dv_l, i + 1)
                actf(pr, lg, ACT.Exp).then_inc(ac_sm, 1)

            def split_high(e, n):
                slot_, size, dst, k, at = PARTS[n]
                act.wait_ge(ld_stage[n], e * (32 if n == 1 else 16) + (32 if n == 1 else 16))
                hi = dst[:, bass.ds(e, 1), k, at:at + size].rearrange("p a f -> p (a f)")
                actf(hi, stage[:, slot_, 0:size], ACT.Copy).then_inc(ac_split, 1)

            low_half(0, range(12))
            aux(0, 0, 0)

            def step(act, i, par):
                first, last_ = isinstance(i, int) and i == 0, isinstance(i, int) and i == STEPS - 1
                for n in range(8):
                    if n < 7:
                        exps(i, 0, n)
                    if not last_:
                        low_half(i + 1, [n])
                aux(i, par, 1)
                value_rows(i)
                if not first:
                    split_high(i - 1, 0)
                if not last_:
                    low_half(i + 1, [8, 9])
                if not first:
                    split_high(i - 1, 1)
                for n in range(7):
                    if n < 2 and not last_:
                        low_half(i + 1, [10 + n])
                    exps(i, 1, n)
                if not first:
                    post_x2(i - 1)
                if not last_:
                    aux(i + 1, 1 - par, 0)
                if not first:
                    post_exp(i - 1)
                    split_high(i - 1, 2)
                    split_high(i - 1, 3)

            attention(step, act)
            for n in range(3):
                split_high(E - 1, n)
            for i, b in ((STEPS - 1, 7), (STEPS, 6)):
                post_x2(i, b)
                post_exp(i)
            split_high(E - 1, 3)
            act.wait_ge(dv_tab, 1)
            for r in nc.values_load_multi_w_load_instructions(itab[0:1, 64 + E // 2:64 + E], engines=[nc.scalar.engine],
                                                              min_val=0, max_val=SPARE - SR)[1]:
                act.dma_start(routed[bass.ds(r, SR), :].rearrange("(p h) w -> p h w", h=2), twice).then_inc(pads_in, 16)
            nc.scalar.preload_act_table(ACT.Gelu_apprx_tanh)

            def gelus(s, q, rows=SR):
                for b in range(3):
                    act.wait_ge(pe_up, s * 3 + (b + 1))
                    if b == 0:
                        if counted(s - 1):
                            act.wait_ge(pe_L2, s - 1)
                    if counted(s * 3 + (b - 2)):
                        act.wait_ge(dv_gl, s * 3 + (b - 2))
                    src = chunks_of(bank[3 * q + b], 0, rows)
                    actf(chunks_of(gh[q], b, rows), src, ACT.Gelu_apprx_tanh)
                    actf(chunks_of(g32[b], 0, rows), src, ACT.Gelu_apprx_tanh).then_inc(ac_g, 1)

            for s in range(5):
                gelus(s, s % 2)
            with act.Fori(0, (LARGE - 5) // 4) as j:
                for n in range(4):
                    gelus(j * 4 + (5 + n), (5 + n) % 2)
            for s in range(LARGE, SLOTS):
                gelus(s, s % 2, P)
            act.wait_ge(dv_out, 1)
            for u in range(2):
                act.dma_start(out[8 * u:8 * u + 8, 0:IMG, :], of[0][:, u, :]).then_inc(out_st, 16)
            for i in range(B // 2):
                act.wait_ge(dv_out, 2 + i)
                act.dma_start(out[2 * i:2 * i + 2, IMG:S, :].rearrange("b t d -> t b d"), of[1 + i]).then_inc(out_st, 16)
            act.wait_ge(out_st, 16 * (2 + B // 2))

        @block.vector
        def _(dve):
            v = nc.vector
            link = Link(dve, dv_link)
            dve.wait_ge(ld_c, 16)
            v.tensor_copy(id16[:], ident)
            v.tensor_scalar(negid16[:], ident, -1.0, None, ALU.mult)
            v.tensor_copy(up16[:], cst[:, C_UP:C_UP + P])
            v.memset(bank[2][:], 0.0)
            v.memset(bank[3][:], 0.0)
            v.memset(ones16[:], 1.0).then_inc(dv_pre, 1)
            dve.wait_ge(ld_halo, 16)
            for t in range(2):
                for s in range(5):
                    dr, dc = SHIFTS[s]
                    view = patch[:, t, :].rearrange("p (r c) -> p r c", r=18)
                    for k in range(2):
                        last = v.bn_stats(bst[:, t, 2 * s + k, :], view[:, dr + 8 * k:dr + 8 * k + 8, 3 * dc:3 * dc + 48])
                link(last)
                link(v.bn_aggr(mv[:, t, :], bst[:, t, :, :].rearrange("p k s -> p (k s)")))
            v.tensor_scalar(ve[:, 0:2], mv[:, 0:2, 1], EPS_TOK, None, ALU.add).then_inc(dv_var0, 1)
            dve.wait_ge(po_rs0, 1)
            for t in range(2):
                v.tensor_scalar(patch[:, t, :], patch[:, t, :], mv[:, t, 0:1], rs[:, t:t + 1], ALU.subtract, ALU.mult).then_inc(dv_patch, 1)
            def tile_stats(t):
                return v.bn_stats(bst_tiles[:, t, :], h1[:, t, :])

            def tile_variances(tiles):
                for t in tiles:
                    last = v.bn_aggr(mv[:, t, :], bst_tiles[:, t, :])
                link(last)
                a, b = tiles[0], tiles[-1] + 1
                v.tensor_scalar(ve[:, a:b], mv[:, a:b, 1], EPS_LN, None, ALU.add).then_inc(dv_var0, 1)

            def norm(i):
                dve.wait_ge(po_rs0, 2 if i < B // 2 else 3)
                if counted(i):
                    dve.wait_ge(dv_hl0, i)
                for u in range(2):
                    t = 2 * i + u
                    last = v.tensor_scalar(xn32[:, u, :], h1[:, t, :], mv[:, t, 0:1], rs[:, t:t + 1], ALU.subtract, ALU.mult)
                link(last)
                if counted(2 * (i - 1)):
                    dve.wait_ge(pe_xt, 2 * (i - 1))
                r = hl[:, i % 2, :, :]
                link(v.tensor_copy(r[:, :, 0:D], xn32[:]))
                v.tensor_tensor(r[:, :, D:2 * P], xn32[:, :, P:D], r[:, :, P:D], ALU.subtract)
                v.tensor_tensor(r[:, :, 2 * P:3 * P], xn32[:, :, 0:P], r[:, :, 0:P], ALU.subtract).then_inc(dv_hl0, 1)

            dve.wait_ge(ld_tw, 16)
            for m in range(CH // 2):
                c = 2 * m
                dve.wait_ge(pe_tt, c + 1)
                if counted(c - XG + 1):
                    dve.wait_ge(pe_tm, c - XG + 1)
                v.tensor_scalar(xg[:, c % XG, :], bank[0][0:CK, 0:256], tokgb[:, 0, c:c + 1], tokgb[:, 1, c:c + 1], ALU.mult, ALU.add).then_inc(dv_tg, 1)
                if 1 <= m < 5:
                    if m % 2:
                        dve.wait_ge(ld_txts[m // 2], 16)
                    for t in range(4 * (m - 1), 4 * m):
                        last = tile_stats(t)
                    if m == 4:
                        link(last)
                        tile_variances(range(B))
                if 0 <= m - XT_AT + 1 < B // 2:
                    norm(m - XT_AT + 1)
            dve.wait_ge(ld_row, 16)
            dve.wait_ge(pe_tm, CH)
            for t in range(2):
                last = v.tensor_tensor(h1[:, B + t, :], bank[2 + t][:, 0:D], rowv, ALU.add)
            link(last)
            for t in range(2):
                last = tile_stats(B + t)
            link(last)
            tile_variances(range(B, NT))
            norm(B // 2)
            dve.wait_ge(pe_xt, B + 1)
            for c in range(3):
                src = bank[4][:].bitcast(F16)[:, P * c:P * c + P].rearrange("p (b t) -> p b t", b=8)
                last = v.tensor_copy(xt[:, c, :].rearrange("p (b t) -> p b t", b=B)[:, 0:8, TXT:S], src)
            last.then_inc(dv_xt, 1)
            dve.wait_ge(po_const, 2)

            def stacks(i, par, chunks):
                for c in chunks:
                    dve.wait_ge(ac_hm, i * 12 + (c + 1))
                    q = stack_of(c)
                    dst = (qs, ks)[q // PAIRS][par][0:STK, q % PAIRS, :, :].rearrange("p u t -> p (u t)")
                    v.scalar_tensor_tensor(dst, bank[c % 2][0:STK, 0:2 * S], bq[:, q:q + 1], hm[c % 2], ALU.add, ALU.subtract).then_inc(dv_st, 1)

            def separate(which, i, par, u):
                src, dst, ready = (ks, kz, dv_kz) if which == "k" else (qs, qz, dv_qz)
                if which == "q":
                    dve.wait_ge(ac_aux, i * 2 + u + 1)
                else:
                    dve.wait_ge(dv_st, i * 12 + 6)
                    if counted(i * 14 + 7 * u - 7 if u else i * 14 - 7):
                        dve.wait_ge(pe_ST, i * 14 + 7 * u - 7 if u else i * 14 - 7)
                for h in range(2):
                    last = v.tensor_scalar(dst[u][:, h, :, :], src[par][:, :, u, :], cst[0:AUG, C_Z + h:C_Z + h + 1], None, ALU.mult)
                if which == "k":
                    for h in range(2):
                        last = v.tensor_scalar(kzi[u][:, :, h, :], ks[par][:, :, u, TXT:S], cst[0:AUG, C_Z + h:C_Z + h + 1], None, ALU.mult)
                last.then_inc(ready, 1)

            def maxima(i, u, n):
                dve.wait_ge(pe_S, i * 16 + (8 * u + n + 1))
                if n == 0:
                    if counted(i * 2 + (u - 1)):
                        dve.wait_ge(pe_A, i * 2 + (u - 1))
                b = bank[2 + n % 2][:, 0:2 * S].rearrange("p (h t) -> p h t", h=2)
                if n < 6:
                    last = v.tensor_reduce(mmax[u][:, 2 * n:2 * n + 2], b, AX, ALU.max)
                elif n == 6:
                    last = v.tensor_reduce(mrem[u][:, 0, :], b, AX, ALU.max)
                else:
                    last = v.tensor_reduce(mrem[u][0:64, 1, :], b[0:64], AX, ALU.max)
                last.then_inc(dv_S, 1)

            def block_values(i):
                dve.wait_ge(pe_V, i * 2 + 2)
                if counted(i * 2):
                    dve.wait_ge(pe_PV, i * 2)
                m = cst[:, C_VM:C_VM + HEADS].rearrange("p (h o) -> p h o", o=1).broadcast_to([P, HEADS, DH])
                for u in range(2):
                    last = v.tensor_tensor(vb[u][:, :, 0:DH], bank[3][:, D * u:D * u + D].rearrange("p (h d) -> p h d", h=HEADS), m, ALU.mult)
                last.then_inc(dv_vb, 1)

            def normalise(i, u, part, before):
                if 1 <= part <= 3:
                    dve.wait_ge(dv_link, before)
                if part == 0:
                    dve.wait_ge(pe_PV, i * 2 + u + 1)
                    last = v.transpose(rden, bank[6][:, 0:32 * NBLK])
                elif part == 1:
                    last = v.reciprocal(rec, rden.rearrange("p (k b) -> p k b", b=32)[:, :, DH:DH + 1].rearrange("p k o -> p (k o)"))
                elif part == 2:
                    last = v.transpose(rden, rec.rearrange("p (k o) -> p k o", o=1).broadcast_to([P, NBLK, 32]))
                elif part == 3:
                    if counted(i * 2 + (u - 1)):
                        dve.wait_ge(pe_OP, i * 2 + (u - 1))
                    v.tensor_tensor(ot[u].rearrange("p j t -> p (j t)"), bank[6][:, 0:3 * S], rden[:, 0:3 * S], ALU.mult).then_inc(dv_n, 1)
                    return
                else:
                    dve.wait_ge(dv_n, i * 2 + u + 1)
                    dst = oti.rearrange("p j i (b t) -> p j (i b) t", b=8)[:, :, bass.ds(i * 2 + u, 1), :].rearrange("p j b t -> p j (b t)")
                    last = v.tensor_copy(dst, ot[u][:, :, TXT:S])
                return link.put(last)

            def residual(i, u):
                dve.wait_ge(pe_OP, i * 2 + u + 1)
                t = h1[:, bass.ds(i * 2 + u, 1), :].rearrange("p a d -> p (a d)")
                v.tensor_tensor(t, bank[u][:, 0:D], t, ALU.add).then_inc(dv_h, 1)

            def post_stats(i, k=0):
                wait_alone(dve, dv_h, i * 2 + 2)
                for u in range(2):
                    last = v.bn_stats(bst[:, u, 0, :], h1[:, bass.ds(i * 2 + u, 1), :].rearrange("p a d -> p (a d)"))
                link(last)
                v.memset(scrap[:], 0.0)
                for u in range(2):
                    last = v.bn_aggr(mv[:, k + u, :], bst[:, u, 0, :])
                link(last)
                v.tensor_scalar(ve[:, k:k + 2], mv[:, k:k + 2, 1], EPS_LN, None, ALU.add).then_inc(dv_var, 1)

            def post_rows(i, part, before, rows=rowb, k=0):
                r = rows[:, :, 0, 0:D].bitcast(F16)
                if part == 0:
                    dve.wait_ge(po_rs, i + 1)
                    for u in range(2):
                        t = h1[:, bass.ds(i * 2 + u, 1), :].rearrange("p a d -> p (a d)")
                        last = v.tensor_scalar(xn32[:, u, :], t, mv[:, k + u, 0:1], rs[:, k + u:k + u + 1], ALU.subtract, ALU.mult)
                    return link.put(last)
                dve.wait_ge(dv_link, before)
                if part == 1:
                    if k == 0 and not (isinstance(i, int) and i == 0):
                        dve.wait_ge(row_st, i * 64)
                    return link.put(v.tensor_copy(r[:, :, 0:D], xn32[:]))
                v.tensor_tensor(r[:, :, D:2 * P], xn32[:, :, P:D], r[:, :, P:D], ALU.subtract)
                v.tensor_tensor(r[:, :, 2 * P:3 * P], xn32[:, :, 0:P], r[:, :, 0:P], ALU.subtract).then_inc(dv_hl, 1)

            def const8(c, shape):
                ap = cst[:, c:c + E]
                return (ap.rearrange("p (o e) -> p o e", o=1) if len(shape) == 3 else ap.rearrange("p (o q e) -> p o q e", o=1, q=1)).broadcast_to(shape)

            def route(i, part, before, b=7, rows=rowb):
                if part:
                    dve.wait_ge(dv_link, before)
                l = bank[b][:, 384:400].rearrange("p (u e) -> p u e", u=2)
                if part == 0:
                    dve.wait_ge(pe_R, i + 1)
                if part < 2:
                    v.memset(scrap[:], 0.0)
                if part == 0:
                    for u in range(2):
                        last = v.max(top[:, u, :], l[:, u, :])
                elif part == 1:
                    for u in range(2):
                        last = v.max_index(topi[:, u, :], top[:, u, :], l[:, u, :])
                elif part == 2:
                    v.tensor_tensor(lg, top, top[:, :, 0:1].broadcast_to([P, 2, E]), ALU.subtract).then_inc(dv_l, 1)
                    last = v.tensor_copy(topf, topi[:, :, 0:2])
                elif part == 3:
                    last = v.tensor_tensor(oh, const8(C_SLOT, [P, 2, 2, E]),
                                           topf.rearrange("p u (k o) -> p u k o", o=1).broadcast_to([P, 2, 2, E]), ALU.is_equal)
                elif part == 4:
                    last = v.tensor_tensor(a16, oh[:, :, 0, :], oh[:, :, 1, :], ALU.add)
                    v.memset(scrap[:], 0.0).then_inc(dv_A, 1)
                elif part == 5:
                    dve.wait_ge(ac_sm, i + 1)
                    last = v.tensor_reduce(den, pr, AX, ALU.add)
                elif part == 6:
                    last = v.reciprocal(den, den)
                else:
                    dve.wait_ge(po_row, i + 1)
                    last = v.tensor_tensor(rows[:, :, :, ROW_GATE:ROW_GATE + 1].rearrange("p u k o -> p u (k o)"), pr[:, :, 0:2],
                                           den.rearrange("p (u o) -> p u o", o=1).broadcast_to([P, 2, 2]), ALU.mult)
                return link.put(last)

            def post_pos(i, b=7, to=pos):
                dve.wait_ge(pe_K, i + 1)
                link(v.tensor_tensor(place, bank[b][:, 400:416].rearrange("p (u e) -> p u e", u=2), const8(C_ER, [P, 2, E]), ALU.add))
                v.tensor_tensor(acc16, acc16, a16[:, 0, :], ALU.add)
                link(v.tensor_tensor(hit, oh, place.rearrange("p u (o e) -> p u o e", o=1).broadcast_to([P, 2, 2, E]), ALU.mult))
                v.tensor_tensor(acc16, acc16, a16[:, 1, :], ALU.add)
                with nc.allow_low_precision(reason="one term of each sum is not zero, a whole number"):
                    v.tensor_reduce(to, hit, AX, ALU.add).then_inc(dv_pos, 1)

            stacks(0, 0, range(12))
            separate("k", 0, 0, 0)
            separate("k", 0, 0, 1)

            for n in range(8):
                maxima(0, 0, n)
            separate("q", 0, 0, 0)
            dve.wait_ge(pe_bv, 1)
            v.tensor_tensor(wp[0:32, 0, :], wp[0:32, 0, :], bank[6][0:32, 0:D], ALU.add).then_inc(dv_wp, 1)
            dve.wait_ge(dv_wp, 1)
            v.memset(bank[6][:, 3 * S:32 * NBLK], 1.0)

            def step(dve, i, par):
                first, last_ = isinstance(i, int) and i == 0, isinstance(i, int) and i == STEPS - 1
                at = None
                for n in range(8):
                    maxima(i, 1, n)
                    if not last_:
                        stacks(i + 1, 1 - par, [n])
                    if n < 5 and not first:
                        at = normalise(i - 1, 1, n, at)
                if not last_:
                    separate("k", i + 1, 1 - par, 0)
                separate("q", i, par, 1)
                block_values(i)
                if not first:
                    dve.wait_ge(dv_link, at)
                    residual(i - 1, 1)
                if not last_:
                    stacks(i + 1, 1 - par, [8, 9])
                if not first:
                    post_stats(i - 1)
                at = rows_at = None
                for n in range(8):
                    if not last_:
                        if n < 2:
                            stacks(i + 1, 1 - par, [10 + n])
                        maxima(i + 1, 0, n)
                    if n < 5:
                        at = normalise(i, 0, n, at)
                    if 1 <= n < 4 and not first:
                        rows_at = post_rows(i - 1, n - 1, rows_at)
                routed_at = None
                if not last_:
                    separate("k", i + 1, 1 - par, 1)
                if not first:
                    for part in range(5):
                        routed_at = route(i - 1, part, routed_at)
                if not last_:
                    separate("q", i + 1, 1 - par, 0)
                dve.wait_ge(dv_link, at)
                residual(i, 0)
                if not first:
                    for part in range(5, 8):
                        routed_at = route(i - 1, part, routed_at)
                    post_pos(i - 1)

            link.per = 44
            attention(step, dve, link)

            def post(i, b, rows, to):
                at = None
                for part in range(8):
                    at = route(i, part, at, b, rows)
                post_pos(i, b, to)

            at = None
            for part in range(5):
                at = normalise(STEPS - 1, 1, part, at)
            dve.wait_ge(dv_link, at)
            residual(STEPS - 1, 1)
            post_stats(STEPS - 1)
            residual(STEPS, 0)
            residual(STEPS, 1)
            post_stats(STEPS, 2)
            for part in range(3):
                at = post_rows(STEPS - 1, part, at)
            dve.wait_ge(dv_hl, STEPS)
            dve.wait_ge(po_zero, 1)
            for part in range(3):
                at = post_rows(STEPS, part, at, rowb_last, 2)
            post(STEPS - 1, 7, rowb, pos)
            post(STEPS, 6, rowb_last, pos_last)
            dve.wait_ge(pe_cnt, 1)
            dve.wait_ge(dv_pos, STEPS + 1)
            cnt, til, cum, fl, half, odd, rank, row8 = [ctab[0:1, 8 * i:8 * i + 8] for i in range(8)]
            cross = ctab[0:1, 64:128].rearrange("p (a b) -> p a b", a=E)
            tri = cst[0:1, C_TRI:C_TRI + E * E].rearrange("p (a b) -> p a b", a=E)
            count1, count2, block1, block2 = [itab[0:1, 32 + 8 * i:40 + 8 * i] for i in range(4)]

            def along(row, n):
                return row.rearrange("p (o e) -> p o e", o=1).broadcast_to([1, n, E])

            def running(to, row):
                link(v.tensor_tensor(cross, along(row, E), tri, ALU.mult))
                link(v.tensor_reduce(to, cross, AX, ALU.add))

            link(v.tensor_copy(cnt, bank[7][0:1, 416:424]))
            v.tensor_tensor(itab[0:1, 64:72], cnt, cst[0:1, C_ER:C_ER + E], ALU.add).then_inc(dv_tab, 1)
            v.tensor_scalar(half, cnt, SR - 1.0, None, ALU.add)
            link(v.tensor_scalar(fl, cnt, P - 1.0, None, ALU.add))
            v.tensor_copy(count2, half)
            link(v.tensor_copy(count1, fl))
            v.tensor_scalar(block2, count2, SR.bit_length() - 1, None, ALU.arith_shift_right)
            link(v.tensor_scalar(block1, count1, P.bit_length() - 1, None, ALU.arith_shift_right))
            v.tensor_copy(half, block2)
            link(v.tensor_copy(fl, block1))
            link(v.scalar_tensor_tensor(odd, half, 2.0, fl, ALU.mult, ALU.subtract))
            running(rank, odd)
            link(v.tensor_scalar(fl, rank, float(SMALL), None, ALU.is_le))
            link(v.tensor_tensor(odd, odd, fl, ALU.mult))
            link(v.tensor_tensor(til, half, odd, ALU.subtract))
            running(cum, til)
            slots = cst[0:1, C_SLOT:C_SLOT + LARGE]
            ge = ctab[0:1, 128:128 + LARGE * E].rearrange("p (s e) -> p s e", s=LARGE)
            st = ctab[0:1, 460:460 + SLOTS]
            ex = ctab[0:1, 510:510 + SLOTS]
            big = slice(0, LARGE)
            link(v.tensor_tensor(ge, slots.rearrange("p (s o) -> p s o", o=1).broadcast_to([1, LARGE, E]), along(cum, LARGE), ALU.is_ge))
            link(v.tensor_reduce(ex[:, big], ge, AX, ALU.add))
            link(v.tensor_tensor(ge, ge, along(til, LARGE), ALU.mult))
            link(v.tensor_reduce(st[:, big], ge, AX, ALU.add))
            link(v.tensor_tensor(st[:, big], slots, st[:, big], ALU.subtract))
            link(v.tensor_scalar(st[:, big], st[:, big], float(SR), None, ALU.mult))
            link(v.scalar_tensor_tensor(st[:, big], ex[:, big], float(REGION), st[:, big], ALU.mult, ALU.add))
            v.tensor_scalar(itab[0:1, big], st[:, big], float(SPARE), None, ALU.min)
            v.tensor_scalar(itab[0:1, 72:72 + LARGE], ex[:, big], float(E - 1), None, ALU.min).then_inc(dv_tab, 1)
            small = slice(LARGE, SLOTS)
            number = cst[0:1, C_SLOT + 1:C_SLOT + 1 + SMALL].rearrange("p (s o) -> p s o", o=1).broadcast_to([1, SMALL, E])
            own = ctab[0:1, 560:560 + SMALL * E].rearrange("p (s e) -> p s e", s=SMALL)
            part = ctab[0:1, 560 + SMALL * E:560 + 2 * SMALL * E].rearrange("p (s e) -> p s e", s=SMALL)
            link(v.tensor_tensor(own, number, along(rank, SMALL), ALU.is_equal))
            link(v.tensor_tensor(own, own, along(odd, SMALL), ALU.mult))
            link(v.scalar_tensor_tensor(row8, til, float(SR), cst[0:1, C_ER:C_ER + E], ALU.mult, ALU.add))
            link(v.tensor_scalar(row8, row8, -float(SPARE), None, ALU.add))
            link(v.tensor_tensor(part, own, along(row8, SMALL), ALU.mult))
            link(v.tensor_reduce(st[:, small], part, AX, ALU.add))
            link(v.tensor_scalar(st[:, small], st[:, small], float(SPARE), None, ALU.add))
            link(v.tensor_tensor(part, own, along(cst[0:1, C_DESC:C_DESC + E], SMALL), ALU.mult))
            link(v.tensor_reduce(ex[:, small], part, AX, ALU.add))
            link(v.tensor_scalar(ex[:, small], ex[:, small], -1.0, float(E), ALU.mult, ALU.add))
            v.tensor_scalar(itab[0:1, small], st[:, small], float(SPARE), None, ALU.min)
            v.tensor_scalar(itab[0:1, 72 + LARGE:72 + SLOTS], ex[:, small], float(E - 1), None, ALU.min).then_inc(dv_tab, 1)

            def low_g(s, q, b, rows):
                dve.wait_ge(ac_g, s * 3 + (b + 1))
                v.tensor_tensor(chunks_of(gl[q], b, rows), chunks_of(g32[b], 0, rows), chunks_of(gh[q], b, rows), ALU.subtract).then_inc(dv_gl, 1)

            def slot_x(s, q, rows=SR):
                dve.wait_ge(pe_mT, s + 1)
                if counted(s * 3 - 3):
                    dve.wait_ge(pe_up, s * 3 - 3)
                x = bank[6][:].bitcast(F16)[:, 0:3 * SR]
                if rows == SR:
                    v.tensor_copy(xe[q].rearrange("p c t -> p (c t)"), x).then_inc(dv_mT, 1)
                else:
                    v.tensor_copy(xe[q][:, :, 0:rows], x.rearrange("p (c t) -> p c t", c=3)[:, :, 0:rows]).then_inc(dv_mT, 1)

            def slot_y(s, p, rows=SR):
                dve.wait_ge(pe_L2, s + 1)
                if not isinstance(s, int) or s >= 4:
                    dve.wait_ge(y_st[p], (s - p) * 8)
                for h in range(rows // P):
                    last = v.tensor_scalar(yb[p][:, h, :], bank[7][:, D * h:D * h + D], xr[p][:, h, ROW_GATE:ROW_GATE + 1], None, ALU.mult)
                last.then_inc(dv_y, 1)

            def slot_step(s, p, rows=SR, before=SR):
                low_g(s, p % 2, 0, rows)
                if not isinstance(s, int) or s + 1 < SLOTS:
                    slot_x(s + 1, (p + 1) % 2, rows)
                low_g(s, p % 2, 1, rows)
                low_g(s, p % 2, 2, rows)
                if not isinstance(s, int) or s:
                    slot_y(s - 1, (p - 1) % 4, before)

            slot_x(0, 0)
            for s in range(5):
                slot_step(s, s % 4)
            with dve.Fori(0, (LARGE - 5) // 4) as j:
                for n in range(4):
                    slot_step(j * 4 + (5 + n), (5 + n) % 4)
            for s in range(LARGE, SLOTS):
                slot_step(s, s % 4, P, SR if s == LARGE else P)
            slot_y(SLOTS - 1, (SLOTS - 1) % 4, P)

            def finish(g):
                t = B if g == 0 else 2 * g - 2
                dve.wait_ge(dv_link, sums[g])
                v.tensor_tensor(of[g], h1[:, t:t + 2, :], yk[g][:, :, 0, :], ALU.add).then_inc(dv_out, 1)

            sums = []
            for g in range(NT // 2):
                dve.wait_ge(yk_ld[g], 32 if g == 0 else 16)
                sums.append(link.put(v.tensor_tensor(yk[g][:, :, 0, :], yk[g][:, :, 0, :], yk[g][:, :, 1, :], ALU.add)))
                if g:
                    finish(g - 1)
            finish(NT // 2 - 1)

        @block.gpsimd
        def _(pool):
            g = nc.gpsimd
            link = Link(pool, po_link)
            link(g.memset(nhalf[:], -0.5))

            def powers(a, b):
                return g.tensor_tensor(rs[:, a:b], ve[:, a:b], nhalf[:, 0:b - a], ALU.pow)

            pool.wait_ge(dv_var0, 1)
            powers(0, 2).then_inc(po_rs0, 1)
            pool.wait_ge(ld_c, 16)
            for u in range(2):
                g.memset(vt[u][:, :, DH:32], 1.0)
                for k in range(DH):
                    g.tensor_copy(vb[u][:, :, DH + k:DH + k + 1].rearrange("p h o -> p (h o)"), cst[:, C_VM:C_VM + HEADS])
                g.memset(mrem[u], 0.0)
            g.memset(acc16, 0.0)
            link(g.memset(padrow, 0.0))
            link(g.memset(padrow[:, ROW_ID:ROW_ID + 1].bitcast(I32), 1 << 24))
            link(g.memset(ks[0][STK:AUG, :, :, :], 1.0))
            g.memset(rowb.rearrange("p u k w -> p (u k w)"), 0.0).then_inc(po_const, 1)

            pool.wait_ge(ld_wa, 48)
            pool.wait_ge(ld_wp, 96)
            for k in range(2):
                g.tensor_copy(wt16[:, 2 * k, :], wa32[:, k, 0:2 * D])
                g.tensor_copy(wv[:, 2 * k, :], wa32[:, k, 2 * D:3 * D])
                last = g.tensor_copy(rw[:, 2 * k, :], rw32[:, k, :])
            link(last)
            for k in range(2):
                g.tensor_tensor(wt16[:, 2 * k + 1, :], wa32[:, k, 0:2 * D], wt16[:, 2 * k, :], ALU.subtract)
                g.tensor_tensor(wv[:, 2 * k + 1, :], wa32[:, k, 2 * D:3 * D], wv[:, 2 * k, :], ALU.subtract)
                last = g.tensor_tensor(rw[:, 2 * k + 1, :], rw32[:, k, :], rw[:, 2 * k, :], ALU.subtract)
            link(last)
            pool.wait_ge(dv_var0, 2)
            powers(0, B).then_inc(po_rs0, 1)
            for k in range(4):
                for s in range(3):
                    dst = wqk[:, k, :, :].rearrange("p r (h s d) -> p (r h) s d", h=2, s=3)[:, :, s, :]
                    last = g.tensor_copy(dst, wt16[:, k, :].rearrange("p (n d) -> p n d", d=DH))
            last.then_inc(po_wqk, 1)
            pool.wait_ge(dv_var0, 3)
            powers(B, NT).then_inc(po_rs0, 1)
            pool.wait_ge(po_rs0, 3)
            pool.wait_ge(pe_tm, CH)
            g.memset(ks[1][STK:AUG, :, :, :], 1.0).then_inc(po_const, 1)
            pool.wait_ge(po_const, 2)
            pool.wait_ge(dv_xt, 1)
            pool.wait_ge(ac_xt, B + 1)

            def image_rows(i):
                if counted(i * 2):
                    wait_alone(pool, pe_V, i * 2)
                for u in range(2):
                    for c in range(3):
                        src = xt[:, c:c + 1, bass.ds((i * 2 + u) * S + TXT, IMG)].broadcast_to([P, 8, IMG])
                        last = g.tensor_copy(xrep[u][:, c, :].rearrange("p (b t) -> p b t", b=8), src)
                last.then_inc(po_xrep, 1)

            def rows_twice(i, rows=rowb):
                wait_alone(pool, dv_hl, i + 1)
                for k in range(2):
                    src = cst[:, C_TID:C_TID + 2 * NT].rearrange("p (t k) -> p t k", k=2)[:, bass.ds(i * 2, 2), k:k + 1]
                    g.tensor_copy(rows[:, :, k, ROW_ID:ROW_ID + 1].bitcast(I32), src)
                g.tensor_copy(rows[:, :, 1, 0:D], rows[:, :, 0, 0:D]).then_inc(po_row, 1)

            def scatter(i, rows=rowb, at=pos):
                wait_alone(pool, dv_pos, i + 1)
                for u in range(2):
                    for k in range(2):
                        g.indirect_dma_start(routed[:, :], bass.IndirectOffsetOnAxis(ap=at[:, u, k:k + 1], axis=0),
                                             rows[:, u, k, :], None).then_inc(row_st, 16)

            def split_low(e, n):
                slot_, size, dst, k, at = PARTS[n]
                wait_alone(pool, ac_split, e * 4 + (n + 1))
                hi = dst[:, bass.ds(e, 1), k, at:at + size].rearrange("p a f -> p (a f)")
                lo = dst[:, bass.ds(e, 1), k + 1, at:at + size].rearrange("p a f -> p (a f)")
                g.tensor_tensor(lo, stage[:, slot_, 0:size], hi, ALU.subtract).then_inc(po_split, 1)

            def step(pool, i, par):
                first, last_ = isinstance(i, int) and i == 0, isinstance(i, int) and i == STEPS - 1
                if not first:
                    wait_alone(pool, dv_var, i)
                    powers(0, 2).then_inc(po_rs, 1)
                if not last_:
                    image_rows(i + 1)
                if not first:
                    rows_twice(i - 1)
                    split_low(i - 1, 0)
                    split_low(i - 1, 1)
                    scatter(i - 1)
                    split_low(i - 1, 2)
                    split_low(i - 1, 3)

            image_rows(0)
            attention(step, pool)
            pool.wait_ge(pe_PV, 2 * STEPS)
            g.memset(rowb_last.rearrange("p u k w -> p (u k w)"), 0.0).then_inc(po_zero, 1)
            pool.wait_ge(dv_var, STEPS)
            powers(0, 2).then_inc(po_rs, 1)
            pool.wait_ge(dv_var, STEPS + 1)
            powers(2, 4).then_inc(po_rs, 1)
            split_low(E - 1, 0)
            rows_twice(STEPS - 1)
            rows_twice(STEPS, rowb_last)
            split_low(E - 1, 1)
            scatter(STEPS - 1)
            scatter(STEPS, rowb_last, pos_last)
            split_low(E - 1, 2)
            split_low(E - 1, 3)

            bound = g.to_reg(N * TOPK - 1)

            def put(s, p, rows=SR):
                wait_alone(pool, dv_y, s + 1 if isinstance(s, int) else g.to_reg(s + 1))
                for h in range(rows // P):
                    g.indirect_dma_start(expert_out[:, :], bass.IndirectOffsetOnAxis(ap=xr[p][:, h, ROW_ID:ROW_ID + 1].bitcast(U32), axis=0),
                                         yb[p][:, h, :], None, bounds_check=bound, oob_is_err=False).then_inc(y_st[p], 16)

            for s in range(5):
                put(s, s % 4)
            with pool.Fori(0, (LARGE - 5) // 4) as j:
                for n in range(4):
                    put(j * 4 + (5 + n), (5 + n) % 4)
            for s in range(LARGE, SLOTS):
                put(s, s % 4, P)


def constants():
    import numpy as np
    c = np.zeros((P, NCONST), np.float32)
    r = np.arange(P)
    c[:, C_ID:C_ID + P] = np.eye(P)
    c[:, C_UP:C_UP + P] = r[:, None] < r[None, :]
    part = (r[:STK] // DH) % 3
    c[:STK, C_LOQ] = part == 2
    c[:STK, C_LOK] = part == 1
    for h in range(2):
        c[48 * h:48 * h + 48, C_Z + h] = 1
        c[STK + h, C_Z + h] = 1
    head = np.arange(HEADS)
    c[:, C_VM:C_VM + HEADS] = (r[:, None] // IMG) == (head[None, :] % 8)
    c[:, C_DESC:C_DESC + E] = E - np.arange(E)
    c[:, C_ER:C_ER + E] = np.arange(E) * REGION
    for t in range(NT):
        token = t * S + IMG + r if t < B else ((t - B) * 8 + r // IMG) * S + r % IMG
        for k in range(2):
            c[:, C_TID + 2 * t + k] = 2 * token + k
    c[:, C_SLOT:C_SLOT + SLOTS + 1] = np.arange(SLOTS + 1)
    c[:, C_TRI:] = np.tril(np.ones((E, E))).ravel()
    return c


def kernel(x, txt, L0_tok_gamma, L0_tok_beta, L0_tok_W, L0_tok_b, L0_attn_w_attn, L0_attn_b_attn, L0_attn_w_proj,
           L0_attn_b_proj, L0_ffn_router_w, L0_ffn_w1, L0_ffn_w2):
    import numpy as np
    import concourse.bacc as bacc
    from concourse.bass_utils import run_bass_kernel_spmd

    x = np.asarray(x)
    xp = np.pad(x, ((0, 0), (1, 1), (1, 1), (0, 0)))
    halo = np.stack([xp[:, 16 * a:16 * a + 18, 16 * b:16 * b + 18, :] for a in range(4) for b in range(4)], 1)

    def by_shift(a):
        a = np.asarray(a).reshape(8, 2, 16, 5, 3, -1)
        a = a.transpose(1, 2, 4, 3, 0, 5).reshape(2, 48, CH, -1)
        return np.pad(a, ((0, 0), (0, 6), (0, 0), (0, 0))).reshape(108, CH, -1)[:CK]

    ba = np.asarray(L0_attn_b_attn)
    bqk = np.tile(ba[:2 * D].reshape(2 * PAIRS, 2, 1, DH), (1, 1, 3, 1)).reshape(2 * PAIRS, STK).T
    wp = np.zeros((4, 32, 3, D), np.float32)
    wp[:, :DH] = np.asarray(L0_attn_w_proj).reshape(3, 4, DH, D).transpose(1, 2, 0, 3)
    wp[0, DH, 0] = np.asarray(L0_attn_b_proj)
    bv = np.zeros((4, 32, 3, 32), np.float32)
    bv[:, :DH, :, DH] = ba[2 * D:].reshape(3, 4, DH).transpose(1, 2, 0)
    arrays = {
        "a_halo": halo.reshape(B * IMG, HALO),
        "a_txt": np.asarray(txt),
        "a_tok_w": by_shift(L0_tok_W),
        "a_tok_gb": np.stack([by_shift(L0_tok_gamma)[..., 0], by_shift(L0_tok_beta)[..., 0]], 1),
        "a_rows": np.asarray(L0_tok_b)[None],
        "a_bv": bv.reshape(P, 3, 32),
        "a_bqk": bqk,
        "a_w_attn": np.asarray(L0_attn_w_attn),
        "a_w_proj": wp.reshape(P, 3, D),
        "a_router": np.asarray(L0_ffn_router_w).T,
        "a_w1": np.asarray(L0_ffn_w1),
        "a_w2": np.asarray(L0_ffn_w2),
        "a_consts": constants(),
    }
    arrays = {k: np.ascontiguousarray(a) for k, a in arrays.items()}
    nc = bacc.Bacc("TRN2", target_bir_lowering=False, num_devices=1)
    args = [nc.dram_tensor(k, a.shape, mybir.dt.from_np(a.dtype), kind="ExternalInput").ap() for k, a in arrays.items()]
    out = nc.dram_tensor("out", (B, S, D), F32, kind="ExternalOutput").ap()
    build_program(nc, *args, out)
    r = run_bass_kernel_spmd(nc, [arrays], core_ids=[0])
    return r.results[0]["out"]
```
